# Optimizing a Trainium2 kernel written in Bass

```python
import numpy as np
import jax
import jax.numpy as jnp

def _softmax(x, axis=-1):
    return jax.nn.softmax(x, axis=axis)

def _gelu(x):
    return jax.nn.gelu(x, approximate=True)

def _silu(x):
    return jax.nn.silu(x)

def _sigmoid(x):
    return jax.nn.sigmoid(x)

def _layernorm(x, axis=-1, eps=1e-05):
    m = jnp.mean(x, axis=axis, keepdims=True)
    v = jnp.var(x, axis=axis, keepdims=True)
    return (x - m) / jnp.sqrt(v + eps)

def _scatter_add(tgt, idx, src, axis=0):
    return tgt.at[idx].add(src)

def _segment_sum(src, seg, n):
    return jax.ops.segment_sum(src, seg, n)
kernel_name = 'mk_adaln_d2_jaxref_r8_6ab921'

def setup_inputs(seed: int=0):
    np.random.seed(seed)
    _w = jnp.asarray

    def _L0_attn_setup():
        import jax, jax.numpy as jnp
        import numpy as np
        D_MODEL, D_STATE, NUM_HEADS = (128, 32, 2)
        D_HEAD = D_STATE // NUM_HEADS
        BATCH, SEQ = (4, 256)
        LN_EPS = 1e-05

        def _ssm(xp, log_neg_lambdas, B_param, C_param):
            b, l, _ = xp.shape
            H, dh = log_neg_lambdas.shape
            xh = xp.reshape(b, l, H, dh)
            lam = jax.nn.sigmoid(log_neg_lambdas)
            u = xh * B_param
            a = jnp.broadcast_to(lam, (b, l, H, dh))

            def comb(e1, e2):
                a1, b1 = e1
                a2, b2 = e2
                return (a1 * a2, a2 * b1 + b2)
            _, h = jax.lax.associative_scan(comb, (a, u), axis=1)
            y = jnp.einsum('blhd,hed->blhe', h, C_param)
            return y.reshape(b, l, H * dh)
        key = jax.random.key(seed)
        ks = jax.random.split(key, 10)
        x = jax.random.normal(ks[0], (BATCH, SEQ, D_MODEL), dtype=jnp.float32)
        log_neg_lambdas = jax.random.normal(ks[1], (NUM_HEADS, D_HEAD), dtype=jnp.float32)
        B_param = jax.random.normal(ks[2], (NUM_HEADS, D_HEAD), dtype=jnp.float32) * 0.1
        C_param = jax.random.normal(ks[3], (NUM_HEADS, D_HEAD, D_HEAD), dtype=jnp.float32) * 0.1
        lim_in = 1.0 / np.sqrt(D_MODEL)
        Wp = jax.random.uniform(ks[4], (D_MODEL, D_STATE), minval=-lim_in, maxval=lim_in, dtype=jnp.float32)
        bp = jax.random.uniform(ks[5], (D_STATE,), minval=-lim_in, maxval=lim_in, dtype=jnp.float32)
        lim_out = 1.0 / np.sqrt(D_STATE)
        Wo = jax.random.uniform(ks[6], (D_STATE, D_MODEL), minval=-lim_out, maxval=lim_out, dtype=jnp.float32)
        bo = jax.random.uniform(ks[7], (D_MODEL,), minval=-lim_out, maxval=lim_out, dtype=jnp.float32)
        ln_gamma = jnp.ones((D_MODEL,), dtype=jnp.float32)
        ln_beta = jnp.zeros((D_MODEL,), dtype=jnp.float32)
        return {'x': x, 'Wp': Wp, 'bp': bp, 'Wo': Wo, 'bo': bo, 'log_neg_lambdas': log_neg_lambdas, 'B_param': B_param, 'C_param': C_param, 'ln_gamma': ln_gamma, 'ln_beta': ln_beta}
    _L0_attn_in = _L0_attn_setup()

    def _L0_ffn_setup():
        import jax, jax.numpy as jnp
        import numpy as np
        D_IN, D_HID = (128, 512)

        def _ternary(key, shape):
            return jax.random.randint(key, shape, -1, 2).astype(jnp.float32)

        def _tlin(x, w, s):
            return jnp.einsum('bsi,oi->bso', x, w) * s
        key = jax.random.key(seed)
        ks = jax.random.split(key, 12)
        inv = lambda fan: 1.0 / np.sqrt(fan).astype(np.float32)
        return {'x': jax.random.normal(ks[0], (4, 256, D_IN), dtype=jnp.float32), 'w1_w': _ternary(ks[1], (D_HID, D_IN)), 'w1_s': jax.random.uniform(ks[2], (D_HID,), dtype=jnp.float32) * inv(D_IN), 'w2_w': _ternary(ks[3], (D_HID, D_IN)), 'w2_s': jax.random.uniform(ks[4], (D_HID,), dtype=jnp.float32) * inv(D_IN), 'h1_w': _ternary(ks[5], (D_HID, D_HID)), 'h1_s': jax.random.uniform(ks[6], (D_HID,), dtype=jnp.float32) * inv(D_HID), 'h2_w': _ternary(ks[7], (D_HID, D_HID)), 'h2_s': jax.random.uniform(ks[8], (D_HID,), dtype=jnp.float32) * inv(D_HID), 'w3_w': _ternary(ks[9], (D_IN, D_HID)), 'w3_s': jax.random.uniform(ks[10], (D_IN,), dtype=jnp.float32) * inv(D_HID)}
    _L0_ffn_in = _L0_ffn_setup()
    _L0_c = _w((lambda *s: np.random.randn(*s).astype(np.float32) * 0.05)(8, 128))
    _L0_wmod = _w((lambda *s: np.random.randn(*s).astype(np.float32) * 0.05)(128, 6 * 128) * 128 ** (-0.5))

    def _L1_attn_setup():
        import jax, jax.numpy as jnp
        from jax import lax
        import numpy as np
        DIM = 128
        H = 8
        DK = 128
        DV = 32
        GATE_NORM = 16.0

        def _gla(x, Wq, Wk, Wv, Wo, Wg, bg, Wog):
            B, S, D = x.shape
            q = (x @ Wq).reshape(B, S, H, DK)
            k = (x @ Wk).reshape(B, S, H, DK) * DK ** (-0.5)
            v = (x @ Wv).reshape(B, S, H, DV)
            alpha = jax.nn.sigmoid((x @ Wg + bg) / GATE_NORM)

            def step(state, inp):
                qt, kt, vt, at = inp
                state = at[..., None, None] * state + kt[..., None] * vt[:, :, None, :]
                out_t = jnp.einsum('bhk,bhkv->bhv', qt, state)
                return (state, out_t)
            state0 = jnp.zeros((B, H, DK, DV), x.dtype)
            xs = (jnp.moveaxis(q, 1, 0), jnp.moveaxis(k, 1, 0), jnp.moveaxis(v, 1, 0), jnp.moveaxis(alpha, 1, 0))
            _, outs = lax.scan(step, state0, xs)
            out = jnp.moveaxis(outs, 0, 1).reshape(B, S, H * DV)
            og = jax.nn.sigmoid(x @ Wog)
            return out * og @ Wo
        key = jax.random.key(seed)
        ks = jax.random.split(key, 8)
        B, S = (2, 512)

        def xavier(k, shape, gain=1.0):
            fan_in, fan_out = (shape[0], shape[1])
            lim = gain * np.sqrt(6.0 / (fan_in + fan_out))
            return jax.random.uniform(k, shape, jnp.float32, -lim, lim)
        g = 2 ** (-2.5)
        return {'x': jax.random.normal(ks[0], (B, S, DIM), jnp.float32), 'Wq': xavier(ks[1], (DIM, H * DK), g), 'Wk': xavier(ks[2], (DIM, H * DK), g), 'Wv': xavier(ks[3], (DIM, H * DV), g), 'Wo': xavier(ks[4], (H * DV, DIM)), 'Wg': xavier(ks[5], (DIM, H)), 'bg': jnp.zeros((H,), jnp.float32), 'Wog': xavier(ks[6], (DIM, H * DV))}
    _L1_attn_in = _L1_attn_setup()

    def _L1_ffn_setup():
        import jax, jax.numpy as jnp
        import numpy as np
        B, S, D, H = (8, 128, 128, 512)
        E, R = (3, 8)
        SCALING = 1.0 / R

        def _mole(x, W, b, A, Bm, Rw):
            gates = jax.nn.softmax(jnp.einsum('bsd,de->bse', x, Rw), axis=-1)
            base = jnp.einsum('bsd,dh->bsh', x, W) + b
            z = jnp.einsum('bsd,edr->ebsr', x, A)
            zg = z * jnp.transpose(gates, (2, 0, 1))[..., None]
            lora = jnp.einsum('ebsr,erh->bsh', zg, Bm)
            return base + SCALING * lora
        key = jax.random.key(seed)
        ks = jax.random.split(key, 12)
        s = lambda k, shape, scale: jax.random.normal(k, shape, dtype=jnp.float32) * scale
        return {'x': s(ks[0], (B, S, D), 1.0), 'W1': s(ks[1], (D, H), D ** (-0.5)), 'b1': jnp.zeros((H,), jnp.float32), 'A1': s(ks[2], (E, D, R), D ** (-0.5)), 'B1': s(ks[3], (E, R, H), 0.0) + s(ks[4], (E, R, H), R ** (-0.5)), 'R1': s(ks[5], (D, E), D ** (-0.5)), 'W2': s(ks[6], (H, D), H ** (-0.5)), 'b2': jnp.zeros((D,), jnp.float32), 'A2': s(ks[7], (E, H, R), H ** (-0.5)), 'B2': s(ks[8], (E, R, D), R ** (-0.5)), 'R2': s(ks[9], (H, E), H ** (-0.5))}
    _L1_ffn_in = _L1_ffn_setup()
    _L1_c = _w((lambda *s: np.random.randn(*s).astype(np.float32) * 0.05)(8, 128))
    _L1_wmod = _w((lambda *s: np.random.randn(*s).astype(np.float32) * 0.05)(128, 6 * 128) * 128 ** (-0.5))
    _d = {'L0_attn_x': _L0_attn_in['x'], 'L0_attn_Wp': _L0_attn_in['Wp'], 'L0_attn_bp': _L0_attn_in['bp'], 'L0_attn_Wo': _L0_attn_in['Wo'], 'L0_attn_bo': _L0_attn_in['bo'], 'L0_attn_log_neg_lambdas': _L0_attn_in['log_neg_lambdas'], 'L0_attn_B_param': _L0_attn_in['B_param'], 'L0_attn_C_param': _L0_attn_in['C_param'], 'L0_attn_ln_gamma': _L0_attn_in['ln_gamma'], 'L0_attn_ln_beta': _L0_attn_in['ln_beta'], 'L0_ffn_w1_w': _L0_ffn_in['w1_w'], 'L0_ffn_w1_s': _L0_ffn_in['w1_s'], 'L0_ffn_w2_w': _L0_ffn_in['w2_w'], 'L0_ffn_w2_s': _L0_ffn_in['w2_s'], 'L0_ffn_h1_w': _L0_ffn_in['h1_w'], 'L0_ffn_h1_s': _L0_ffn_in['h1_s'], 'L0_ffn_h2_w': _L0_ffn_in['h2_w'], 'L0_ffn_h2_s': _L0_ffn_in['h2_s'], 'L0_ffn_w3_w': _L0_ffn_in['w3_w'], 'L0_ffn_w3_s': _L0_ffn_in['w3_s'], 'L0_c': _L0_c, 'L0_wmod': _L0_wmod, 'L1_attn_Wq': _L1_attn_in['Wq'], 'L1_attn_Wk': _L1_attn_in['Wk'], 'L1_attn_Wv': _L1_attn_in['Wv'], 'L1_attn_Wo': _L1_attn_in['Wo'], 'L1_attn_Wg': _L1_attn_in['Wg'], 'L1_attn_bg': _L1_attn_in['bg'], 'L1_attn_Wog': _L1_attn_in['Wog'], 'L1_ffn_W1': _L1_ffn_in['W1'], 'L1_ffn_b1': _L1_ffn_in['b1'], 'L1_ffn_A1': _L1_ffn_in['A1'], 'L1_ffn_B1': _L1_ffn_in['B1'], 'L1_ffn_R1': _L1_ffn_in['R1'], 'L1_ffn_W2': _L1_ffn_in['W2'], 'L1_ffn_b2': _L1_ffn_in['b2'], 'L1_ffn_A2': _L1_ffn_in['A2'], 'L1_ffn_B2': _L1_ffn_in['B2'], 'L1_ffn_R2': _L1_ffn_in['R2'], 'L1_c': _L1_c, 'L1_wmod': _L1_wmod}
    _x0 = _d['L0_attn_x']
    _d['L0_attn_x'] = jax.random.normal(jax.random.fold_in(jax.random.key(seed), 1), (8, 512, 128), dtype=_x0.dtype)
    del _x0
    return _d

def reference(L0_attn_x, L0_attn_Wp, L0_attn_bp, L0_attn_Wo, L0_attn_bo, L0_attn_log_neg_lambdas, L0_attn_B_param, L0_attn_C_param, L0_attn_ln_gamma, L0_attn_ln_beta, L0_ffn_w1_w, L0_ffn_w1_s, L0_ffn_w2_w, L0_ffn_w2_s, L0_ffn_h1_w, L0_ffn_h1_s, L0_ffn_h2_w, L0_ffn_h2_s, L0_ffn_w3_w, L0_ffn_w3_s, L0_c, L0_wmod, L1_attn_Wq, L1_attn_Wk, L1_attn_Wv, L1_attn_Wo, L1_attn_Wg, L1_attn_bg, L1_attn_Wog, L1_ffn_W1, L1_ffn_b1, L1_ffn_A1, L1_ffn_B1, L1_ffn_R1, L1_ffn_W2, L1_ffn_b2, L1_ffn_A2, L1_ffn_B2, L1_ffn_R2, L1_c, L1_wmod):

    def _L0_attn_ref(x, Wp, bp, Wo, bo, log_neg_lambdas, B_param, C_param, ln_gamma, ln_beta):
        import jax, jax.numpy as jnp
        import numpy as np
        D_MODEL, D_STATE, NUM_HEADS = (128, 32, 2)
        D_HEAD = D_STATE // NUM_HEADS
        BATCH, SEQ = (4, 256)
        LN_EPS = 1e-05

        def _ssm(xp, log_neg_lambdas, B_param, C_param):
            b, l, _ = xp.shape
            H, dh = log_neg_lambdas.shape
            xh = xp.reshape(b, l, H, dh)
            lam = jax.nn.sigmoid(log_neg_lambdas)
            u = xh * B_param
            a = jnp.broadcast_to(lam, (b, l, H, dh))

            def comb(e1, e2):
                a1, b1 = e1
                a2, b2 = e2
                return (a1 * a2, a2 * b1 + b2)
            _, h = jax.lax.associative_scan(comb, (a, u), axis=1)
            y = jnp.einsum('blhd,hed->blhe', h, C_param)
            return y.reshape(b, l, H * dh)
        residual = x
        xp = x @ Wp + bp
        y = _ssm(xp, log_neg_lambdas, B_param, C_param)
        out = y @ Wo + bo
        z = out + residual
        mean = jnp.mean(z, axis=-1, keepdims=True)
        var = jnp.var(z, axis=-1, keepdims=True)
        return (z - mean) / jnp.sqrt(var + LN_EPS) * ln_gamma + ln_beta

    def _L0_ffn_ref(x, w1_w, w1_s, w2_w, w2_s, h1_w, h1_s, h2_w, h2_s, w3_w, w3_s):
        import jax, jax.numpy as jnp
        import numpy as np
        D_IN, D_HID = (128, 512)

        def _ternary(key, shape):
            return jax.random.randint(key, shape, -1, 2).astype(jnp.float32)

        def _tlin(x, w, s):
            return jnp.einsum('bsi,oi->bso', x, w) * s
        h = jax.nn.silu(_tlin(x, w1_w, w1_s)) * _tlin(x, w2_w, w2_s)
        h = jax.nn.gelu(_tlin(h, h1_w, h1_s), approximate=False)
        h = jax.nn.gelu(_tlin(h, h2_w, h2_s), approximate=False)
        return _tlin(h, w3_w, w3_s)

    def _L1_attn_ref(x, Wq, Wk, Wv, Wo, Wg, bg, Wog):
        import jax, jax.numpy as jnp
        from jax import lax
        import numpy as np
        DIM = 128
        H = 8
        DK = 128
        DV = 32
        GATE_NORM = 16.0

        def _gla(x, Wq, Wk, Wv, Wo, Wg, bg, Wog):
            B, S, D = x.shape
            q = (x @ Wq).reshape(B, S, H, DK)
            k = (x @ Wk).reshape(B, S, H, DK) * DK ** (-0.5)
            v = (x @ Wv).reshape(B, S, H, DV)
            alpha = jax.nn.sigmoid((x @ Wg + bg) / GATE_NORM)

            def step(state, inp):
                qt, kt, vt, at = inp
                state = at[..., None, None] * state + kt[..., None] * vt[:, :, None, :]
                out_t = jnp.einsum('bhk,bhkv->bhv', qt, state)
                return (state, out_t)
            state0 = jnp.zeros((B, H, DK, DV), x.dtype)
            xs = (jnp.moveaxis(q, 1, 0), jnp.moveaxis(k, 1, 0), jnp.moveaxis(v, 1, 0), jnp.moveaxis(alpha, 1, 0))
            _, outs = lax.scan(step, state0, xs)
            out = jnp.moveaxis(outs, 0, 1).reshape(B, S, H * DV)
            og = jax.nn.sigmoid(x @ Wog)
            return out * og @ Wo
        return _gla(x, Wq, Wk, Wv, Wo, Wg, bg, Wog)

    def _L1_ffn_ref(x, W1, b1, A1, B1, R1, W2, b2, A2, B2, R2):
        import jax, jax.numpy as jnp
        import numpy as np
        B, S, D, H = (8, 128, 128, 512)
        E, R = (3, 8)
        SCALING = 1.0 / R

        def _mole(x, W, b, A, Bm, Rw):
            gates = jax.nn.softmax(jnp.einsum('bsd,de->bse', x, Rw), axis=-1)
            base = jnp.einsum('bsd,dh->bsh', x, W) + b
            z = jnp.einsum('bsd,edr->ebsr', x, A)
            zg = z * jnp.transpose(gates, (2, 0, 1))[..., None]
            lora = jnp.einsum('ebsr,erh->bsh', zg, Bm)
            return base + SCALING * lora
        h = _mole(x, W1, b1, A1, B1, R1)
        h = jax.nn.relu(h)
        return _mole(h, W2, b2, A2, B2, R2)
    x = L0_attn_x
    mod = (_silu(L0_c) @ L0_wmod).reshape(L0_c.shape[0], 6, 1, -1)
    sa, ca, ga, sb, cb, gb = (mod[:, 0], mod[:, 1], mod[:, 2], mod[:, 3], mod[:, 4], mod[:, 5])
    ga = (2 * (ga >= 0) - 1) * jnp.maximum(jnp.abs(ga), 0.25)
    gb = (2 * (gb >= 0) - 1) * jnp.maximum(jnp.abs(gb), 0.25)
    h = _layernorm(x, axis=-1) * (1 + ca) + sa
    x = x + ga * _L0_attn_ref(h, L0_attn_Wp, L0_attn_bp, L0_attn_Wo, L0_attn_bo, L0_attn_log_neg_lambdas, L0_attn_B_param, L0_attn_C_param, L0_attn_ln_gamma, L0_attn_ln_beta)
    h = _layernorm(x, axis=-1) * (1 + cb) + sb
    x = x + gb * _L0_ffn_ref(h, L0_ffn_w1_w, L0_ffn_w1_s, L0_ffn_w2_w, L0_ffn_w2_s, L0_ffn_h1_w, L0_ffn_h1_s, L0_ffn_h2_w, L0_ffn_h2_s, L0_ffn_w3_w, L0_ffn_w3_s)
    mod = (_silu(L1_c) @ L1_wmod).reshape(L1_c.shape[0], 6, 1, -1)
    sa, ca, ga, sb, cb, gb = (mod[:, 0], mod[:, 1], mod[:, 2], mod[:, 3], mod[:, 4], mod[:, 5])
    ga = (2 * (ga >= 0) - 1) * jnp.maximum(jnp.abs(ga), 0.25)
    gb = (2 * (gb >= 0) - 1) * jnp.maximum(jnp.abs(gb), 0.25)
    h = _layernorm(x, axis=-1) * (1 + ca) + sa
    x = x + ga * _L1_attn_ref(h, L1_attn_Wq, L1_attn_Wk, L1_attn_Wv, L1_attn_Wo, L1_attn_Wg, L1_attn_bg, L1_attn_Wog)
    h = _layernorm(x, axis=-1) * (1 + cb) + sb
    x = x + gb * _L1_ffn_ref(h, L1_ffn_W1, L1_ffn_b1, L1_ffn_A1, L1_ffn_B1, L1_ffn_R1, L1_ffn_W2, L1_ffn_b2, L1_ffn_A2, L1_ffn_B2, L1_ffn_R2)
    return x

_drawn_inputs = setup_inputs


def setup_inputs(seed=0):
    import zlib

    import numpy as np

    out = dict(_drawn_inputs(seed))
    spreads = {'L0_attn_ln_gamma': (1.0, 0.2),
     'L0_attn_ln_beta': (0.0, 0.1),
     'L1_attn_bg': (0.0, 0.1),
     'L1_ffn_b1': (0.0, 0.1),
     'L1_ffn_b2': (0.0, 0.1)}
    factors = {}
    for name, (base, spread) in spreads.items():
        noise = np.random.default_rng([zlib.crc32(name.encode()), seed]).standard_normal(out[name].shape)
        drawn = base * np.exp(spread * noise) if base else spread * noise
        out[name] = jnp.asarray(drawn.astype(out[name].dtype))
    for name, factor in factors.items():
        out[name] = (out[name] * factor).astype(out[name].dtype)
    return out
```

```python
from contextlib import ExitStack

import concourse.bass as bass
from concourse import mybir

F32 = mybir.dt.float32
F32R = mybir.dt.float32r
ACT = mybir.ActivationFunctionType
ALU = mybir.AluOpType
AX_X = mybir.AxisListType.X

P = 128
B = 8
S = 512
T = S // P
D = 128
SD = 32
NH = 8
DV = 32
HV = NH * DV
HID = 512
KH = HID // P
E = 3
R = 8
ER = E * R
AR = ER + E
DK = 128
LN_EPS = 1e-5
GATE_NORM = 16.0
GLO = 32
W1, W2, H1, H2, W3 = 0, 512, 1024, 3072, 5120
WCOLS = 5632
VO, F1, GT = 0, 512, 1024
VCOLS = 1024 + 128
SA, CA, GA, SB, CB, GB = range(6)


def build(nc, d, out):
    with ExitStack() as ctx:
        def sb(name, shape, dt=F32):
            return ctx.enter_context(nc.sbuf_tensor(name, shape, dt))

        r = {"set_up": ctx.enter_context(nc.semaphore("set_up"))}
        r["x"] = sb("x", [P, B, T, D])
        r["ident"] = sb("ident", [P, P])
        r["ident4"] = sb("ident4", [P, S])
        r["neg_half"] = sb("neg_half", [P, T])
        r["mod"] = sb("mod", [P, 2, 4, B])
        r["gain_attn0"] = sb("gain_attn0", [P, B, D])
        r["bias_attn0"] = sb("bias_attn0", [P, B, D])
        r["gain_ffn0"] = sb("gain_ffn0", [P, B])
        r["gain_attn1"] = sb("gain_attn1", [P, B, D])
        r["gain_ffn1"] = sb("gain_ffn1", [P, B, D])
        r["w_scale"] = sb("w_scale", [P, 4, KH])
        r["v_hi"] = sb("v_hi", [P, VCOLS], F32R)
        r["v_lo"] = sb("v_lo", [P, VCOLS], F32R)
        r["m_hi"] = sb("m_hi", [P, NH, P], F32R)
        r["m_lo"] = sb("m_lo", [P, NH, P], F32R)
        r["wp"] = sb("wp", [P, SD])
        r["bp"] = sb("bp", [SD, 1])
        r["lam"] = sb("lam", [SD, S])
        r["cw"] = sb("cw", [SD + 1, D])
        r["wo"] = sb("wo", [P, 2, D])
        r["gate_bias"] = sb("gate_bias", [P, 1])
        r["sel"] = sb("sel", [GLO + NH, NH, P], F32R)
        r["keep"] = sb("keep", [GLO + NH, S])
        r["eye8"] = sb("eye8", [NH, NH])
        r["ones8"] = sb("ones8", [NH, P])
        r["b1e"] = sb("b1e", [ER + 1, HID])
        r["b2e"] = sb("b2e", [ER + 1, D])
        r["ar1"] = sb("ar1", [P, AR])
        r["war2"] = sb("war2", [P, KH, D + AR])
        psum = [ctx.enter_context(nc.psum_tensor(f"bank{n}", [P, S], F32)) for n in range(8)]

        with nc.sbuf_tensor("w_hi", [P, WCOLS], F32R) as w_hi, nc.sbuf_tensor("w_lo", [P, WCOLS], F32R) as w_lo:
            r["w_hi"], r["w_lo"] = w_hi, w_lo
            setup(nc, d, r, psum)
            ssm_block(nc, r, psum)
            ternary_ffn(nc, r, psum)
        linear_attention(nc, r, psum)
        lora_ffn(nc, r, psum, out)


class Signals:

    def __init__(self, nc):
        self.nc, self.held = nc, []

    def __enter__(self):
        return self

    def __call__(self, name):
        self.held.append(self.nc.alloc_semaphore(name))
        return self.held[-1]

    def __exit__(self, *error):
        if error[0] is None:
            self.nc.clear_and_free_semaphores(self.held)
            self.nc.all_engine_barrier()


def wait_apart(eng, r, signal, count):
    if not isinstance(count, int):
        count = eng.to_reg(count)
    eng.wait_ge(r["set_up"], 1)
    eng.wait_ge(signal, count)


def over(ap, axis, shape):
    return ap.unsqueeze(axis).broadcast_to(shape)


def split_mm(pe, acc, w, x, start, stop):
    pe.matmul(acc, w[0], x[0], start=start, stop=False)
    pe.matmul(acc, w[0], x[1], start=False, stop=False)
    return pe.matmul(acc, w[1], x[0], start=False, stop=stop)


def setup(nc, d, r, psum):
    with ExitStack() as ctx:
        def sb(name, shape, dt=F32):
            return ctx.enter_context(nc.sbuf_tensor(name, shape, dt))

        sem = ctx.enter_context(Signals(nc))

        cT = sb("cT", [P, 2, B])
        scT = sb("scT", [P, 2, B])
        sc_wide = sb("sc_wide", [P, 2, B, P])
        wmod = sb("wmod", [P, 2, 6, D])
        gamma = sb("gamma", [P, D])
        beta = sb("beta", [P, D])
        w3s = sb("w3s", [P, 1])
        mag_col = sb("mag_col", [P, B])
        sgn_col = sb("sgn_col", [P, B])
        gate_col = sb("gate_col", [P, B])
        b_row = sb("b_row", [P, SD])
        b_col = sb("b_col", [SD, 1])
        bp_raw = sb("bp_raw", [SD, 1])
        lam_raw = sb("lam_raw", [SD, 1])
        lam_col = sb("lam_col", [SD, 1])
        c_diag = sb("c_diag", [SD, SD])
        wo0 = sb("wo0", [SD, D])
        wqT = sb("wqT", [P, NH, D])
        wkT = sb("wkT", [P, NH, D])
        w_raw = sb("w_raw", [P, WCOLS])
        v_raw = sb("v_raw", [P, VCOLS])
        m_raw = sb("m_raw", [P, NH * P])
        sel_raw = sb("sel_raw", [GLO + NH, NH, P])
        gb_raw = sb("gb_raw", [P, 1])
        mag = sb("mag", [P, S])
        sgn = sb("sgn", [P, S])
        gate = sb("gate", [P, S])

        loaded_cond = sem("loaded_cond")
        loaded_small = sem("loaded_small")
        loaded_w = sem("loaded_w")
        loaded_qk = sem("loaded_qk")
        loaded_l1 = sem("loaded_l1")
        loaded_x = sem("loaded_x")
        zeroed = sem("zeroed")
        silu_ready = sem("silu_ready")
        wide_ready = sem("wide_ready")
        mod_mm = sem("mod_mm")
        mod_read = sem("mod_read")
        gates_mm = sem("gates_mm")
        cw_mm = sem("cw_mm")
        qk_mm = sem("qk_mm")
        qk_read = sem("qk_read")
        lam_ready = sem("lam_ready")
        mag_ready = sem("mag_ready")
        sgn_ready = sem("sgn_ready")
        gate_ready = sem("gate_ready")
        gate_used = sem("gate_used")
        col_ready = sem("col_ready")
        w_high = sem("w_high")
        v_high = sem("v_high")
        m_copied = sem("m_copied")
        m_high = sem("m_high")

        GATES = [(0, GA), (1, GA), (1, GB)]
        n_small = 0
        with nc.Block() as block:
            small = [
                (gamma[:, :], d["ln_gamma"].partition_broadcast(P)), (beta[:, :], d["ln_beta"].partition_broadcast(P)),
                (w3s[:, :], d["w3_s"]), (b_row[:, :], d["B_row"].partition_broadcast(P)),
                (b_col[:, :], d["B_col"]), (bp_raw[:, :], d["bp"]), (lam_raw[:, :], d["lam"]),
                (wo0[:, :], d["Wo0"]), (r["wp"][:, :], d["Wp"]), (r["ident"][:, :], d["ident"]),
                (r["cw"][SD:SD + 1, :], d["bo"]), (r["w_scale"][:, :, :], d["w_scale"]),
            ]
            n_small = len(small) + 2
            l1 = [
                (r["wo"][:, :, :], d["Wo1"]), (gb_raw[0:NH, :], d["bg"]), (gb_raw[GLO:GLO + NH, :], d["bg"]),
                (sel_raw[:, :, :], d["sel"]), (r["keep"][:, :], d["keep"]), (r["eye8"][:, :], d["eye8"]),
                (r["b1e"][:, :], d["B1e"]), (r["b2e"][:, :], d["B2e"]), (r["ar1"][:, :], d["AR1"]),
                (r["war2"][:, :, :], d["WAR2"]), (v_raw[:, VO:VO + 2 * HV], d["WvWog"]), (v_raw[:, F1:F1 + HID], d["W1"]),
                (v_raw[:, GT:GT + NH], d["Wg"]), (v_raw[:, GT + GLO:GT + GLO + NH], d["Wg"]),
            ]

            @block.sync
            def _(sp):
                sp.dma_start(cT[:, :, :], d["cT"]).then_inc(loaded_cond, 16)
                sp.dma_start(wmod[:, :, :, :], d["wmod"]).then_inc(loaded_cond, 16)
                for b in range(B):
                    sp.dma_start(r["x"][:, b, :, :], d["x"][b].rearrange("(t p) n -> p t n", p=P)).then_inc(loaded_x, 16)
                sp.dma_start(wqT[:, :, :], d["WqT"]).then_inc(loaded_qk, 16)
                sp.dma_start(wkT[:, :, :], d["WkT"]).then_inc(loaded_qk, 16)
                sp.dma_start(w_raw[:, :], d["w_all"]).then_inc(loaded_w, 16)
                sp.wait_ge(loaded_x, 16 * B)

            @block.gpsimd
            def _(pool):
                pool.memset(c_diag[:, :], 0.0).then_inc(zeroed, 1)
                pool.memset(v_raw[:, GT:GT + P], 0.0).then_inc(zeroed, 1)
                pool.memset(gb_raw[:, :], 0.0).then_inc(zeroed, 1)
                pool.memset(r["ones8"][:, :], 1.0).then_inc(zeroed, 1)
                pool.memset(r["neg_half"][:, :], -0.5).then_inc(zeroed, 1)
                pool.wait_ge(loaded_small, 16 * n_small)
                for t in range(T):
                    pool.tensor_copy(r["ident4"][:, t * P:(t + 1) * P], r["ident"][:, :])
                pool.wait_ge(w_high, 1)
                pool.tensor_tensor(r["w_lo"][:, 0:WCOLS // 2], w_raw[:, 0:WCOLS // 2], r["w_hi"][:, 0:WCOLS // 2].bitcast(F32), ALU.subtract)

            @block.scalar
            def _(act):
                for dst, src in small:
                    act.dma_start(dst, src).then_inc(loaded_small, 16)
                act.wait_ge(zeroed, 3)
                for h in range(2):
                    o = h * SD // 2
                    act.dma_start(c_diag[o:o + SD // 2, o:o + SD // 2], d["C"][h]).then_inc(loaded_small, 16)
                for dst, src in l1:
                    act.dma_start(dst, src).then_inc(loaded_l1, 16)
                act.wait_ge(loaded_cond, 32)
                act.activation(scT[:, :, :], cT[:, :, :], ACT.Silu).then_inc(silu_ready, 1)
                act.wait_ge(loaded_small, 16 * n_small)
                act.activation(lam_col[:, :], lam_raw[:, :], ACT.Sigmoid).then_inc(lam_ready, 1)
                act.wait_ge(cw_mm, 1)
                act.copy(r["cw"][0:SD, :], psum[6][0:SD, 0:D])
                act.wait_ge(loaded_l1, 16 * len(l1))
                act.mul(r["gate_bias"][:, :], gb_raw[:, :], 1.0 / GATE_NORM)
                act.mul(r["b1e"][0:ER, :], r["b1e"][0:ER, :], 1.0 / R)
                act.mul(r["b2e"][0:ER, :], r["b2e"][0:ER, :], 1.0 / R)
                for n in range(2):
                    act.wait_ge(qk_mm, n + 1)
                    act.mul(m_raw[:, n * S:(n + 1) * S], psum[n][:, :], DK ** -0.5).then_inc(m_copied, 1)

            @block.tensor
            def _(pe):
                pe.wait_ge(silu_ready, 1)
                n = 0
                for layer in range(2):
                    for j, kind in enumerate((SA, CA, SB, CB)):
                        col = (layer * 4 + j) * B
                        mm = pe.matmul(psum[7][:, col:col + B], wmod[:, layer, kind, :], scT[:, layer, :], start=True, stop=True)
                mm = pe.matmul(psum[7][:, 8 * B:9 * B], wmod[:, 0, GB, :], scT[:, 0, :], start=True, stop=True)
                mm.then_inc(mod_mm, 1)
                pe.wait_ge(loaded_small, 16 * n_small)
                pe.matmul(psum[6][0:SD, 0:D], c_diag[:, :], wo0[:, :], start=True, stop=True).then_inc(cw_mm, 1)
                pe.wait_ge(wide_ready, 2)
                for k, (layer, kind) in enumerate(GATES):
                    for half in range(2):
                        bank = 2 * k + half
                        for q in range(4):
                            mm = pe.matmul(psum[bank][:, q * P:(q + 1) * P], sc_wide[:, layer, half * 4 + q, :], wmod[:, layer, kind, :], start=True, stop=True)
                        mm.then_inc(gates_mm, 1)
                pe.wait_ge(loaded_qk, 32)
                pe.wait_ge(mag_ready, 12)
                for h in range(NH):
                    mm = pe.matmul(psum[h // 4][:, (h % 4) * P:(h % 4 + 1) * P], wqT[:, h, :], wkT[:, h, :], start=True, stop=True)
                    if h % 4 == 3:
                        mm.then_inc(qk_mm, 1)

            @block.vector
            def _(dve):
                dve.wait_ge(silu_ready, 1)
                for layer in range(2):
                    dve.tensor_copy(sc_wide[:, layer, :, :], over(scT[:, layer, :], 2, [P, B, P])).then_inc(wide_ready, 1)
                dve.wait_ge(mod_mm, 1)
                src = psum[7][:, 0:8 * B].rearrange("p (l k b) -> p l k b", l=2, k=4)
                for k in range(4):
                    dve.tensor_scalar(r["mod"][:, :, k, :], src[:, :, k, :], float(k % 2), None, ALU.add)
                dve.wait_ge(loaded_small, 16 * n_small)
                dve.tensor_tensor(r["wp"][:, :], r["wp"][:, :], b_row[:, :], ALU.mult)
                dve.tensor_tensor(r["bp"][:, :], bp_raw[:, :], b_col[:, :], ALU.mult)
                g = psum[7][:, 8 * B:9 * B]
                dve.tensor_scalar(mag_col[:, :], g, -1.0, 0.25, ALU.mult, ALU.max).then_inc(col_ready, 1)
                dve.tensor_scalar(sgn_col[:, :], g, 0.0, 2.0, ALU.is_ge, ALU.mult).then_inc(col_ready, 1)
                dve.wait_ge(col_ready, 2)
                dve.tensor_tensor(mag_col[:, :], mag_col[:, :], g, ALU.max).then_inc(col_ready, 1)
                dve.wait_ge(col_ready, 3)
                dve.scalar_tensor_tensor(out=gate_col[:, :], in0=sgn_col[:, :], scalar=-1.0, in1=mag_col[:, :], op0=ALU.add, op1=ALU.mult).then_inc(col_ready, 1)
                dve.wait_ge(col_ready, 4)
                dve.tensor_scalar(r["gain_ffn0"][:, :], gate_col[:, :], w3s[:, 0:1], None, ALU.mult)
                dve.wait_ge(lam_ready, 1)
                dve.tensor_copy(r["lam"][:, :], lam_col[:, 0:1].broadcast_to([SD, S]))
                for n in range(6):
                    k, half = n // 2, n % 2
                    dve.wait_ge(gates_mm, n + 1)
                    g = psum[n][:, :]
                    if n:
                        dve.wait_ge(gate_ready, n)
                    dve.tensor_scalar(mag[:, :], g, -1.0, 0.25, ALU.mult, ALU.max).then_inc(mag_ready, 1)
                    dve.tensor_scalar(sgn[:, :], g, 0.0, 2.0, ALU.is_ge, ALU.mult).then_inc(sgn_ready, 1)
                    dve.wait_ge(mag_ready, 2 * n + 1)
                    dve.tensor_tensor(mag[:, :], mag[:, :], g, ALU.max).then_inc(mag_ready, 1)
                    dve.wait_ge(mag_ready, 2 * n + 2)
                    dve.wait_ge(sgn_ready, n + 1)
                    if k >= 1:
                        name = ("gain_attn1", "gain_ffn1")[k - 1]
                        dst = r[name][:, 4 * half:4 * half + 4, :].rearrange("p b n -> p (b n)")
                    else:
                        if n:
                            dve.wait_ge(gate_used, n)
                        dst = gate[:, :]
                    dve.scalar_tensor_tensor(out=dst, in0=sgn[:, :], scalar=-1.0, in1=mag[:, :], op0=ALU.add, op1=ALU.mult).then_inc(gate_ready, 1)
                    if k >= 1:
                        continue
                    dve.wait_ge(gate_ready, n + 1)
                    g4 = gate[:, :].rearrange("p (b n) -> p b n", b=4)
                    here = slice(4 * half, 4 * half + 4)
                    dve.tensor_tensor(r["gain_attn0"][:, here, :], g4, over(gamma[:, :], 1, [P, 4, D]), ALU.mult)
                    dve.tensor_tensor(r["bias_attn0"][:, here, :], g4, over(beta[:, :], 1, [P, 4, D]), ALU.mult).then_inc(gate_used, 1)
                dve.wait_ge(loaded_w, 16)
                dve.tensor_copy(r["w_hi"][:, :], w_raw[:, :]).then_inc(w_high, 1)
                dve.wait_ge(w_high, 1)
                dve.tensor_tensor(r["w_lo"][:, WCOLS // 2:], w_raw[:, WCOLS // 2:], r["w_hi"][:, WCOLS // 2:].bitcast(F32), ALU.subtract)
                dve.wait_ge(loaded_l1, 16 * len(l1))
                dve.tensor_copy(r["sel"][:, :, :], sel_raw[:, :, :])
                dve.tensor_copy(r["v_hi"][:, :], v_raw[:, :]).then_inc(v_high, 1)
                dve.wait_ge(v_high, 1)
                dve.tensor_tensor(r["v_lo"][:, :], v_raw[:, :], r["v_hi"][:, :].bitcast(F32), ALU.subtract)
                dve.wait_ge(m_copied, 2)
                dve.tensor_copy(r["m_hi"][:, :, :].rearrange("p h n -> p (h n)"), m_raw[:, :]).then_inc(m_high, 1)
                dve.wait_ge(m_high, 1)
                dve.tensor_tensor(r["m_lo"][:, :, :].rearrange("p h n -> p (h n)"), m_raw[:, :], r["m_hi"][:, :, :].rearrange("p h n -> p (h n)").bitcast(F32), ALU.subtract).then_inc(r["set_up"], 1)


def norm_buffers(sb, sem, tag, slots):
    return [{
        "stats": sb(f"{tag}_stats{s}", [P, T, 6]), "mv": sb(f"{tag}_mv{s}", [P, T, 2]),
        "var": sb(f"{tag}_var{s}", [P, T]), "rstd": sb(f"{tag}_rstd{s}", [P, T]),
        "out": sb(f"{tag}_out{s}", [P, T, D]),
        "stats_ready": sem(f"{tag}_stats_ready{s}"), "moments_ready": sem(f"{tag}_moments_ready{s}"),
        "var_ready": sem(f"{tag}_var_ready{s}"), "rstd_ready": sem(f"{tag}_rstd_ready{s}"),
        "ready": sem(f"{tag}_ready{s}"),
    } for s in range(slots)]


def norm_moments(dve, r, n, i, tile):
    for t in range(T):
        ins = dve.bn_stats(n["stats"][:, t, :], tile(t))
    ins.then_inc(n["stats_ready"], 1)
    wait_apart(dve, r, n["stats_ready"], i + 1)
    for t in range(T):
        ins = dve.bn_aggr(n["mv"][:, t, :], n["stats"][:, t, :])
    ins.then_inc(n["moments_ready"], 1)


def norm_rstd(pool, r, n, i):
    wait_apart(pool, r, n["moments_ready"], i + 1)
    pool.tensor_scalar(n["var"][:, :], n["mv"][:, :, 1], LN_EPS, None, ALU.add).then_inc(n["var_ready"], 1)
    pool.wait_ge(n["var_ready"], i + 1)
    pool.tensor_tensor(n["rstd"][:, :], n["var"][:, :], r["neg_half"][:, :], ALU.pow).then_inc(n["rstd_ready"], 1)


def norm_apply(dve, n, i, tile):
    dve.wait_ge(n["rstd_ready"], i + 1)
    for t in range(T):
        ins = dve.tensor_scalar(n["out"][:, t, :], tile(t), n["mv"][:, t, 0:1], n["rstd"][:, t:t + 1], ALU.subtract, ALU.mult)
    ins.then_inc(n["ready"], 1)


def flip(pe, bank, src, r):
    for t in range(T):
        ins = pe.transpose(bank[:, t * P:(t + 1) * P], src(t), r["ident"][:, :])
    return ins


def modulate(act, r, dst, bank, layer, kind, b):
    return act.activation(dst, bank, ACT.Identity, scale=r["mod"][:, layer, kind + 1, bass.ds(b, 1)], bias=r["mod"][:, layer, kind, bass.ds(b, 1)])


def ssm_block(nc, r, psum):
    SLOTS = 4
    with ExitStack() as ctx:
        def sb(name, shape, dt=F32):
            return ctx.enter_context(nc.sbuf_tensor(name, shape, dt))

        sem = ctx.enter_context(Signals(nc))

        slots = range(SLOTS)
        n1 = norm_buffers(sb, sem, "ssm_in", SLOTS)
        n2 = norm_buffers(sb, sem, "ssm_out", SLOTS)
        hT = [sb(f"ssm_hT{s}", [P, S]) for s in slots]
        u = [sb(f"ssm_u{s}", [SD, S]) for s in slots]
        state = [sb(f"ssm_state{s}", [SD + 1, S]) for s in slots]
        upd = [sb(f"ssm_upd{s}", [P, T, D]) for s in slots]
        flipped = [sem(f"ssm_flipped{s}") for s in slots]
        h_ready = [sem(f"ssm_h_ready{s}") for s in slots]
        u_mm = [sem(f"ssm_u_mm{s}") for s in slots]
        u_ready = [sem(f"ssm_u_ready{s}") for s in slots]
        scanned = [sem(f"ssm_scanned{s}") for s in slots]
        z_mm = [sem(f"ssm_z_mm{s}") for s in slots]
        scaled = [sem(f"ssm_scaled{s}") for s in slots]
        upd_ready = [sem(f"ssm_upd_ready{s}") for s in slots]
        added = [sem(f"ssm_added{s}") for s in slots]
        ones_set = sem("ssm_ones_set")
        bank_a = psum[0:4]
        bank_u = psum[4:8]

        with nc.Block() as block:
            @block.vector
            def _(dve):
                for s in slots:
                    dve.memset(state[s][SD:SD + 1, :], 1.0).then_inc(ones_set, 1)
                with dve.Fori(0, B // SLOTS) as i:
                    for s in slots:
                        norm_moments(dve, r, n1[s], i, lambda t: r["x"][:, bass.ds(i * SLOTS + s, 1), t, :])
                    for s in slots:
                        norm_apply(dve, n1[s], i, lambda t: r["x"][:, bass.ds(i * SLOTS + s, 1), t, :])
                    for s in slots:
                        dve.wait_ge(u_ready[s], i + 1)
                        dve.tensor_tensor_scan(state[s][0:SD, :], r["lam"][:, :], u[s][:, :], 0.0, ALU.mult, ALU.add).then_inc(scanned[s], 1)
                    for s in slots:
                        z = bank_a[s]
                        dve.wait_ge(z_mm[s], i + 1)
                        norm_moments(dve, r, n2[s], i, lambda t: z[:, t * P:(t + 1) * P])
                    for s in slots:
                        norm_apply(dve, n2[s], i, lambda t: bank_a[s][:, t * P:(t + 1) * P])
                    for s in slots:
                        dve.wait_ge(upd_ready[s], i + 1)
                        x = r["x"][:, bass.ds(i * SLOTS + s, 1), :, :].rearrange("p b t n -> p (b t) n")
                        dve.tensor_tensor(x, x, upd[s][:, :, :], ALU.add).then_inc(added[s], 1)

            @block.gpsimd
            def _(pool):
                with pool.Fori(0, B // SLOTS) as i:
                    for s in slots:
                        norm_rstd(pool, r, n1[s], i)
                    for s in slots:
                        norm_rstd(pool, r, n2[s], i)
                    for s in slots:
                        b = bass.ds(i * SLOTS + s, 1)
                        pool.wait_ge(n2[s]["ready"], i + 1)
                        pool.wait_ge(added[s], i)
                        pool.tensor_tensor(upd[s][:, :, :], n2[s]["out"][:, :, :], r["gain_attn0"][:, b, :].broadcast_to([P, T, D]), ALU.mult).then_inc(scaled[s], 1)
                        pool.wait_ge(scaled[s], i + 1)
                        pool.tensor_tensor(upd[s][:, :, :], upd[s][:, :, :], r["bias_attn0"][:, b, :].broadcast_to([P, T, D]), ALU.add).then_inc(upd_ready[s], 1)

            @block.scalar
            def _(act):
                with act.Fori(0, B // SLOTS) as i:
                    for s in slots:
                        act.wait_ge(flipped[s], i + 1)
                        modulate(act, r, hT[s][:, :], bank_a[s][:, :], 0, 0, i * SLOTS + s).then_inc(h_ready[s], 1)
                    for s in slots:
                        act.wait_ge(u_mm[s], i + 1)
                        act.activation(u[s][:, :], bank_u[s][0:SD, :], ACT.Identity, bias=r["bp"][:, 0:1]).then_inc(u_ready[s], 1)

            @block.tensor
            def _(pe):
                pe.wait_ge(ones_set, SLOTS)
                with pe.Fori(0, B // SLOTS) as i:
                    for s in slots:
                        pe.wait_ge(n1[s]["ready"], i + 1)
                        pe.wait_ge(n2[s]["ready"], i)
                        flip(pe, bank_a[s], lambda t: n1[s]["out"][:, t, :], r).then_inc(flipped[s], 1)
                    for s in slots:
                        pe.wait_ge(h_ready[s], i + 1)
                        pe.matmul(bank_u[s][0:SD, :], r["wp"][:, :], hT[s][:, :], start=True, stop=True).then_inc(u_mm[s], 1)
                    for s in slots:
                        pe.wait_ge(scanned[s], i + 1)
                        for t in range(T):
                            c = slice(t * P, (t + 1) * P)
                            pe.matmul(bank_a[s][:, c], hT[s][:, c], r["ident"][:, :], start=True, stop=False)
                            mm = pe.matmul(bank_a[s][:, c], state[s][:, c], r["cw"][:, :], start=False, stop=True)
                        mm.then_inc(z_mm[s], 1)


def ternary_ffn(nc, r, psum):
    SLOTS = 2
    RING = 4
    with ExitStack() as ctx:
        def sb(name, shape, dt=F32):
            return ctx.enter_context(nc.sbuf_tensor(name, shape, dt))

        sem = ctx.enter_context(Signals(nc))

        slots = range(SLOTS)
        n = norm_buffers(sb, sem, "ffn", SLOTS)
        hf = [sb(f"ffn_h{s}", [P, S]) for s in slots]
        h = [[sb(f"ffn_h_{q}{s}", [P, S], F32R) for q in ("hi", "lo")] for s in slots]
        hid = [[[sb(f"ffn_g{k}_{q}{s}", [P, KH, S], F32R) for q in ("hi", "lo")] for k in range(2)] for s in slots]
        gate = [sb(f"ffn_gate{m}", [P, S]) for m in range(2)]
        full = [sb(f"ffn_full{m}", [P, S]) for m in range(4)]
        yT = [sb(f"ffn_yT{s}", [P, S]) for s in slots]
        flipped = [sem(f"ffn_flipped{s}") for s in slots]
        h_ready = [sem(f"ffn_h_ready{s}") for s in slots]
        h_high = [sem(f"ffn_h_high{s}") for s in slots]
        h_low = [sem(f"ffn_h_low{s}") for s in slots]
        ring_mm = sem("ffn_ring_mm")
        gate_ready = sem("ffn_gate_ready")
        product_ready = sem("ffn_product_ready")
        gelu_ready = sem("ffn_gelu_ready")
        high = sem("ffn_high")
        low = sem("ffn_low")
        y_mm = [sem(f"ffn_y_mm{s}") for s in slots]
        scaled = [sem(f"ffn_scaled{s}") for s in slots]
        y_flipped = [sem(f"ffn_y_flipped{s}") for s in slots]
        added = [sem(f"ffn_added{s}") for s in slots]
        ring = psum[0:RING]
        bank_y = psum[4:6]
        bank_t = psum[6:8]

        TILES = [(s, 0, m) for s in slots for m in range(KH)] + [(s, k, m) for k in (1, 2) for s in slots for m in range(KH)]
        N = len(TILES)
        BANKS = [(j, which) for j, (_, k, _) in enumerate(TILES) for which in ((0, 1) if k == 0 else (0,))]
        NB = len(BANKS)
        N0 = SLOTS * KH

        def made(i, j):
            return i * N + j + 1

        def layer_done(i, s, k):
            return made(i, TILES.index((s, k, KH - 1)))

        def products(i, j):
            return i * N0 + j + 1

        def gelus(i, j):
            return i * (N - N0) + j - N0 + 1

        with nc.Block() as block:
            def pair(i, last):
                return i

            @block.vector
            def _(dve):
                def tile_of(i, s):
                    return lambda t: r["x"][:, bass.ds(i * SLOTS + s, 1), t, :] if not isinstance(i, int) else r["x"][:, i * SLOTS + s, t, :]

                def body(i, more):
                    for s in slots:
                        dve.wait_ge(h_ready[s], i + 1)
                        dve.tensor_copy(h[s][0][:, :], hf[s][:, :]).then_inc(h_high[s], 1)
                    for j, (s, k, m) in enumerate(TILES):
                        f = full[j % 4]
                        if k == 0:
                            dve.wait_ge(gate_ready, products(i, j))
                            dve.wait_ge(ring_mm, i * NB + 2 * j + 2)
                            if j >= 4:
                                dve.wait_ge(low, made(i, j - 4))
                            else:
                                dve.wait_ge(low, i * N)
                            dve.scalar_tensor_tensor(out=f[:, :], in0=ring[(2 * j + 1) % RING][:, :], scalar=r["w_scale"][:, 1, m:m + 1], in1=gate[j % 2][:, :], op0=ALU.mult, op1=ALU.mult).then_inc(product_ready, 1)
                            dve.wait_ge(product_ready, products(i, j))
                            dve.wait_ge(y_mm[s], i)
                        else:
                            dve.wait_ge(gelu_ready, gelus(i, j))
                        dve.tensor_copy(hid[s][k % 2][0][:, m, :], f[:, :]).then_inc(high, 1)
                        if j == N - 1 - KH:
                            pass
                        if more and j == N - 5:
                            for q in slots:
                                norm_moments(dve, r, n[q], i + 1, tile_of(i + 1, q))
                        if more and j == N - 3:
                            for q in slots:
                                norm_apply(dve, n[q], i + 1, tile_of(i + 1, q))
                    for s in slots:
                        dve.wait_ge(y_flipped[s], i + 1)
                        x = r["x"][:, bass.ds(i * SLOTS + s, 1), :, :].rearrange("p b t n -> p (b t n)")
                        dve.tensor_tensor(x, x, bank_y[s][:, :], ALU.add).then_inc(added[s], 1)

                for q in slots:
                    norm_moments(dve, r, n[q], 0, tile_of(0, q))
                for q in slots:
                    norm_apply(dve, n[q], 0, tile_of(0, q))
                with dve.Fori(0, B // SLOTS - 1) as i:
                    body(i, True)
                body(B // SLOTS - 1, False)

            @block.gpsimd
            def _(pool):
                def body(i, more):
                    for s in slots:
                        pool.wait_ge(h_high[s], i + 1)
                        pool.tensor_tensor(h[s][1][:, :], hf[s][:, :], h[s][0][:, :].bitcast(F32), ALU.subtract).then_inc(h_low[s], 1)
                    for j, (s, k, m) in enumerate(TILES):
                        pool.wait_ge(high, made(i, j))
                        pool.tensor_tensor(hid[s][k % 2][1][:, m, :], full[j % 4][:, :], hid[s][k % 2][0][:, m, :].bitcast(F32), ALU.subtract).then_inc(low, 1)
                        if more and j == N - 5:
                            for q in slots:
                                norm_rstd(pool, r, n[q], i + 1)
                for q in slots:
                    norm_rstd(pool, r, n[q], 0)
                with pool.Fori(0, B // SLOTS - 1) as i:
                    body(i, True)
                body(B // SLOTS - 1, False)

            @block.scalar
            def _(act):
                with act.Fori(0, B // SLOTS) as i:
                    for s in slots:
                        act.wait_ge(flipped[s], i + 1)
                        act.wait_ge(h_low[s], i)
                        modulate(act, r, hf[s][:, :], bank_t[s][:, :], 0, 2, i * SLOTS + s).then_inc(h_ready[s], 1)
                    for j, (s, k, m) in enumerate(TILES):
                        if k == 0:
                            act.wait_ge(ring_mm, i * NB + 2 * j + 1)
                            if j >= 2:
                                act.wait_ge(product_ready, products(i, j - 2))
                            else:
                                act.wait_ge(product_ready, i * N0)
                            act.activation(gate[j % 2][:, :], ring[(2 * j) % RING][:, :], ACT.Silu, scale=r["w_scale"][:, 0, m:m + 1]).then_inc(gate_ready, 1)
                        else:
                            act.wait_ge(ring_mm, i * NB + N0 + j + 1)
                            act.wait_ge(low, made(i, j - 4))
                            act.activation(full[j % 4][:, :], ring[(N0 + j) % RING][:, :], ACT.Gelu, scale=r["w_scale"][:, 1 + k, m:m + 1]).then_inc(gelu_ready, 1)
                    for s in slots:
                        act.wait_ge(y_mm[s], i + 1)
                        act.wait_ge(y_flipped[s], i)
                        act.activation(yT[s][:, :], bank_y[s][:, :], ACT.Copy, scale=r["gain_ffn0"][:, bass.ds(i * SLOTS + s, 1)]).then_inc(scaled[s], 1)

            @block.tensor
            def _(pe):
                def w(col, k, width):
                    at = col + k * width
                    return r["w_hi"][:, at:at + P], r["w_lo"][:, at:at + P]

                with pe.Fori(0, B // SLOTS) as i:
                    for s in slots:
                        pe.wait_ge(n[s]["ready"], i + 1)
                        pe.wait_ge(h_ready[s], i)
                        flip(pe, bank_t[s], lambda t: n[s]["out"][:, t, :], r).then_inc(flipped[s], 1)
                    for g, (j, which) in enumerate(BANKS):
                        s, k, m = TILES[j]
                        acc = ring[g % RING]
                        if g >= RING:
                            pj, pw = BANKS[g - RING]
                            if TILES[pj][1] == 0:
                                pe.wait_ge(product_ready if pw else gate_ready, products(i, pj))
                            else:
                                pe.wait_ge(gelu_ready, gelus(i, pj))
                        else:
                            pe.wait_ge(gelu_ready, i * (N - N0))
                        if k == 0:
                            if m == 0 and which == 0:
                                pe.wait_ge(h_low[s], i + 1)
                            col = (W1, W2)[which] + m * P
                            mm = split_mm(pe, acc[:, :], w(col, 0, 0), [h[s][q][:, :] for q in range(2)], True, True)
                        else:
                            if m == 0:
                                pe.wait_ge(low, layer_done(i, s, k - 1))
                            x = hid[s][(k - 1) % 2]
                            for kk in range(KH):
                                mm = split_mm(pe, acc[:, :], w((H1, H2)[k - 1] + m * P, kk, HID), [x[q][:, kk, :] for q in range(2)], kk == 0, kk == KH - 1)
                        mm.then_inc(ring_mm, 1)
                    for s in slots:
                        pe.wait_ge(low, layer_done(i, s, 2))
                        pe.wait_ge(added[s], i)
                        for kk in range(KH):
                            mm = split_mm(pe, bank_y[s][:, :], w(W3, kk, D), [hid[s][0][q][:, kk, :] for q in range(2)], kk == 0, kk == KH - 1)
                        mm.then_inc(y_mm[s], 1)
                    for s in slots:
                        pe.wait_ge(scaled[s], i + 1)
                        flip(pe, bank_y[s], lambda t: yT[s][:, t * P:(t + 1) * P], r).then_inc(y_flipped[s], 1)


def linear_attention(nc, r, psum):
    SLOTS = 2
    RING = 4
    with ExitStack() as ctx:
        def sb(name, shape, dt=F32):
            return ctx.enter_context(nc.sbuf_tensor(name, shape, dt))

        sem = ctx.enter_context(Signals(nc))

        slots = range(SLOTS)
        n = norm_buffers(sb, sem, "att", SLOTS)
        hT = [sb(f"att_hT{s}", [P, S]) for s in slots]
        h = [[sb(f"att_h_{q}{s}", [P, S], F32R) for q in ("hi", "lo")] for s in slots]
        htok = [sb(f"att_htok{s}", [P, T, D]) for s in slots]
        qT = [sb(f"att_qT{s}", [P, NH, S]) for s in slots]
        v = [sb(f"att_v{s}", [P, T, HV]) for s in slots]
        og = [sb(f"att_og{s}", [P, T, HV]) for s in slots]
        alpha = [sb(f"att_alpha{s}", [GLO + NH, S]) for s in slots]
        cut = [sb(f"att_cut{s}", [GLO + NH, S]) for s in slots]
        start = [sb(f"att_start{s}", [NH, S]) for s in slots]
        decay_in = [sb(f"att_decay_in{s}", [GLO + NH, S], F32R) for s in slots]
        cum = [sb(f"att_cum{s}", [NH, S]) for s in slots]
        ends = [sb(f"att_ends{s}", [NH, T, NH]) for s in slots]
        cumT = [sb(f"att_cumT{s}", [P, T, NH]) for s in slots]
        total = [sb(f"att_total{s}", [P, T, NH]) for s in slots]
        decay = [sb(f"att_decay{m}", [P, S]) for m in range(2)]
        prob = [sb(f"att_prob{m}", [P, S]) for m in range(2)]
        vw = sb("att_vw", [P, T, HV])
        state = sb("att_state", [P, T, HV])
        mix = sb("att_mix", [P, T, HV])
        gT = sb("att_gT", [P, 2, S])
        upd = [htok[s] for s in slots]

        def sems(name):
            return [sem(f"att_{name}{s}") for s in slots]

        ring_mm = sem("att_ring_mm")
        flipped, h_ready, h_high, h_low = sems("flipped"), sems("h_ready"), sems("h_high"), sems("h_low")
        q_ready, vo_ready, v_ready, alpha_ready = sems("q_ready"), sems("vo_ready"), sems("v_ready"), sems("alpha_ready")
        htok_ready, cut_ready, high_ready, decays_ready = sems("htok_ready"), sems("cut_ready"), sems("high_ready"), sems("decays_ready")
        start_ready, cum_ready, ends_ready = sems("start_ready"), sems("cum_ready"), sems("ends_ready")
        cumT_ready, total_ready = sems("cumT_ready"), sems("total_ready")
        decay_ready, prob_ready, vw_ready = sem("att_decay_ready"), sem("att_prob_ready"), sem("att_vw_ready")
        intra_mm, inter_mm, state_ready = sem("att_intra_mm"), sem("att_inter_mm"), sem("att_state_ready")
        mixed, gated, gT_ready, scaled, added = sem("att_mixed"), sem("att_gated"), sem("att_gT_ready"), sems("scaled"), sems("added")
        ring = psum[0:RING]
        bank_o = psum[4:6]
        bank_s = psum[6:8]

        USES = []
        for s in slots:
            USES += [(s, "flip", 0)] + [(s, "q", k) for k in range(NH)] + [(s, "vo", t) for t in range(T)] + [(s, "alpha", 0), (s, "htok", 0)]
        for s in slots:
            USES += [(s, "cumT", 0), (s, "total", 0)]
            for k in range(NH):
                USES += [(s, "decay", k), (s, "score", k)]
            USES += [(s, "state", c) for c in range(3)]
        for s in slots:
            USES += [(s, "gT", k) for k in range(2)] + [(s, "y", 0)]
        FULLS = len(USES)
        while len(USES) % RING:
            USES.append((0, "none", 0))
        N = len(USES)

        def reader(use):
            s, what, k = use
            return {
                "flip": (h_ready[s], 1, 0), "q": (q_ready[s], NH, k), "vo": (vo_ready[s], T, k), "alpha": (alpha_ready[s], 1, 0),
                "htok": (htok_ready[s], 1, 0), "cumT": (cumT_ready[s], 1, 0), "total": (total_ready[s], 1, 0),
                "decay": (decay_ready, SLOTS * NH, s * NH + k), "score": (prob_ready, SLOTS * NH, s * NH + k),
                "state": (state_ready, SLOTS * 3, s * 3 + k), "gT": (gT_ready, SLOTS * 2, s * 2 + k), "y": (scaled[s], 1, 0),
            }.get(what)

        def full(i, s, what, k=0):
            return i * FULLS + USES.index((s, what, k)) + 1

        def bank(s, what, k=0):
            return ring[USES.index((s, what, k)) % RING]

        def nth(i, s, per, k):
            return i * SLOTS * per + s * per + k + 1

        with nc.Block() as block:
            def x_tile(i, s):
                return lambda t: r["x"][:, bass.ds(i * SLOTS + s, 1), t, :]

            def x_all(i, s):
                return r["x"][:, bass.ds(i * SLOTS + s, 1), :, :].rearrange("p b t n -> p (b t) n")

            @block.vector
            def _(dve):
                def body(i, more):
                    for s in slots:
                        dve.wait_ge(h_ready[s], i + 1)
                        dve.tensor_copy(h[s][0][:, :], hT[s][:, :]).then_inc(h_high[s], 1)
                        for t in range(T):
                            dve.wait_ge(vo_ready[s], i * T + t + 1)
                            ins = dve.tensor_copy(v[s][:, t, :], bank(s, "vo", t)[:, 0:HV])
                            ins.then_inc(v_ready[s], 1)
                        dve.wait_ge(alpha_ready[s], i + 1)
                        dve.tensor_tensor(cut[s][:, :], alpha[s][:, :], r["keep"][:, :], ALU.mult).then_inc(cut_ready[s], 1)
                        dve.wait_ge(cut_ready[s], i + 1)
                        dve.tensor_copy(decay_in[s][:, :], cut[s][:, :]).then_inc(high_ready[s], 1)
                        dve.tensor_tensor(start[s][:, :], alpha[s][0:NH, :], cut[s][0:NH, :], ALU.subtract).then_inc(start_ready[s], 1)
                        dve.wait_ge(high_ready[s], i + 1)
                        lo = slice(GLO, GLO + NH)
                        dve.tensor_tensor(decay_in[s][lo, :], cut[s][lo, :], decay_in[s][lo, :].bitcast(F32), ALU.subtract).then_inc(decays_ready[s], 1)
                        dve.wait_ge(start_ready[s], i + 1)
                        dve.tensor_tensor_scan(cum[s][:, :], cut[s][0:NH, :], start[s][:, :], 0.0, ALU.mult, ALU.add).then_inc(cum_ready[s], 1)
                        dve.wait_ge(cum_ready[s], i + 1)
                        last = cum[s][:, :].rearrange("p (c n) -> p c n", c=T)[:, :, P - 1:P]
                        dve.tensor_tensor(ends[s][:, :, :], last.broadcast_to([NH, T, NH]), over(r["eye8"][:, :], 1, [NH, T, NH]), ALU.mult).then_inc(ends_ready[s], 1)
                    for s in slots:
                        dve.wait_ge(ring_mm, full(i, s, "cumT"))
                        dve.tensor_copy(cumT[s][:, :, :].rearrange("p c n -> p (c n)"), bank(s, "cumT")[:, 0:T * NH]).then_inc(cumT_ready[s], 1)
                        dve.wait_ge(ring_mm, full(i, s, "total"))
                        dve.tensor_copy(total[s][:, :, :].rearrange("p c n -> p (c n)"), bank(s, "total")[:, 0:T * NH]).then_inc(total_ready[s], 1)
                        for k in range(NH):
                            m = (s * NH + k) % 2
                            dve.wait_ge(ring_mm, full(i, s, "decay", k))
                            if s * NH + k >= 2:
                                dve.wait_ge(vw_ready, nth(i, s, NH, k - 2))
                            else:
                                dve.wait_ge(vw_ready, i * SLOTS * NH)
                            dve.tensor_tensor_scan(decay[m][:, :], bank(s, "decay", k)[:, :], r["ident4"][:, :], 0.0, ALU.mult, ALU.add).then_inc(decay_ready, 1)
                            dve.wait_ge(decay_ready, nth(i, s, NH, k))
                            dve.wait_ge(ring_mm, full(i, s, "score", k))
                            if s * NH + k >= 2:
                                dve.wait_ge(intra_mm, nth(i, s, NH, k - 2))
                            else:
                                dve.wait_ge(intra_mm, i * SLOTS * NH)
                            dve.tensor_tensor(prob[m][:, :], bank(s, "score", k)[:, :], decay[m][:, :], ALU.mult).then_inc(prob_ready, 1)
                        for c in range(3):
                            new = state[:, c + 1, :]
                            ps = bank(s, "state", c)[:, 0:HV]
                            dve.wait_ge(ring_mm, full(i, s, "state", c))
                            if c == 0:
                                dve.wait_ge(inter_mm, i * SLOTS + s)
                                dve.tensor_copy(new, ps).then_inc(state_ready, 1)
                            else:
                                dve.wait_ge(state_ready, nth(i, s, 3, c - 1))
                                tot = over(total[s][:, c, :], 2, [P, NH, DV])
                                dve.tensor_tensor(mix[:, c, :].rearrange("p (h n) -> p h n", h=NH), state[:, c, :].rearrange("p (h n) -> p h n", h=NH), tot, ALU.mult).then_inc(mixed, 1)
                                dve.wait_ge(mixed, i * SLOTS * MIXES + s * MIXES + c)
                                dve.tensor_tensor(new, mix[:, c, :], ps, ALU.add).then_inc(state_ready, 1)
                        dve.wait_ge(inter_mm, i * SLOTS + s + 1)
                        for c in range(1, T):
                            src = bank_s[(c - 1) // 2][:, ((c - 1) % 2) * HV:((c - 1) % 2 + 1) * HV]
                            ins = dve.tensor_tensor(mix[:, c, :].rearrange("p (h n) -> p h n", h=NH), src.rearrange("p (h n) -> p h n", h=NH), over(cumT[s][:, c, :], 2, [P, NH, DV]), ALU.mult)
                        ins.then_inc(mixed, 1)
                        dve.wait_ge(mixed, i * SLOTS * MIXES + s * MIXES + 3)
                        dve.wait_ge(intra_mm, nth(i, s, NH, NH - 1))
                        dve.tensor_copy(mix[:, 0, :], bank_o[0][:, 0:HV])
                        dve.tensor_tensor(mix[:, 1, :], mix[:, 1, :], bank_o[0][:, HV:2 * HV], ALU.add)
                        dve.tensor_tensor(mix[:, 2:4, :].rearrange("p c n -> p (c n)"), mix[:, 2:4, :].rearrange("p c n -> p (c n)"), bank_o[1][:, :], ALU.add).then_inc(mixed, 1)
                        dve.wait_ge(mixed, i * SLOTS * MIXES + s * MIXES + 4)
                        dve.tensor_tensor(og[s][:, :, :], mix[:, :, :], og[s][:, :, :], ALU.mult).then_inc(gated, 1)
                    if more:
                        for s in slots:
                            norm_moments(dve, r, n[s], i + 1, x_tile(i + 1, s))
                        for s in slots:
                            norm_apply(dve, n[s], i + 1, x_tile(i + 1, s))
                    for s in slots:
                        dve.wait_ge(ring_mm, full(i, s, "y"))
                        dve.wait_ge(added[s], i)
                        g = r["gain_attn1"][:, bass.ds(i * SLOTS + s, 1), :].broadcast_to([P, T, D])
                        dve.tensor_tensor(upd[s][:, :, :], bank(s, "y")[:, :].rearrange("p (t n) -> p t n", t=T), g, ALU.mult).then_inc(scaled[s], 1)

                MIXES = 4
                for s in slots:
                    norm_moments(dve, r, n[s], 0, x_tile(0, s))
                for s in slots:
                    norm_apply(dve, n[s], 0, x_tile(0, s))
                with dve.Fori(0, B // SLOTS - 1) as i:
                    body(i, True)
                body(B // SLOTS - 1, False)

            @block.gpsimd
            def _(pool):
                def body(i, more):
                    for s in slots:
                        pool.wait_ge(h_high[s], i + 1)
                        pool.tensor_tensor(h[s][1][:, :], hT[s][:, :], h[s][0][:, :].bitcast(F32), ALU.subtract).then_inc(h_low[s], 1)
                    for s in slots:
                        pool.wait_ge(v_ready[s], (i + 1) * T)
                        for k in range(NH):
                            m = (s * NH + k) % 2
                            pool.wait_ge(decay_ready, nth(i, s, NH, k))
                            if k == 0:
                                pool.wait_ge(state_ready, (i * SLOTS + s) * 3)
                            heads = slice(k * DV, (k + 1) * DV)
                            last = decay[m][:, :].rearrange("p (c n) -> p c n", c=T)[:, :, P - 1:P]
                            pool.tensor_tensor(vw[:, :, heads], v[s][:, :, heads], last.broadcast_to([P, T, DV]), ALU.mult).then_inc(vw_ready, 1)
                    if more:
                        for s in slots:
                            norm_rstd(pool, r, n[s], i + 1)
                    for s in slots:
                        pool.wait_ge(scaled[s], i + 1)
                        pool.tensor_tensor(x_all(i, s), x_all(i, s), upd[s][:, :, :], ALU.add).then_inc(added[s], 1)

                for s in slots:
                    norm_rstd(pool, r, n[s], 0)
                with pool.Fori(0, B // SLOTS - 1) as i:
                    body(i, True)
                body(B // SLOTS - 1, False)

            @block.scalar
            def _(act):
                with act.Fori(0, B // SLOTS) as i:
                    for s in slots:
                        act.wait_ge(ring_mm, full(i, s, "flip"))
                        act.wait_ge(h_low[s], i)
                        modulate(act, r, hT[s][:, :], bank(s, "flip")[:, :], 1, 0, i * SLOTS + s).then_inc(h_ready[s], 1)
                        for k in range(NH):
                            act.wait_ge(ring_mm, full(i, s, "q", k))
                            if k == 0:
                                act.wait_ge(inter_mm, i * SLOTS)
                            act.copy(qT[s][:, k, :], bank(s, "q", k)[:, :]).then_inc(q_ready[s], 1)
                        for t in range(T):
                            act.wait_ge(ring_mm, full(i, s, "vo", t))
                            if t == 0:
                                act.wait_ge(gT_ready, i * SLOTS * 2)
                            act.activation(og[s][:, t, :], bank(s, "vo", t)[:, HV:2 * HV], ACT.Sigmoid).then_inc(vo_ready[s], 1)
                        act.wait_ge(ring_mm, full(i, s, "alpha"))
                        act.activation(alpha[s][:, :], bank(s, "alpha")[0:GLO + NH, :], ACT.Sigmoid, scale=1.0 / GATE_NORM, bias=r["gate_bias"][0:GLO + NH, 0:1]).then_inc(alpha_ready[s], 1)
                        act.wait_ge(ring_mm, full(i, s, "htok"))
                        act.copy(htok[s][:, :, :].rearrange("p t n -> p (t n)"), bank(s, "htok")[:, :]).then_inc(htok_ready[s], 1)
                    for s in slots:
                        for k in range(2):
                            act.wait_ge(ring_mm, full(i, s, "gT", k))
                            act.copy(gT[:, k, :], bank(s, "gT", k)[:, :]).then_inc(gT_ready, 1)

            @block.tensor
            def _(pe):
                def claim(i, s, what, k=0):
                    at = USES.index((s, what, k))
                    before = USES[at - RING] if at >= RING else USES[at - RING + N]
                    if reader(before) is None:
                        before = USES[at - 2 * RING + N]
                    signal, per, index = reader(before)
                    pe.wait_ge(signal, i * per + (index + 1 if at >= RING else 0))
                    if what == "vo" or True:
                        if before[1] == "vo":
                            pe.wait_ge(v_ready[before[0]], i * T + (before[2] + 1 if at >= RING else 0))
                    return ring[at % RING]

                with pe.Fori(0, B // SLOTS) as i:
                    for s in slots:
                        pe.wait_ge(n[s]["ready"], i + 1)
                        b = claim(i, s, "flip")
                        flip(pe, b, lambda t: n[s]["out"][:, t, :], r).then_inc(ring_mm, 1)
                        pe.wait_ge(h_low[s], i + 1)
                        hh = [h[s][q][:, :] for q in range(2)]
                        for k in range(NH):
                            b = claim(i, s, "q", k)
                            split_mm(pe, b[:, :], (r["m_hi"][:, k, :], r["m_lo"][:, k, :]), hh, True, True).then_inc(ring_mm, 1)
                        for t in range(T):
                            b = claim(i, s, "vo", t)
                            c = slice(t * P, (t + 1) * P)
                            split_mm(pe, b[:, :], [q[:, c] for q in hh], (r["v_hi"][:, VO:VO + 2 * HV], r["v_lo"][:, VO:VO + 2 * HV]), True, True).then_inc(ring_mm, 1)
                        b = claim(i, s, "alpha")
                        split_mm(pe, b[:, :], (r["v_hi"][:, GT:GT + P], r["v_lo"][:, GT:GT + P]), hh, True, True).then_inc(ring_mm, 1)
                        b = claim(i, s, "htok")
                        flip(pe, b, lambda t: hT[s][:, t * P:(t + 1) * P], r).then_inc(ring_mm, 1)
                    for s in slots:
                        wait_apart(pe, r, cum_ready[s], i + 1)
                        b = claim(i, s, "cumT")
                        for c in range(T):
                            mm = pe.transpose(b[:, c * NH:(c + 1) * NH], cum[s][:, c * P:(c + 1) * P], r["ident"][0:NH, 0:NH])
                        mm.then_inc(ring_mm, 1)
                        pe.wait_ge(ends_ready[s], i + 1)
                        b = claim(i, s, "total")
                        pe.matmul(b[:, 0:T * NH], r["ones8"][:, :], ends[s][:, :, :].rearrange("p c n -> p (c n)"), start=True, stop=True).then_inc(ring_mm, 1)
                        pe.wait_ge(decays_ready[s], i + 1)
                        pe.wait_ge(q_ready[s], (i + 1) * NH)

                        def inside(k):
                            m = (s * NH + k) % 2
                            pe.wait_ge(prob_ready, nth(i, s, NH, k))
                            if k == 0:
                                pe.wait_ge(gated, i * SLOTS + s)
                            for c in range(T):
                                o = bank_o[c // 2][:, (c % 2) * HV + k * DV:(c % 2) * HV + (k + 1) * DV]
                                mm = pe.matmul(o, prob[m][:, c * P:(c + 1) * P], v[s][:, c, k * DV:(k + 1) * DV], start=True, stop=True)
                            mm.then_inc(intra_mm, 1)

                        for k in range(NH):
                            b = claim(i, s, "decay", k)
                            pe.matmul(b[:, :], r["sel"][:, k, :], decay_in[s][:, :], start=True, stop=True).then_inc(ring_mm, 1)
                            b = claim(i, s, "score", k)
                            for c in range(T):
                                cc = slice(c * P, (c + 1) * P)
                                mm = pe.matmul(b[:, cc], hT[s][:, cc], qT[s][:, k, cc], start=True, stop=True)
                            mm.then_inc(ring_mm, 1)
                            if k >= 1:
                                if k == 1:
                                    pe.wait_ge(v_ready[s], (i + 1) * T)
                                inside(k - 1)
                        pe.wait_ge(vw_ready, nth(i, s, NH, NH - 1))
                        pe.wait_ge(htok_ready[s], i + 1)
                        for c in range(3):
                            b = claim(i, s, "state", c)
                            pe.matmul(b[:, 0:HV], htok[s][:, c, :], vw[:, c, :], start=True, stop=True).then_inc(ring_mm, 1)
                        inside(NH - 1)
                        for c in range(1, T):
                            pe.wait_ge(state_ready, nth(i, s, 3, c - 1))
                            for k in range(NH):
                                at = ((c - 1) % 2) * HV + k * DV
                                mm = pe.matmul(bank_s[(c - 1) // 2][:, at:at + DV], qT[s][:, k, c * P:(c + 1) * P], state[:, c, k * DV:(k + 1) * DV], start=True, stop=True)
                        mm.then_inc(inter_mm, 1)
                    for s in slots:
                        pe.wait_ge(gated, i * SLOTS + s + 1)
                        for k in range(2):
                            b = claim(i, s, "gT", k)
                            flip(pe, b, lambda t: og[s][:, t, k * P:(k + 1) * P], r).then_inc(ring_mm, 1)
                        pe.wait_ge(gT_ready, (i * SLOTS + s + 1) * 2)
                        b = claim(i, s, "y")
                        for t in range(T):
                            c = slice(t * P, (t + 1) * P)
                            for k in range(2):
                                mm = pe.matmul(b[:, c], gT[:, k, c], r["wo"][:, k, :], start=(k == 0), stop=(k == 1))
                        mm.then_inc(ring_mm, 1)


def lora_ffn(nc, r, psum, out):
    SLOTS = 2
    with ExitStack() as ctx:
        def sb(name, shape, dt=F32):
            return ctx.enter_context(nc.sbuf_tensor(name, shape, dt))

        sem = ctx.enter_context(Signals(nc))

        slots = range(SLOTS)
        n = norm_buffers(sb, sem, "lora", SLOTS)
        hT = [sb(f"lora_hT{s}", [P, S]) for s in slots]
        h = [[sb(f"lora_h_{q}{s}", [P, S], F32R) for q in ("hi", "lo")] for s in slots]
        hid = [sb(f"lora_hid{s}", [P, KH, S]) for s in slots]
        def pairs(name, shape):
            return [[sb(f"lora_{name}{k}{s}", shape) for s in slots] for k in range(2)]

        top, shifted, expo = pairs("top", [P, T]), pairs("shifted", [P, T, E]), pairs("expo", [P, T, E])
        den, inv, prob = pairs("den", [P, T]), pairs("inv", [P, T]), pairs("prob", [P, T, E])
        zg, zT = pairs("zg", [P, T, ER]), pairs("zT", [ER + 1, S])
        upd = [sb(f"lora_upd{s}", [P, T, D]) for s in slots]
        res = [sb(f"lora_res{s}", [P, T, D]) for s in slots]

        def sems(name):
            return [sem(f"lora_{name}{s}") for s in slots]

        def sems2(name):
            return [sems(f"{name}_{k}_") for k in range(2)]

        ones_set = sem("lora_ones_set")
        flipped, h_ready, h_high, h_low = sems("flipped"), sems("h_ready"), sems("h_high"), sems("h_low")
        down_mm, top_ready, shift_ready, expo_ready = sems2("down_mm"), sems2("top_ready"), sems2("shift_ready"), sems2("expo_ready")
        den_ready, inv_ready, prob_ready, zg_ready = sems2("den_ready"), sems2("inv_ready"), sems2("prob_ready"), sems2("zg_ready")
        zT_mm, zT_ready = sems2("zT_mm"), sems2("zT_ready")
        hid_mm, hid_ready = sem("lora_hid_mm"), sem("lora_hid_ready")
        y_mm, scaled, res_ready, stored = sems("y_mm"), sems("scaled"), sems("res_ready"), sems("stored")
        bank_t = psum[0:2]
        ring = psum[2:4]
        bank_e = [psum[4:6], psum[6:8]]
        WIDE = 256

        def down(k, s, t0, t1):
            if k == 0:
                return bank_t[s][:, 0:T * 32].rearrange("p (t n) -> p t n", t=T)[:, t0:t1, 0:AR]
            return bank_e[s][t0 // 2][:, :].rearrange("p (t n) -> p t n", t=2)[:, 0:t1 - t0, D:D + AR]

        SPANS = [[(0, T)], [(0, 2), (2, T)]]

        with nc.Block() as block:
            @block.vector
            def _(dve):
                def x_tile(i, s):
                    return lambda t: r["x"][:, bass.ds(i * SLOTS + s, 1), t, :]

                def route(i, s, k):
                    dve.wait_ge(down_mm[k][s], i + 1)
                    for a, b in SPANS[k]:
                        ins = dve.tensor_reduce(top[k][s][:, a:b], down(k, s, a, b)[:, :, ER:AR], AX_X, ALU.max)
                    ins.then_inc(top_ready[k][s], 1)
                    dve.wait_ge(top_ready[k][s], i + 1)
                    for a, b in SPANS[k]:
                        ins = dve.tensor_tensor(shifted[k][s][:, a:b, :], down(k, s, a, b)[:, :, ER:AR], over(top[k][s][:, a:b], 2, [P, b - a, E]), ALU.subtract)
                    ins.then_inc(shift_ready[k][s], 1)
                    dve.wait_ge(expo_ready[k][s], i + 1)
                    dve.tensor_reduce(den[k][s][:, :], expo[k][s][:, :, :], AX_X, ALU.add).then_inc(den_ready[k][s], 1)
                    dve.wait_ge(den_ready[k][s], i + 1)
                    dve.reciprocal(inv[k][s][:, :], den[k][s][:, :]).then_inc(inv_ready[k][s], 1)
                    dve.wait_ge(inv_ready[k][s], i + 1)
                    dve.tensor_tensor(prob[k][s][:, :, :], expo[k][s][:, :, :], over(inv[k][s][:, :], 2, [P, T, E]), ALU.mult).then_inc(prob_ready[k][s], 1)
                    dve.wait_ge(prob_ready[k][s], i + 1)
                    for a, b in SPANS[k]:
                        for t in range(a, b):
                            z = down(k, s, a, b)[:, t - a, 0:ER].rearrange("p (e n) -> p e n", e=E)
                            ins = dve.tensor_tensor(zg[k][s][:, t, :].rearrange("p (e n) -> p e n", e=E), z, over(prob[k][s][:, t, :], 2, [P, E, R]), ALU.mult)
                    ins.then_inc(zg_ready[k][s], 1)

                def body(i, more):
                    for s in slots:
                        dve.wait_ge(h_ready[s], i + 1)
                        dve.tensor_copy(h[s][0][:, :], hT[s][:, :]).then_inc(h_high[s], 1)
                    for s in slots:
                        route(i, s, 0)
                    if more:
                        for s in slots:
                            norm_moments(dve, r, n[s], i + 1, x_tile(i + 1, s))
                        for s in slots:
                            norm_apply(dve, n[s], i + 1, x_tile(i + 1, s))
                    for s in slots:
                        route(i, s, 1)
                    for s in slots:
                        dve.wait_ge(y_mm[s], i + 1)
                        dve.wait_ge(res_ready[s], i)
                        g = r["gain_ffn1"][:, bass.ds(i * SLOTS + s, 1), :].broadcast_to([P, 2, D])
                        for q in range(2):
                            y = bank_e[s][q][:, :].rearrange("p (t n) -> p t n", t=2)[:, :, 0:D]
                            ins = dve.tensor_tensor(upd[s][:, 2 * q:2 * q + 2, :], y, g, ALU.mult)
                        ins.then_inc(scaled[s], 1)

                for k in range(2):
                    for s in slots:
                        dve.memset(zT[k][s][:, :], 1.0).then_inc(ones_set, 1)
                for s in slots:
                    norm_moments(dve, r, n[s], 0, x_tile(0, s))
                for s in slots:
                    norm_apply(dve, n[s], 0, x_tile(0, s))
                with dve.Fori(0, B // SLOTS - 1) as i:
                    body(i, True)
                body(B // SLOTS - 1, False)

            @block.gpsimd
            def _(pool):
                def body(i, more):
                    for s in slots:
                        pool.wait_ge(h_high[s], i + 1)
                        pool.tensor_tensor(h[s][1][:, :], hT[s][:, :], h[s][0][:, :].bitcast(F32), ALU.subtract).then_inc(h_low[s], 1)
                    if more:
                        for s in slots:
                            norm_rstd(pool, r, n[s], i + 1)
                    for s in slots:
                        pool.wait_ge(scaled[s], i + 1)
                        pool.wait_ge(stored[s], i * 16)
                        x = r["x"][:, bass.ds(i * SLOTS + s, 1), :, :].rearrange("p b t n -> p (b t) n")
                        pool.tensor_tensor(res[s][:, :, :], x, upd[s][:, :, :], ALU.add).then_inc(res_ready[s], 1)

                for s in slots:
                    norm_rstd(pool, r, n[s], 0)
                with pool.Fori(0, B // SLOTS - 1) as i:
                    body(i, True)
                body(B // SLOTS - 1, False)

            @block.sync
            def _(sp):
                with sp.Fori(0, B // SLOTS) as i:
                    for s in slots:
                        sp.wait_ge(res_ready[s], i + 1)
                        dst = out[bass.ds(i * SLOTS + s, 1), :, :].rearrange("b (t p) n -> p (b t) n", p=P)
                        sp.dma_start(dst, res[s][:, :, :]).then_inc(stored[s], 16)
                for s in slots:
                    sp.wait_ge(stored[s], 16 * (B // SLOTS))

            @block.scalar
            def _(act):
                act.wait_ge(ones_set, 4)
                with act.Fori(0, B // SLOTS) as i:
                    for s in slots:
                        act.wait_ge(flipped[s], i + 1)
                        act.wait_ge(h_low[s], i)
                        modulate(act, r, hT[s][:, :], bank_t[s][:, :], 1, 2, i * SLOTS + s).then_inc(h_ready[s], 1)
                    for s in slots:
                        act.wait_ge(shift_ready[0][s], i + 1)
                        act.activation(expo[0][s][:, :, :], shifted[0][s][:, :, :], ACT.Exp).then_inc(expo_ready[0][s], 1)
                    for s in slots:
                        act.wait_ge(zT_mm[0][s], i + 1)
                        act.copy(zT[0][s][0:ER, :], bank_t[s][0:ER, :]).then_inc(zT_ready[0][s], 1)
                    for s in slots:
                        for m in range(KH):
                            g = s * KH + m
                            act.wait_ge(hid_mm, i * SLOTS * KH + g + 1)
                            act.wait_ge(down_mm[1][s], i)
                            act.activation(hid[s][:, m, :], ring[g % 2][:, :], ACT.Relu).then_inc(hid_ready, 1)
                    for s in slots:
                        act.wait_ge(shift_ready[1][s], i + 1)
                        act.activation(expo[1][s][:, :, :], shifted[1][s][:, :, :], ACT.Exp).then_inc(expo_ready[1][s], 1)
                    for s in slots:
                        act.wait_ge(zT_mm[1][s], i + 1)
                        act.copy(zT[1][s][0:ER, :], bank_t[s][0:ER, :]).then_inc(zT_ready[1][s], 1)

            @block.tensor
            def _(pe):
                def flip_z(i, s, k):
                    pe.wait_ge(zg_ready[k][s], i + 1)
                    for t in range(T):
                        mm = pe.transpose(bank_t[s][0:ER, t * P:(t + 1) * P], zg[k][s][:, t, :], r["ident"][:, :])
                    mm.then_inc(zT_mm[k][s], 1)

                with pe.Fori(0, B // SLOTS) as i:
                    for s in slots:
                        pe.wait_ge(n[s]["ready"], i + 1)
                        pe.wait_ge(zT_ready[1][s], i)
                        flip(pe, bank_t[s], lambda t: n[s]["out"][:, t, :], r).then_inc(flipped[s], 1)
                    for s in slots:
                        pe.wait_ge(h_ready[s], i + 1)
                        for t in range(T):
                            mm = pe.matmul(bank_t[s][:, t * 32:t * 32 + AR], hT[s][:, t * P:(t + 1) * P], r["ar1"][:, :], start=True, stop=True)
                        mm.then_inc(down_mm[0][s], 1)
                    for s in slots:
                        flip_z(i, s, 0)
                    for s in slots:
                        pe.wait_ge(h_low[s], i + 1)
                        for m in range(KH):
                            g = s * KH + m
                            pe.wait_ge(hid_ready, i * SLOTS * KH + max(g - 1, 0))
                            c = slice(m * P, (m + 1) * P)
                            b = ring[g % 2]
                            at = slice(F1 + m * P, F1 + (m + 1) * P)
                            split_mm(pe, b[:, :], (r["v_hi"][:, at], r["v_lo"][:, at]), [h[s][q][:, :] for q in range(2)], True, False)
                            if m == 0:
                                pe.wait_ge(zT_ready[0][s], i + 1)
                            pe.matmul(b[:, :], r["b1e"][:, c], zT[0][s][:, :], start=False, stop=True).then_inc(hid_mm, 1)
                    for s in slots:
                        pe.wait_ge(hid_ready, i * SLOTS * KH + (s + 1) * KH)
                        pe.wait_ge(scaled[s], i)
                        for t in range(T):
                            b = bank_e[s][t // 2]
                            at = (t % 2) * WIDE
                            for k in range(KH):
                                mm = pe.matmul(b[:, at:at + D + AR], hid[s][:, k, t * P:(t + 1) * P], r["war2"][:, k, :], start=(k == 0 and t % 2 == 0), stop=(k == KH - 1), skip_group_check=True)
                        mm.then_inc(down_mm[1][s], 1)
                    for s in slots:
                        flip_z(i, s, 1)
                    for s in slots:
                        pe.wait_ge(zT_ready[1][s], i + 1)
                        for t in range(T):
                            at = (t % 2) * WIDE
                            mm = pe.matmul(bank_e[s][t // 2][:, at:at + D], zT[1][s][:, t * P:(t + 1) * P], r["b2e"][:, :], start=False, stop=True, skip_group_check=True)
                        mm.then_inc(y_mm[s], 1)


def kernel(**inputs):
    import numpy as np
    import concourse.bacc as bacc
    from concourse import mybir as _mybir
    from concourse.bass_utils import run_bass_kernel_spmd

    a = {k: np.asarray(v) for k, v in inputs.items()}

    def col(x, n=None):
        return x.reshape(-1, 1)

    def tiles(wT, k):
        return wT.reshape(k, P, -1).transpose(1, 0, 2).reshape(P, -1)

    keep = np.ones((GLO + NH, S), np.float32)
    keep[:, ::P] = 0
    sel = np.zeros((GLO + NH, NH, P), np.float32)
    for h in range(NH):
        sel[h, h] = sel[GLO + h, h] = 1
    A1 = a["L1_ffn_A1"].transpose(1, 0, 2).reshape(D, ER)
    A2 = a["L1_ffn_A2"].transpose(1, 0, 2).reshape(HID, ER)
    arrays = {
        "x": a["L0_attn_x"],
        "cT": np.stack([a["L0_c"].T, a["L1_c"].T], 1),
        "wmod": np.stack([a["L0_wmod"].reshape(D, 6, D), a["L1_wmod"].reshape(D, 6, D)], 1),
        "ln_gamma": a["L0_attn_ln_gamma"], "ln_beta": a["L0_attn_ln_beta"],
        "B_row": a["L0_attn_B_param"].reshape(-1), "B_col": col(a["L0_attn_B_param"]),
        "bp": col(a["L0_attn_bp"]), "lam": col(a["L0_attn_log_neg_lambdas"]),
        "Wp": a["L0_attn_Wp"], "Wo0": a["L0_attn_Wo"], "bo": a["L0_attn_bo"].reshape(1, D), "C": a["L0_attn_C_param"],
        "w3_s": col(a["L0_ffn_w3_s"]),
        "w_scale": np.stack([a[f"L0_ffn_{k}_s"].reshape(KH, P).T for k in ("w1", "w2", "h1", "h2")], 1),
        "w_all": np.concatenate([
            a["L0_ffn_w1_w"].T, a["L0_ffn_w2_w"].T, tiles(a["L0_ffn_h1_w"].T, KH),
            tiles(a["L0_ffn_h2_w"].T, KH), tiles(a["L0_ffn_w3_w"].T, KH)], 1),
        "WqT": a["L1_attn_Wq"].reshape(D, NH, DK).transpose(2, 1, 0),
        "WkT": a["L1_attn_Wk"].reshape(D, NH, DK).transpose(2, 1, 0),
        "WvWog": np.concatenate([a["L1_attn_Wv"], a["L1_attn_Wog"]], 1),
        "Wg": a["L1_attn_Wg"], "bg": col(a["L1_attn_bg"]),
        "Wo1": a["L1_attn_Wo"].reshape(2, P, D).transpose(1, 0, 2),
        "W1": a["L1_ffn_W1"],
        "B1e": np.concatenate([a["L1_ffn_B1"].reshape(ER, HID), a["L1_ffn_b1"].reshape(1, HID)], 0),
        "B2e": np.concatenate([a["L1_ffn_B2"].reshape(ER, D), a["L1_ffn_b2"].reshape(1, D)], 0),
        "AR1": np.concatenate([A1, a["L1_ffn_R1"]], 1),
        "WAR2": np.concatenate([a["L1_ffn_W2"], A2, a["L1_ffn_R2"]], 1).reshape(KH, P, D + AR).transpose(1, 0, 2),
        "ident": np.eye(P, dtype=np.float32), "eye8": np.eye(NH, dtype=np.float32), "keep": keep, "sel": sel,
    }
    nc = bacc.Bacc("TRN2", target_bir_lowering=False, num_devices=1)
    given, d = {}, {}
    for name, x in arrays.items():
        x = np.ascontiguousarray(x)
        given[f"in_{name}"] = x
        d[name] = nc.dram_tensor(f"in_{name}", x.shape, _mybir.dt.from_np(x.dtype), kind="ExternalInput").ap()
    out = nc.dram_tensor("out", (B, S, D), _mybir.dt.float32, kind="ExternalOutput").ap()
    build(nc, d, out)
    result = run_bass_kernel_spmd(nc, [given], core_ids=[0])
    return result.results[0]["out"]
```

```python
from contextlib import ExitStack

import concourse.bass as bass
from concourse import mybir

F32 = mybir.dt.float32
F32R = mybir.dt.float32r
ACT = mybir.ActivationFunctionType
ALU = mybir.AluOpType
AX_X = mybir.AxisListType.X

P = 128
B = 8
S = 512
T = S // P
D = 128
SD = 32
NH = 8
DV = 32
HV = NH * DV
HID = 512
KH = HID // P
E = 3
R = 8
ER = E * R
AR = ER + E
DK = 128
LN_EPS = 1e-5
GATE_NORM = 16.0
GLO = 32
W1, W2, H1, H2, W3 = 0, 512, 1024, 3072, 5120
WCOLS = 5632
VO, F1, GT = 0, 512, 1024
VCOLS = 1024 + 128
SA, CA, GA, SB, CB, GB = range(6)


def build(nc, d, out):
    with ExitStack() as ctx:
        def sb(name, shape, dt=F32):
            return ctx.enter_context(nc.sbuf_tensor(name, shape, dt))

        r = {"set_up": ctx.enter_context(nc.semaphore("set_up"))}
        r["x"] = sb("x", [P, B, T, D])
        r["ident"] = sb("ident", [P, P])
        r["ident4"] = sb("ident4", [P, S])
        r["neg_half"] = sb("neg_half", [P, T])
        r["mod"] = sb("mod", [P, 2, 4, B])
        r["gain_ffn0"] = sb("gain_ffn0", [P, B])
        r["gain_attn1"] = sb("gain_attn1", [P, B, D])
        r["gain_ffn1"] = sb("gain_ffn1", [P, B, D])
        r["v_hi"] = sb("v_hi", [P, VCOLS], F32R)
        r["v_lo"] = sb("v_lo", [P, VCOLS], F32R)
        r["m_hi"] = sb("m_hi", [P, NH, P], F32R)
        r["m_lo"] = sb("m_lo", [P, NH, P], F32R)
        r["bp"] = sb("bp", [SD, 1])
        r["wo"] = sb("wo", [P, 2, D])
        r["gate_bias"] = sb("gate_bias", [P, 1])
        r["sel"] = sb("sel", [GLO + NH, NH, P], F32R)
        r["sel32"] = sb("sel32", [GLO + NH, 2, P], F32R)
        r["keep"] = sb("keep", [GLO + NH, S])
        r["eye8"] = sb("eye8", [NH, NH])
        r["ones8"] = sb("ones8", [NH, P])
        r["b1e"] = sb("b1e", [ER + 1, HID])
        r["b2e"] = sb("b2e", [ER + 1, D])
        r["ar1"] = sb("ar1", [P, AR])
        r["war2"] = sb("war2", [P, KH, D + AR])
        psum = [ctx.enter_context(nc.psum_tensor(f"bank{n}", [P, S], F32)) for n in range(8)]

        with ExitStack() as block0:
            def sb0(name, shape, dt=F32):
                return block0.enter_context(nc.sbuf_tensor(name, shape, dt))

            r["w_hi"] = sb0("w_hi", [P, WCOLS], F32R)
            r["w_lo"] = sb0("w_lo", [P, WCOLS], F32R)
            r["gain_attn0"] = sb0("gain_attn0", [P, B, D])
            r["bias_attn0"] = sb0("bias_attn0", [P, B, D])
            r["w_scale"] = sb0("w_scale", [P, 4, KH])
            r["wp"] = sb0("wp", [P, SD])
            r["lam"] = sb0("lam", [SD, S])
            r["cw"] = sb0("cw", [SD + 1, D])
            setup(nc, d, r, psum)
            ssm_block(nc, r, psum)
            ternary_ffn(nc, r, psum)
        linear_attention(nc, r, psum)
        lora_ffn(nc, r, psum, out)


class Signals:

    def __init__(self, nc):
        self.nc, self.held = nc, []

    def __enter__(self):
        return self

    def __call__(self, name):
        self.held.append(self.nc.alloc_semaphore(name))
        return self.held[-1]

    def __exit__(self, *error):
        if error[0] is None:
            self.nc.clear_and_free_semaphores(self.held)
            self.nc.all_engine_barrier()


def wait_apart(eng, r, signal, count):
    if not isinstance(count, int):
        count = eng.to_reg(count)
    eng.wait_ge(r["set_up"], 1)
    eng.wait_ge(signal, count)


def over(ap, axis, shape):
    return ap.unsqueeze(axis).broadcast_to(shape)


def split_mm(pe, acc, w, x, start, stop):
    pe.matmul(acc, w[0], x[0], start=start, stop=False)
    pe.matmul(acc, w[0], x[1], start=False, stop=False)
    return pe.matmul(acc, w[1], x[0], start=False, stop=stop)


def setup(nc, d, r, psum):
    with ExitStack() as ctx:
        def sb(name, shape, dt=F32):
            return ctx.enter_context(nc.sbuf_tensor(name, shape, dt))

        sem = ctx.enter_context(Signals(nc))

        cT = sb("cT", [P, 2, B])
        scT = sb("scT", [P, 2, B])
        sc_wide = sb("sc_wide", [P, 2, B, P])
        wmod = sb("wmod", [P, 2, 6, D])
        gamma = sb("gamma", [P, D])
        beta = sb("beta", [P, D])
        w3s = sb("w3s", [P, 1])
        mag_col = sb("mag_col", [P, B])
        sgn_col = sb("sgn_col", [P, B])
        gate_col = sb("gate_col", [P, B])
        b_row = sb("b_row", [P, SD])
        b_col = sb("b_col", [SD, 1])
        bp_raw = sb("bp_raw", [SD, 1])
        lam_raw = sb("lam_raw", [SD, 1])
        lam_col = sb("lam_col", [SD, 1])
        c_diag = sb("c_diag", [SD, SD])
        wo0 = sb("wo0", [SD, D])
        wqT = sb("wqT", [P, NH, D])
        wkT = sb("wkT", [P, NH, D])
        w_raw = sb("w_raw", [P, WCOLS])
        v_raw = sb("v_raw", [P, VCOLS])
        m_raw = sb("m_raw", [P, NH * P])
        sel_raw = sb("sel_raw", [GLO + NH, NH, P])
        sel32_raw = sb("sel32_raw", [GLO + NH, 2, P])
        gb_raw = sb("gb_raw", [P, 1])
        mag = sb("mag", [P, S])
        sgn = sb("sgn", [P, S])
        gate = sb("gate", [P, S])

        loaded_cond = sem("loaded_cond")
        loaded_small = sem("loaded_small")
        loaded_w = sem("loaded_w")
        loaded_qk = sem("loaded_qk")
        loaded_l1 = sem("loaded_l1")
        loaded_x = sem("loaded_x")
        zeroed = sem("zeroed")
        silu_ready = sem("silu_ready")
        wide_ready = sem("wide_ready")
        mod_mm = sem("mod_mm")
        mod_read = sem("mod_read")
        gates_mm = sem("gates_mm")
        cw_mm = sem("cw_mm")
        qk_mm = sem("qk_mm")
        qk_read = sem("qk_read")
        lam_ready = sem("lam_ready")
        mag_ready = sem("mag_ready")
        sgn_ready = sem("sgn_ready")
        gate_ready = sem("gate_ready")
        gate_used = sem("gate_used")
        col_ready = sem("col_ready")
        w_high = sem("w_high")
        v_high = sem("v_high")
        m_copied = sem("m_copied")
        m_high = sem("m_high")

        GATES = [(0, GA), (1, GA), (1, GB)]
        n_small = 0
        with nc.Block() as block:
            small = [
                (gamma[:, :], d["ln_gamma"].partition_broadcast(P)), (beta[:, :], d["ln_beta"].partition_broadcast(P)),
                (w3s[:, :], d["w3_s"]), (b_row[:, :], d["B_row"].partition_broadcast(P)),
                (b_col[:, :], d["B_col"]), (bp_raw[:, :], d["bp"]), (lam_raw[:, :], d["lam"]),
                (wo0[:, :], d["Wo0"]), (r["wp"][:, :], d["Wp"]), (r["ident"][:, :], d["ident"]),
                (r["cw"][SD:SD + 1, :], d["bo"]), (r["w_scale"][:, :, :], d["w_scale"]),
            ]
            n_small = len(small) + 2
            l1 = [
                (r["wo"][:, :, :], d["Wo1"]), (gb_raw[0:NH, :], d["bg"]), (gb_raw[GLO:GLO + NH, :], d["bg"]),
                (sel_raw[:, :, :], d["sel"]), (sel32_raw[:, :, :], d["sel32"]), (r["keep"][:, :], d["keep"]), (r["eye8"][:, :], d["eye8"]),
                (r["b1e"][:, :], d["B1e"]), (r["b2e"][:, :], d["B2e"]), (r["ar1"][:, :], d["AR1"]),
                (r["war2"][:, :, :], d["WAR2"]), (v_raw[:, VO:VO + 2 * HV], d["WvWog"]), (v_raw[:, F1:F1 + HID], d["W1"]),
                (v_raw[:, GT:GT + NH], d["Wg"]), (v_raw[:, GT + GLO:GT + GLO + NH], d["Wg"]),
            ]

            @block.sync
            def _(sp):
                sp.dma_start(cT[:, :, :], d["cT"]).then_inc(loaded_cond, 16)
                sp.dma_start(wmod[:, :, :, :], d["wmod"]).then_inc(loaded_cond, 16)
                for b in range(B):
                    sp.dma_start(r["x"][:, b, :, :], d["x"][b].rearrange("(t p) n -> p t n", p=P)).then_inc(loaded_x, 16)
                sp.dma_start(wqT[:, :, :], d["WqT"]).then_inc(loaded_qk, 16)
                sp.dma_start(wkT[:, :, :], d["WkT"]).then_inc(loaded_qk, 16)
                sp.dma_start(w_raw[:, :], d["w_all"]).then_inc(loaded_w, 16)
                sp.wait_ge(loaded_x, 16 * B)

            @block.gpsimd
            def _(pool):
                pool.memset(c_diag[:, :], 0.0).then_inc(zeroed, 1)
                pool.memset(v_raw[:, GT:GT + P], 0.0).then_inc(zeroed, 1)
                pool.memset(gb_raw[:, :], 0.0).then_inc(zeroed, 1)
                pool.memset(r["ones8"][:, :], 1.0).then_inc(zeroed, 1)
                pool.memset(r["neg_half"][:, :], -0.5).then_inc(zeroed, 1)
                pool.wait_ge(loaded_small, 16 * n_small)
                for t in range(T):
                    pool.tensor_copy(r["ident4"][:, t * P:(t + 1) * P], r["ident"][:, :])
                pool.wait_ge(w_high, 1)
                pool.tensor_tensor(r["w_lo"][:, 0:WCOLS // 2], w_raw[:, 0:WCOLS // 2], r["w_hi"][:, 0:WCOLS // 2].bitcast(F32), ALU.subtract)

            @block.scalar
            def _(act):
                for dst, src in small:
                    act.dma_start(dst, src).then_inc(loaded_small, 16)
                act.wait_ge(zeroed, 3)
                for h in range(2):
                    o = h * SD // 2
                    act.dma_start(c_diag[o:o + SD // 2, o:o + SD // 2], d["C"][h]).then_inc(loaded_small, 16)
                for dst, src in l1:
                    act.dma_start(dst, src).then_inc(loaded_l1, 16)
                act.wait_ge(loaded_cond, 32)
                act.activation(scT[:, :, :], cT[:, :, :], ACT.Silu).then_inc(silu_ready, 1)
                act.wait_ge(loaded_small, 16 * n_small)
                act.activation(lam_col[:, :], lam_raw[:, :], ACT.Sigmoid).then_inc(lam_ready, 1)
                act.wait_ge(cw_mm, 1)
                act.copy(r["cw"][0:SD, :], psum[6][0:SD, 0:D])
                act.wait_ge(loaded_l1, 16 * len(l1))
                act.mul(r["gate_bias"][:, :], gb_raw[:, :], 1.0 / GATE_NORM)
                act.mul(r["b1e"][0:ER, :], r["b1e"][0:ER, :], 1.0 / R)
                act.mul(r["b2e"][0:ER, :], r["b2e"][0:ER, :], 1.0 / R)
                for n in range(2):
                    act.wait_ge(qk_mm, n + 1)
                    act.mul(m_raw[:, n * S:(n + 1) * S], psum[n][:, :], DK ** -0.5).then_inc(m_copied, 1)

            @block.tensor
            def _(pe):
                pe.wait_ge(silu_ready, 1)
                n = 0
                for layer in range(2):
                    for j, kind in enumerate((SA, CA, SB, CB)):
                        col = (layer * 4 + j) * B
                        mm = pe.matmul(psum[7][:, col:col + B], wmod[:, layer, kind, :], scT[:, layer, :], start=True, stop=True)
                mm = pe.matmul(psum[7][:, 8 * B:9 * B], wmod[:, 0, GB, :], scT[:, 0, :], start=True, stop=True)
                mm.then_inc(mod_mm, 1)
                pe.wait_ge(loaded_small, 16 * n_small)
                pe.matmul(psum[6][0:SD, 0:D], c_diag[:, :], wo0[:, :], start=True, stop=True).then_inc(cw_mm, 1)
                pe.wait_ge(wide_ready, 2)
                for k, (layer, kind) in enumerate(GATES):
                    for half in range(2):
                        bank = 2 * k + half
                        for q in range(4):
                            mm = pe.matmul(psum[bank][:, q * P:(q + 1) * P], sc_wide[:, layer, half * 4 + q, :], wmod[:, layer, kind, :], start=True, stop=True)
                        mm.then_inc(gates_mm, 1)
                pe.wait_ge(loaded_qk, 32)
                pe.wait_ge(mag_ready, 12)
                for h in range(NH):
                    mm = pe.matmul(psum[h // 4][:, (h % 4) * P:(h % 4 + 1) * P], wqT[:, h, :], wkT[:, h, :], start=True, stop=True)
                    if h % 4 == 3:
                        mm.then_inc(qk_mm, 1)

            @block.vector
            def _(dve):
                dve.wait_ge(silu_ready, 1)
                for layer in range(2):
                    dve.tensor_copy(sc_wide[:, layer, :, :], over(scT[:, layer, :], 2, [P, B, P])).then_inc(wide_ready, 1)
                dve.wait_ge(mod_mm, 1)
                src = psum[7][:, 0:8 * B].rearrange("p (l k b) -> p l k b", l=2, k=4)
                for k in range(4):
                    dve.tensor_scalar(r["mod"][:, :, k, :], src[:, :, k, :], float(k % 2), None, ALU.add)
                dve.wait_ge(loaded_small, 16 * n_small)
                dve.tensor_tensor(r["wp"][:, :], r["wp"][:, :], b_row[:, :], ALU.mult)
                dve.tensor_tensor(r["bp"][:, :], bp_raw[:, :], b_col[:, :], ALU.mult)
                g = psum[7][:, 8 * B:9 * B]
                dve.tensor_scalar(mag_col[:, :], g, -1.0, 0.25, ALU.mult, ALU.max).then_inc(col_ready, 1)
                dve.tensor_scalar(sgn_col[:, :], g, 0.0, 2.0, ALU.is_ge, ALU.mult).then_inc(col_ready, 1)
                dve.wait_ge(col_ready, 2)
                dve.tensor_tensor(mag_col[:, :], mag_col[:, :], g, ALU.max).then_inc(col_ready, 1)
                dve.wait_ge(col_ready, 3)
                dve.scalar_tensor_tensor(out=gate_col[:, :], in0=sgn_col[:, :], scalar=-1.0, in1=mag_col[:, :], op0=ALU.add, op1=ALU.mult).then_inc(col_ready, 1)
                dve.wait_ge(col_ready, 4)
                dve.tensor_scalar(r["gain_ffn0"][:, :], gate_col[:, :], w3s[:, 0:1], None, ALU.mult)
                dve.wait_ge(lam_ready, 1)
                dve.tensor_copy(r["lam"][:, :], lam_col[:, 0:1].broadcast_to([SD, S]))
                for n in range(6):
                    k, half = n // 2, n % 2
                    dve.wait_ge(gates_mm, n + 1)
                    g = psum[n][:, :]
                    if n:
                        dve.wait_ge(gate_ready, n)
                    dve.tensor_scalar(mag[:, :], g, -1.0, 0.25, ALU.mult, ALU.max).then_inc(mag_ready, 1)
                    dve.tensor_scalar(sgn[:, :], g, 0.0, 2.0, ALU.is_ge, ALU.mult).then_inc(sgn_ready, 1)
                    dve.wait_ge(mag_ready, 2 * n + 1)
                    dve.tensor_tensor(mag[:, :], mag[:, :], g, ALU.max).then_inc(mag_ready, 1)
                    dve.wait_ge(mag_ready, 2 * n + 2)
                    dve.wait_ge(sgn_ready, n + 1)
                    if k >= 1:
                        name = ("gain_attn1", "gain_ffn1")[k - 1]
                        dst = r[name][:, 4 * half:4 * half + 4, :].rearrange("p b n -> p (b n)")
                    else:
                        if n:
                            dve.wait_ge(gate_used, n)
                        dst = gate[:, :]
                    dve.scalar_tensor_tensor(out=dst, in0=sgn[:, :], scalar=-1.0, in1=mag[:, :], op0=ALU.add, op1=ALU.mult).then_inc(gate_ready, 1)
                    if k >= 1:
                        continue
                    dve.wait_ge(gate_ready, n + 1)
                    g4 = gate[:, :].rearrange("p (b n) -> p b n", b=4)
                    here = slice(4 * half, 4 * half + 4)
                    dve.tensor_tensor(r["gain_attn0"][:, here, :], g4, over(gamma[:, :], 1, [P, 4, D]), ALU.mult)
                    dve.tensor_tensor(r["bias_attn0"][:, here, :], g4, over(beta[:, :], 1, [P, 4, D]), ALU.mult).then_inc(gate_used, 1)
                dve.wait_ge(loaded_w, 16)
                dve.tensor_copy(r["w_hi"][:, :], w_raw[:, :]).then_inc(w_high, 1)
                dve.wait_ge(w_high, 1)
                dve.tensor_tensor(r["w_lo"][:, WCOLS // 2:], w_raw[:, WCOLS // 2:], r["w_hi"][:, WCOLS // 2:].bitcast(F32), ALU.subtract)
                dve.wait_ge(loaded_l1, 16 * len(l1))
                dve.tensor_copy(r["sel"][:, :, :], sel_raw[:, :, :])
                dve.tensor_copy(r["sel32"][:, :, :], sel32_raw[:, :, :])
                dve.tensor_copy(r["v_hi"][:, :], v_raw[:, :]).then_inc(v_high, 1)
                dve.wait_ge(v_high, 1)
                dve.tensor_tensor(r["v_lo"][:, :], v_raw[:, :], r["v_hi"][:, :].bitcast(F32), ALU.subtract)
                dve.wait_ge(m_copied, 2)
                dve.tensor_copy(r["m_hi"][:, :, :].rearrange("p h n -> p (h n)"), m_raw[:, :]).then_inc(m_high, 1)
                dve.wait_ge(m_high, 1)
                dve.tensor_tensor(r["m_lo"][:, :, :].rearrange("p h n -> p (h n)"), m_raw[:, :], r["m_hi"][:, :, :].rearrange("p h n -> p (h n)").bitcast(F32), ALU.subtract).then_inc(r["set_up"], 1)


def norm_buffers(sb, sem, tag, slots):
    return [{
        "stats": sb(f"{tag}_stats{s}", [P, T, 6]), "mv": sb(f"{tag}_mv{s}", [P, T, 2]),
        "var": sb(f"{tag}_var{s}", [P, T]), "rstd": sb(f"{tag}_rstd{s}", [P, T]),
        "out": sb(f"{tag}_out{s}", [P, T, D]),
        "stats_ready": sem(f"{tag}_stats_ready{s}"), "moments_ready": sem(f"{tag}_moments_ready{s}"),
        "var_ready": sem(f"{tag}_var_ready{s}"), "rstd_ready": sem(f"{tag}_rstd_ready{s}"),
        "ready": sem(f"{tag}_ready{s}"),
    } for s in range(slots)]


def norm_moments(dve, r, n, i, tile):
    for t in range(T):
        ins = dve.bn_stats(n["stats"][:, t, :], tile(t))
    ins.then_inc(n["stats_ready"], 1)
    wait_apart(dve, r, n["stats_ready"], i + 1)
    for t in range(T):
        ins = dve.bn_aggr(n["mv"][:, t, :], n["stats"][:, t, :])
    ins.then_inc(n["moments_ready"], 1)


def norm_rstd(pool, r, n, i):
    wait_apart(pool, r, n["moments_ready"], i + 1)
    pool.tensor_scalar(n["var"][:, :], n["mv"][:, :, 1], LN_EPS, None, ALU.add).then_inc(n["var_ready"], 1)
    pool.wait_ge(n["var_ready"], i + 1)
    pool.tensor_tensor(n["rstd"][:, :], n["var"][:, :], r["neg_half"][:, :], ALU.pow).then_inc(n["rstd_ready"], 1)


def norm_apply(dve, n, i, tile):
    dve.wait_ge(n["rstd_ready"], i + 1)
    for t in range(T):
        ins = dve.tensor_scalar(n["out"][:, t, :], tile(t), n["mv"][:, t, 0:1], n["rstd"][:, t:t + 1], ALU.subtract, ALU.mult)
    ins.then_inc(n["ready"], 1)


def flip(pe, bank, src, r):
    for t in range(T):
        ins = pe.transpose(bank[:, t * P:(t + 1) * P], src(t), r["ident"][:, :])
    return ins


def modulate(act, r, dst, bank, layer, kind, b):
    return act.activation(dst, bank, ACT.Identity, scale=r["mod"][:, layer, kind + 1, bass.ds(b, 1)], bias=r["mod"][:, layer, kind, bass.ds(b, 1)])


def ssm_block(nc, r, psum):
    SLOTS = 4
    with ExitStack() as ctx:
        def sb(name, shape, dt=F32):
            return ctx.enter_context(nc.sbuf_tensor(name, shape, dt))

        sem = ctx.enter_context(Signals(nc))

        slots = range(SLOTS)
        n1 = norm_buffers(sb, sem, "ssm_in", SLOTS)
        n2 = norm_buffers(sb, sem, "ssm_out", SLOTS)
        hT = [sb(f"ssm_hT{s}", [P, S]) for s in slots]
        u = [sb(f"ssm_u{s}", [SD, S]) for s in slots]
        state = [sb(f"ssm_state{s}", [SD + 1, S]) for s in slots]
        upd = [sb(f"ssm_upd{s}", [P, T, D]) for s in slots]
        flipped = [sem(f"ssm_flipped{s}") for s in slots]
        h_ready = [sem(f"ssm_h_ready{s}") for s in slots]
        u_mm = [sem(f"ssm_u_mm{s}") for s in slots]
        u_ready = [sem(f"ssm_u_ready{s}") for s in slots]
        scanned = [sem(f"ssm_scanned{s}") for s in slots]
        z_mm = [sem(f"ssm_z_mm{s}") for s in slots]
        scaled = [sem(f"ssm_scaled{s}") for s in slots]
        upd_ready = [sem(f"ssm_upd_ready{s}") for s in slots]
        added = [sem(f"ssm_added{s}") for s in slots]
        ones_set = sem("ssm_ones_set")
        bank_a = psum[0:4]
        bank_u = psum[4:8]

        with nc.Block() as block:
            @block.vector
            def _(dve):
                for s in slots:
                    dve.memset(state[s][SD:SD + 1, :], 1.0).then_inc(ones_set, 1)
                with dve.Fori(0, B // SLOTS) as i:
                    for s in slots:
                        norm_moments(dve, r, n1[s], i, lambda t: r["x"][:, bass.ds(i * SLOTS + s, 1), t, :])
                    for s in slots:
                        norm_apply(dve, n1[s], i, lambda t: r["x"][:, bass.ds(i * SLOTS + s, 1), t, :])
                    for s in slots:
                        dve.wait_ge(u_ready[s], i + 1)
                        dve.tensor_tensor_scan(state[s][0:SD, :], r["lam"][:, :], u[s][:, :], 0.0, ALU.mult, ALU.add).then_inc(scanned[s], 1)
                    for s in slots:
                        z = bank_a[s]
                        dve.wait_ge(z_mm[s], i + 1)
                        norm_moments(dve, r, n2[s], i, lambda t: z[:, t * P:(t + 1) * P])
                    for s in slots:
                        norm_apply(dve, n2[s], i, lambda t: bank_a[s][:, t * P:(t + 1) * P])
                    for s in slots:
                        dve.wait_ge(upd_ready[s], i + 1)
                        x = r["x"][:, bass.ds(i * SLOTS + s, 1), :, :].rearrange("p b t n -> p (b t) n")
                        dve.tensor_tensor(x, x, upd[s][:, :, :], ALU.add).then_inc(added[s], 1)

            @block.gpsimd
            def _(pool):
                with pool.Fori(0, B // SLOTS) as i:
                    for s in slots:
                        norm_rstd(pool, r, n1[s], i)
                    for s in slots:
                        norm_rstd(pool, r, n2[s], i)
                    for s in slots:
                        b = bass.ds(i * SLOTS + s, 1)
                        pool.wait_ge(n2[s]["ready"], i + 1)
                        pool.wait_ge(added[s], i)
                        pool.tensor_tensor(upd[s][:, :, :], n2[s]["out"][:, :, :], r["gain_attn0"][:, b, :].broadcast_to([P, T, D]), ALU.mult).then_inc(scaled[s], 1)
                        pool.wait_ge(scaled[s], i + 1)
                        pool.tensor_tensor(upd[s][:, :, :], upd[s][:, :, :], r["bias_attn0"][:, b, :].broadcast_to([P, T, D]), ALU.add).then_inc(upd_ready[s], 1)

            @block.scalar
            def _(act):
                with act.Fori(0, B // SLOTS) as i:
                    for s in slots:
                        act.wait_ge(flipped[s], i + 1)
                        modulate(act, r, hT[s][:, :], bank_a[s][:, :], 0, 0, i * SLOTS + s).then_inc(h_ready[s], 1)
                    for s in slots:
                        act.wait_ge(u_mm[s], i + 1)
                        act.activation(u[s][:, :], bank_u[s][0:SD, :], ACT.Identity, bias=r["bp"][:, 0:1]).then_inc(u_ready[s], 1)

            @block.tensor
            def _(pe):
                pe.wait_ge(ones_set, SLOTS)
                with pe.Fori(0, B // SLOTS) as i:
                    for s in slots:
                        pe.wait_ge(n1[s]["ready"], i + 1)
                        pe.wait_ge(n2[s]["ready"], i)
                        flip(pe, bank_a[s], lambda t: n1[s]["out"][:, t, :], r).then_inc(flipped[s], 1)
                    for s in slots:
                        pe.wait_ge(h_ready[s], i + 1)
                        pe.matmul(bank_u[s][0:SD, :], r["wp"][:, :], hT[s][:, :], start=True, stop=True).then_inc(u_mm[s], 1)
                    for s in slots:
                        pe.wait_ge(scanned[s], i + 1)
                        for t in range(T):
                            c = slice(t * P, (t + 1) * P)
                            pe.matmul(bank_a[s][:, c], hT[s][:, c], r["ident"][:, :], start=True, stop=False)
                            mm = pe.matmul(bank_a[s][:, c], state[s][:, c], r["cw"][:, :], start=False, stop=True)
                        mm.then_inc(z_mm[s], 1)


def ternary_ffn(nc, r, psum):
    SLOTS = 2
    RING = 4
    with ExitStack() as ctx:
        def sb(name, shape, dt=F32):
            return ctx.enter_context(nc.sbuf_tensor(name, shape, dt))

        sem = ctx.enter_context(Signals(nc))

        slots = range(SLOTS)
        n = norm_buffers(sb, sem, "ffn", SLOTS)
        hf = [sb(f"ffn_h{s}", [P, S]) for s in slots]
        h = [[sb(f"ffn_h_{q}{s}", [P, S], F32R) for q in ("hi", "lo")] for s in slots]
        hid = [[[sb(f"ffn_g{k}_{q}{s}", [P, KH, S], F32R) for q in ("hi", "lo")] for k in range(2)] for s in slots]
        gate = [sb(f"ffn_gate{m}", [P, S]) for m in range(2)]
        full = [sb(f"ffn_full{m}", [P, S]) for m in range(4)]
        yT = hf
        flipped = [sem(f"ffn_flipped{s}") for s in slots]
        h_ready = [sem(f"ffn_h_ready{s}") for s in slots]
        h_high = [sem(f"ffn_h_high{s}") for s in slots]
        h_low = [sem(f"ffn_h_low{s}") for s in slots]
        ring_mm = sem("ffn_ring_mm")
        gate_ready = sem("ffn_gate_ready")
        product_ready = sem("ffn_product_ready")
        gelu_ready = sem("ffn_gelu_ready")
        high = sem("ffn_high")
        low = sem("ffn_low")
        y_mm = [sem(f"ffn_y_mm{s}") for s in slots]
        scaled = [sem(f"ffn_scaled{s}") for s in slots]
        y_flipped = [sem(f"ffn_y_flipped{s}") for s in slots]
        added = [sem(f"ffn_added{s}") for s in slots]
        ring = psum[0:RING]
        bank_y = psum[4:6]
        bank_t = psum[6:8]

        TILES = [(s, 0, m) for s in slots for m in range(KH)] + [(s, k, m) for k in (1, 2) for s in slots for m in range(KH)]
        N = len(TILES)
        BANKS = [(j, which) for j, (_, k, _) in enumerate(TILES) for which in ((0, 1) if k == 0 else (0,))]
        NB = len(BANKS)
        N0 = SLOTS * KH

        def made(i, j):
            return i * N + j + 1

        def layer_done(i, s, k):
            return made(i, TILES.index((s, k, KH - 1)))

        def products(i, j):
            return i * N0 + j + 1

        def gelus(i, j):
            return i * (N - N0) + j - N0 + 1

        with nc.Block() as block:
            def pair(i, last):
                return i

            @block.vector
            def _(dve):
                def tile_of(i, s):
                    return lambda t: r["x"][:, bass.ds(i * SLOTS + s, 1), t, :] if not isinstance(i, int) else r["x"][:, i * SLOTS + s, t, :]

                def body(i, more):
                    for s in slots:
                        dve.wait_ge(h_ready[s], i + 1)
                        dve.tensor_copy(h[s][0][:, :], hf[s][:, :]).then_inc(h_high[s], 1)
                    for j, (s, k, m) in enumerate(TILES):
                        f = full[j % 4]
                        if k == 0:
                            dve.wait_ge(gate_ready, products(i, j))
                            dve.wait_ge(ring_mm, i * NB + 2 * j + 2)
                            if j >= 4:
                                dve.wait_ge(low, made(i, j - 4))
                            else:
                                dve.wait_ge(low, i * N)
                            dve.scalar_tensor_tensor(out=f[:, :], in0=ring[(2 * j + 1) % RING][:, :], scalar=r["w_scale"][:, 1, m:m + 1], in1=gate[j % 2][:, :], op0=ALU.mult, op1=ALU.mult).then_inc(product_ready, 1)
                            dve.wait_ge(product_ready, products(i, j))
                            dve.wait_ge(y_mm[s], i)
                        else:
                            dve.wait_ge(gelu_ready, gelus(i, j))
                        dve.tensor_copy(hid[s][k % 2][0][:, m, :], f[:, :]).then_inc(high, 1)
                        if j == N - 1 - KH:
                            pass
                        if more and j == N - 5:
                            for q in slots:
                                norm_moments(dve, r, n[q], i + 1, tile_of(i + 1, q))
                        if more and j == N - 3:
                            for q in slots:
                                norm_apply(dve, n[q], i + 1, tile_of(i + 1, q))
                    for s in slots:
                        dve.wait_ge(y_flipped[s], i + 1)
                        x = r["x"][:, bass.ds(i * SLOTS + s, 1), :, :].rearrange("p b t n -> p (b t n)")
                        dve.tensor_tensor(x, x, bank_y[s][:, :], ALU.add).then_inc(added[s], 1)

                for q in slots:
                    norm_moments(dve, r, n[q], 0, tile_of(0, q))
                for q in slots:
                    norm_apply(dve, n[q], 0, tile_of(0, q))
                with dve.Fori(0, B // SLOTS - 1) as i:
                    body(i, True)
                body(B // SLOTS - 1, False)

            @block.gpsimd
            def _(pool):
                def body(i, more):
                    for s in slots:
                        pool.wait_ge(h_high[s], i + 1)
                        pool.tensor_tensor(h[s][1][:, :], hf[s][:, :], h[s][0][:, :].bitcast(F32), ALU.subtract).then_inc(h_low[s], 1)
                    for j, (s, k, m) in enumerate(TILES):
                        pool.wait_ge(high, made(i, j))
                        pool.tensor_tensor(hid[s][k % 2][1][:, m, :], full[j % 4][:, :], hid[s][k % 2][0][:, m, :].bitcast(F32), ALU.subtract).then_inc(low, 1)
                        if more and j == N - 5:
                            for q in slots:
                                norm_rstd(pool, r, n[q], i + 1)
                for q in slots:
                    norm_rstd(pool, r, n[q], 0)
                with pool.Fori(0, B // SLOTS - 1) as i:
                    body(i, True)
                body(B // SLOTS - 1, False)

            @block.scalar
            def _(act):
                with act.Fori(0, B // SLOTS) as i:
                    for s in slots:
                        act.wait_ge(flipped[s], i + 1)
                        act.wait_ge(h_low[s], i)
                        modulate(act, r, hf[s][:, :], bank_t[s][:, :], 0, 2, i * SLOTS + s).then_inc(h_ready[s], 1)
                    for j, (s, k, m) in enumerate(TILES):
                        if k == 0:
                            act.wait_ge(ring_mm, i * NB + 2 * j + 1)
                            if j >= 2:
                                act.wait_ge(product_ready, products(i, j - 2))
                            else:
                                act.wait_ge(product_ready, i * N0)
                            act.activation(gate[j % 2][:, :], ring[(2 * j) % RING][:, :], ACT.Silu, scale=r["w_scale"][:, 0, m:m + 1]).then_inc(gate_ready, 1)
                        else:
                            act.wait_ge(ring_mm, i * NB + N0 + j + 1)
                            act.wait_ge(low, made(i, j - 4))
                            act.activation(full[j % 4][:, :], ring[(N0 + j) % RING][:, :], ACT.Gelu, scale=r["w_scale"][:, 1 + k, m:m + 1]).then_inc(gelu_ready, 1)
                    for s in slots:
                        act.wait_ge(y_mm[s], i + 1)
                        act.wait_ge(y_flipped[s], i)
                        act.activation(yT[s][:, :], bank_y[s][:, :], ACT.Copy, scale=r["gain_ffn0"][:, bass.ds(i * SLOTS + s, 1)]).then_inc(scaled[s], 1)

            @block.tensor
            def _(pe):
                def w(col, k, width):
                    at = col + k * width
                    return r["w_hi"][:, at:at + P], r["w_lo"][:, at:at + P]

                with pe.Fori(0, B // SLOTS) as i:
                    for s in slots:
                        pe.wait_ge(n[s]["ready"], i + 1)
                        pe.wait_ge(h_ready[s], i)
                        flip(pe, bank_t[s], lambda t: n[s]["out"][:, t, :], r).then_inc(flipped[s], 1)
                    for g, (j, which) in enumerate(BANKS):
                        s, k, m = TILES[j]
                        acc = ring[g % RING]
                        if g >= RING:
                            pj, pw = BANKS[g - RING]
                            if TILES[pj][1] == 0:
                                pe.wait_ge(product_ready if pw else gate_ready, products(i, pj))
                            else:
                                pe.wait_ge(gelu_ready, gelus(i, pj))
                        else:
                            pe.wait_ge(gelu_ready, i * (N - N0))
                        if k == 0:
                            if m == 0 and which == 0:
                                pe.wait_ge(h_low[s], i + 1)
                            col = (W1, W2)[which] + m * P
                            mm = split_mm(pe, acc[:, :], w(col, 0, 0), [h[s][q][:, :] for q in range(2)], True, True)
                        else:
                            if m == 0:
                                pe.wait_ge(low, layer_done(i, s, k - 1))
                            x = hid[s][(k - 1) % 2]
                            for kk in range(KH):
                                mm = split_mm(pe, acc[:, :], w((H1, H2)[k - 1] + m * P, kk, HID), [x[q][:, kk, :] for q in range(2)], kk == 0, kk == KH - 1)
                        mm.then_inc(ring_mm, 1)
                    for s in slots:
                        pe.wait_ge(low, layer_done(i, s, 2))
                        pe.wait_ge(added[s], i)
                        for kk in range(KH):
                            mm = split_mm(pe, bank_y[s][:, :], w(W3, kk, D), [hid[s][0][q][:, kk, :] for q in range(2)], kk == 0, kk == KH - 1)
                        mm.then_inc(y_mm[s], 1)
                    for s in slots:
                        pe.wait_ge(scaled[s], i + 1)
                        flip(pe, bank_y[s], lambda t: yT[s][:, t * P:(t + 1) * P], r).then_inc(y_flipped[s], 1)


def linear_attention(nc, r, psum):
    SLOTS = 2
    PAIRS = B // SLOTS
    RING = 4
    with ExitStack() as ctx:
        def sb(name, shape, dt=F32):
            return ctx.enter_context(nc.sbuf_tensor(name, shape, dt))

        sem = ctx.enter_context(Signals(nc))

        slots = range(SLOTS)
        n = norm_buffers(sb, sem, "att", SLOTS)
        hT = [sb(f"att_hT{s}", [P, S]) for s in slots]
        h = [[sb(f"att_h_{q}{s}", [P, S], F32R) for q in ("hi", "lo")] for s in slots]
        htok = [sb(f"att_htok{s}", [P, T, D]) for s in slots]
        qT = [sb(f"att_qT{s}", [P, NH, S]) for s in slots]
        v = [sb(f"att_v{s}", [P, T, HV]) for s in slots]
        og = [sb(f"att_og{s}", [P, 2, S]) for s in slots]
        GR = GLO + NH
        alpha = [sb(f"att_alpha{s}", [GR, S]) for s in slots]
        cut = [sb(f"att_cut{s}", [GR, S]) for s in slots]
        start = [sb(f"att_start{s}", [GR, S]) for s in slots]
        cut_in = [sb(f"att_cut_in{s}", [GR, S], F32R) for s in slots]
        cum = [sb(f"att_cum{s}", [GR, S]) for s in slots]
        cum_in = [sb(f"att_cum_in{s}", [GR, S], F32R) for s in slots]
        ends = [sb(f"att_ends{s}", [NH, T, NH]) for s in slots]
        total = [sb(f"att_total{s}", [P, T, NH]) for s in slots]
        wide = [sb(f"att_wide{s}", [P, 2, S]) for s in slots]
        decay = [sb(f"att_decay{m}", [P, S]) for m in range(2)]
        prob = [sb(f"att_prob{m}", [P, S]) for m in range(2)]
        vw = [sb(f"att_vw{s}", [P, T, HV]) for s in slots]
        state = [sb(f"att_state{s}", [P, T, HV]) for s in slots]
        grown = sb("att_grown", [P, HV])
        inner = [sb(f"att_inner{s}", [P, 2, S]) for s in slots]
        outer = [sb(f"att_outer{s}", [P, 2, S]) for s in slots]
        upd = [sb(f"att_upd{s}", [P, T, D]) for s in slots]

        def sems(name):
            return [sem(f"att_{name}{s}") for s in slots]

        ring_mm = sem("att_ring_mm")
        h_ready, h_high, h_low = sems("h_ready"), sems("h_high"), sems("h_low")
        q_ready, v_ready, og_ready, htok_ready = sems("q_ready"), sems("v_ready"), sems("og_ready"), sems("htok_ready")
        alpha_ready, cut_ready, cut_high, cut_low = sems("alpha_ready"), sems("cut_ready"), sems("cut_high"), sems("cut_low")
        start_ready, cum_ready, cum_high, cum_low = sems("start_ready"), sems("cum_ready"), sems("cum_high"), sems("cum_low")
        ends_ready, total_ready, wide_ready = sems("ends_ready"), sems("total_ready"), sems("wide_ready")
        decay_ready, prob_ready, vw_ready = sem("att_decay_ready"), sem("att_prob_ready"), sem("att_vw_ready")
        intra_mm, inter_mm, state_ready, grown_ready = sems("intra_mm"), sems("inter_mm"), sems("state_ready"), sem("att_grown_ready")
        inner_ready, outer_ready, summed, gated = sems("inner_ready"), sems("outer_ready"), sems("summed"), sems("gated")
        scaled, added = sems("scaled"), sems("added")
        ring = psum[0:RING]
        bank_o = psum[4:6]
        bank_s = psum[6:8]

        def project_uses(s, a):
            return ([(s, a, "alpha", 0)] + [(s, a, "q", k) for k in range(NH)],
                    [(s, a, "v", 0), (s, a, "v", 1), (s, a, "og", 0), (s, a, "og", 1), (s, a, "htok", 0),
                     (s, a, "total", 0), (s, a, "wide", 0), (s, a, "wide", 1)])

        FLIP1, FLIP0 = 5, 6

        def pair_uses(more):
            uses = []
            for s, at in ((0, FLIP1), (1, FLIP0)):
                for k in range(NH):
                    uses += [(s, 0, "decay", k), (s, 0, "score", k)]
                    if k == at and s == 0:
                        uses.append((1, 0, "flip", 0))
                    if k == at and s == 1 and more:
                        uses.append((0, 1, "flip", 0))
                if s == 0:
                    a, b = project_uses(1, 0)
                    uses += a + b + [(0, 0, "state", c) for c in range(3)]
            uses += [(0, 0, "y", 0)] + [(1, 0, "state", c) for c in range(3)]
            if more:
                a, b = project_uses(0, 1)
                return uses + a + [(1, 0, "y", 0)] + b
            return uses + [(1, 0, "y", 0)]

        a, b = project_uses(0, 0)
        FIRST = [(0, 0, "flip", 0)] + a + b
        OFFSET = -len(FIRST) % RING
        USES = {more: pair_uses(more) for more in (True, False)}
        assert len(USES[True]) % RING == 0 and USES[True][-RING:] == [(s, 1, w, k) for s, _, w, k in FIRST[-RING:]]

        class Ring:

            def __init__(self, i, more):
                self.i, self.uses = i, FIRST if i is None else USES[more]
                self.base = 0 if i is None else len(FIRST) + i * len(USES[True])
                self.skew = OFFSET if i is None else 0

            def full(self, *use):
                return self.base + self.uses.index(use) + 1

            def bank(self, *use):
                return ring[(self.skew + self.uses.index(use)) % RING]

            def pair(self, ahead):
                return ahead if self.i is None else self.i + ahead

            def claim(self, pe, *use):
                at = self.uses.index(use) - RING
                if at >= 0:
                    s, ahead, what, k = self.uses[at]
                    i = self.pair(ahead)
                elif self.i is not None:
                    s, _, what, k = FIRST[at]
                    i = self.i
                else:
                    return self.bank(*use)
                signal, count = {
                    "flip": (h_ready[s], i + 1), "alpha": (alpha_ready[s], i + 1), "q": (q_ready[s], i * NH + k + 1),
                    "v": (v_ready[s], i * 2 + k + 1), "og": (og_ready[s], i * 2 + k + 1), "htok": (htok_ready[s], i + 1),
                    "total": (total_ready[s], i + 1), "wide": (wide_ready[s], i * 2 + k + 1),
                    "decay": (decay_ready, nth(i, s, NH, k)), "score": (prob_ready, nth(i, s, NH, k)),
                    "state": (state_ready[s], i * 3 + k + 1), "y": (scaled[s], i + 1),
                }[what]
                pe.wait_ge(signal, count)
                return self.bank(*use)

        def nth(i, s, per, k):
            return i * SLOTS * per + s * per + k + 1

        with nc.Block() as block:
            def x_tile(i, s):
                return lambda t: r["x"][:, bass.ds(i * SLOTS + s, 1), t, :]

            def by_head(ap):
                return ap.rearrange("p (h n) -> p h n", h=NH)

            @block.vector
            def _(dve):
                def split(i, s):
                    dve.wait_ge(h_ready[s], i + 1)
                    dve.tensor_copy(h[s][0][:, :], hT[s][:, :]).then_inc(h_high[s], 1)

                def decays(i, s):
                    dve.wait_ge(alpha_ready[s], i + 1)
                    dve.tensor_tensor(cut[s][:, :], alpha[s][:, :], r["keep"][:, :], ALU.mult).then_inc(cut_ready[s], 1)
                    dve.wait_ge(cut_ready[s], i + 1)
                    dve.tensor_tensor(start[s][:, :], alpha[s][:, :], cut[s][:, :], ALU.subtract).then_inc(start_ready[s], 1)
                    dve.wait_ge(start_ready[s], i + 1)
                    dve.tensor_tensor_scan(cum[s][:, :], cut[s][:, :], start[s][:, :], 0.0, ALU.mult, ALU.add).then_inc(cum_ready[s], 1)
                    dve.wait_ge(cum_ready[s], i + 1)
                    last = cum[s][0:NH, :].rearrange("p (c n) -> p c n", c=T)[:, :, P - 1:P]
                    dve.tensor_tensor(ends[s][:, :, :], last.broadcast_to([NH, T, NH]), over(r["eye8"][:, :], 1, [NH, T, NH]), ALU.mult).then_inc(ends_ready[s], 1)

                def values(g, i, a, s):
                    for k in range(2):
                        dve.wait_ge(ring_mm, g.full(s, a, "v", k))
                        dve.tensor_copy(v[s][:, 2 * k:2 * k + 2, :].rearrange("p c n -> p (c n)"), g.bank(s, a, "v", k)[:, :]).then_inc(v_ready[s], 1)
                    dve.wait_ge(ring_mm, g.full(s, a, "total", 0))
                    dve.tensor_copy(total[s][:, :, :].rearrange("p c n -> p (c n)"), g.bank(s, a, "total", 0)[:, 0:T * NH]).then_inc(total_ready[s], 1)

                def head(g, i, s, k):
                    m = k % 2
                    dve.wait_ge(ring_mm, g.full(s, 0, "decay", k))
                    if s or k >= 2:
                        dve.wait_ge(vw_ready, nth(i, s, NH, k - 2))
                    dve.tensor_tensor_scan(decay[m][:, :], g.bank(s, 0, "decay", k)[:, :], r["ident4"][:, :], 0.0, ALU.mult, ALU.add).then_inc(decay_ready, 1)
                    dve.wait_ge(decay_ready, nth(i, s, NH, k))
                    dve.wait_ge(ring_mm, g.full(s, 0, "score", k))
                    if k >= 2:
                        dve.wait_ge(intra_mm[s], i * NH + k - 1)
                    elif s:
                        dve.wait_ge(intra_mm[0], i * NH + NH - 1 + k)
                    dve.tensor_tensor(prob[m][:, :], g.bank(s, 0, "score", k)[:, :], decay[m][:, :], ALU.mult).then_inc(prob_ready, 1)

                def states(g, i, s):
                    for c in range(3):
                        new = state[s][:, c + 1, :]
                        ps = g.bank(s, 0, "state", c)[:, 0:HV]
                        dve.wait_ge(ring_mm, g.full(s, 0, "state", c))
                        if c == 0:
                            dve.tensor_copy(new, ps).then_inc(state_ready[s], 1)
                            continue
                        dve.wait_ge(state_ready[s], i * 3 + c)
                        dve.tensor_tensor(by_head(grown[:, :]), by_head(state[s][:, c, :]), over(total[s][:, c, :], 2, [P, NH, DV]), ALU.mult).then_inc(grown_ready, 1)
                        dve.wait_ge(grown_ready, nth(i, s, 2, c - 1))
                        dve.tensor_tensor(new, grown[:, :], ps, ALU.add).then_inc(state_ready[s], 1)

                def across(i, s):
                    dve.wait_ge(inter_mm[s], i + 1)
                    dve.wait_ge(wide_ready[s], (i + 1) * 2)
                    for q in range(2):
                        ins = dve.tensor_tensor(outer[s][:, q, P:S], bank_s[q][:, P:S], wide[s][:, q, P:S], ALU.mult)
                    ins.then_inc(outer_ready[s], 1)

                def scale(g, i, s):
                    dve.wait_ge(ring_mm, g.full(s, 0, "y", 0))
                    gain = r["gain_attn1"][:, bass.ds(i * SLOTS + s, 1), :].broadcast_to([P, T, D])
                    dve.tensor_tensor(upd[s][:, :, :], g.bank(s, 0, "y", 0)[:, :].rearrange("p (t n) -> p t n", t=T), gain, ALU.mult).then_inc(scaled[s], 1)

                def body(i, more):
                    g = Ring(i, more)
                    for k in range(NH):
                        head(g, i, 0, k)
                        if k == FLIP1 + 1:
                            split(i, 1)
                    decays(i, 1)
                    values(g, i, 0, 1)
                    states(g, i, 0)
                    if more:
                        norm_moments(dve, r, n[0], i + 1, x_tile(i + 1, 0))
                    for k in range(NH):
                        head(g, i, 1, k)
                        if k == 2:
                            across(i, 0)
                            if more:
                                norm_apply(dve, n[0], i + 1, x_tile(i + 1, 0))
                        if k == FLIP0 + 1 and more:
                            split(i + 1, 0)
                    scale(g, i, 0)
                    states(g, i, 1)
                    if more:
                        decays(i + 1, 0)
                    across(i, 1)
                    if more:
                        norm_moments(dve, r, n[1], i + 1, x_tile(i + 1, 1))
                    scale(g, i, 1)
                    if more:
                        values(g, i + 1, 1, 0)
                        norm_apply(dve, n[1], i + 1, x_tile(i + 1, 1))

                for s in slots:
                    norm_moments(dve, r, n[s], 0, x_tile(0, s))
                for s in slots:
                    norm_apply(dve, n[s], 0, x_tile(0, s))
                split(0, 0)
                decays(0, 0)
                values(Ring(None, True), 0, 0, 0)
                with dve.Fori(0, PAIRS - 1) as i:
                    body(i, True)
                body(PAIRS - 1, False)

            @block.gpsimd
            def _(pool):
                def low_h(i, s):
                    pool.wait_ge(h_high[s], i + 1)
                    pool.tensor_tensor(h[s][1][:, :], hT[s][:, :], h[s][0][:, :].bitcast(F32), ALU.subtract).then_inc(h_low[s], 1)

                def low_decays(i, s, before, count):
                    lo = slice(GLO, GR)
                    pool.wait_ge(before, count)
                    pool.wait_ge(cut_high[s], i + 1)
                    pool.tensor_tensor(cut_in[s][lo, :], cut[s][lo, :], cut_in[s][lo, :].bitcast(F32), ALU.subtract).then_inc(cut_low[s], 1)
                    pool.wait_ge(cum_high[s], i + 1)
                    pool.tensor_tensor(cum_in[s][lo, :], cum[s][lo, :], cum_in[s][lo, :].bitcast(F32), ALU.subtract).then_inc(cum_low[s], 1)
                    pool.wait_ge(cum_low[s], i + 1)

                def decay_v(i, s, k):
                    if k == 0:
                        pool.wait_ge(v_ready[s], (i + 1) * 2)
                    pool.wait_ge(decay_ready, nth(i, s, NH, k))
                    hs = slice(k * DV, (k + 1) * DV)
                    last = decay[k % 2][:, :].rearrange("p (c n) -> p c n", c=T)[:, :, P - 1:P]
                    pool.tensor_tensor(vw[s][:, :, hs], v[s][:, :, hs], last.broadcast_to([P, T, DV]), ALU.mult).then_inc(vw_ready, 1)

                def gate(i, s):
                    pool.wait_ge(inner_ready[s], (i + 1) * 2)
                    pool.wait_ge(outer_ready[s], i + 1)
                    pool.tensor_tensor(outer[s][:, :, P:S], outer[s][:, :, P:S], inner[s][:, :, P:S], ALU.add).then_inc(summed[s], 1)
                    pool.tensor_tensor(outer[s][:, :, 0:P], inner[s][:, :, 0:P], og[s][:, :, 0:P], ALU.mult)
                    pool.wait_ge(summed[s], i + 1)
                    pool.tensor_tensor(outer[s][:, :, P:S], outer[s][:, :, P:S], og[s][:, :, P:S], ALU.mult).then_inc(gated[s], 1)

                def add(i, s):
                    pool.wait_ge(scaled[s], i + 1)
                    x = r["x"][:, bass.ds(i * SLOTS + s, 1), :, :].rearrange("p b t n -> p (b t) n")
                    pool.tensor_tensor(x, x, upd[s][:, :, :], ALU.add).then_inc(added[s], 1)

                def body(i, more):
                    for k in range(NH):
                        decay_v(i, 0, k)
                        if k == FLIP1 + 1:
                            low_h(i, 1)
                    low_decays(i, 1, vw_ready, nth(i, 0, NH, NH - 1))
                    if more:
                        norm_rstd(pool, r, n[0], i + 1)
                    for k in range(NH):
                        decay_v(i, 1, k)
                        if k == 3:
                            gate(i, 0)
                    if more:
                        low_h(i + 1, 0)
                    add(i, 0)
                    if more:
                        low_decays(i + 1, 0, added[0], i + 1)
                    gate(i, 1)
                    if more:
                        norm_rstd(pool, r, n[1], i + 1)
                    add(i, 1)

                for s in slots:
                    norm_rstd(pool, r, n[s], 0)
                low_h(0, 0)
                low_decays(0, 0, h_low[0], 1)
                with pool.Fori(0, PAIRS - 1) as i:
                    body(i, True)
                body(PAIRS - 1, False)

            @block.scalar
            def _(act):
                def bring_h(g, i, a, s):
                    act.wait_ge(ring_mm, g.full(s, a, "flip", 0))
                    modulate(act, r, hT[s][:, :], g.bank(s, a, "flip", 0)[:, :], 1, 0, i * SLOTS + s).then_inc(h_ready[s], 1)

                def queries(g, s, a, ks):
                    for k in ks:
                        act.wait_ge(ring_mm, g.full(s, a, "q", k))
                        act.copy(qT[s][:, k, :], g.bank(s, a, "q", k)[:, :]).then_inc(q_ready[s], 1)

                def project(g, i, a, s):
                    act.wait_ge(ring_mm, g.full(s, a, "alpha", 0))
                    act.activation(alpha[s][:, :], g.bank(s, a, "alpha", 0)[0:GR, :], ACT.Sigmoid, scale=1.0 / GATE_NORM, bias=r["gate_bias"][0:GR, 0:1]).then_inc(alpha_ready[s], 1)
                    queries(g, s, a, range(0, 2))
                    act.wait_ge(cut_ready[s], i + 1)
                    act.copy(cut_in[s][:, :], cut[s][:, :]).then_inc(cut_high[s], 1)
                    queries(g, s, a, range(2, 5))
                    act.wait_ge(cum_ready[s], i + 1)
                    act.copy(cum_in[s][:, :], cum[s][:, :]).then_inc(cum_high[s], 1)
                    queries(g, s, a, range(5, NH))
                    for q in range(2):
                        act.wait_ge(ring_mm, g.full(s, a, "og", q))
                        act.activation(og[s][:, q, :], g.bank(s, a, "og", q)[:, :], ACT.Sigmoid).then_inc(og_ready[s], 1)
                    act.wait_ge(ring_mm, g.full(s, a, "htok", 0))
                    act.copy(htok[s][:, :, :].rearrange("p t n -> p (t n)"), g.bank(s, a, "htok", 0)[:, :]).then_inc(htok_ready[s], 1)
                    for q in range(2):
                        act.wait_ge(ring_mm, g.full(s, a, "wide", q))
                        act.copy(wide[s][:, q, :], g.bank(s, a, "wide", q)[:, :]).then_inc(wide_ready[s], 1)

                def keep_inner(i, s):
                    act.wait_ge(intra_mm[s], (i + 1) * NH)
                    for q in range(2):
                        act.copy(inner[s][:, q, :], bank_o[q][:, :]).then_inc(inner_ready[s], 1)

                def body(i, more):
                    g = Ring(i, more)
                    bring_h(g, i, 0, 1)
                    project(g, i, 0, 1)
                    keep_inner(i, 0)
                    if more:
                        bring_h(g, i + 1, 1, 0)
                    keep_inner(i, 1)
                    if more:
                        project(g, i + 1, 1, 0)

                first = Ring(None, True)
                bring_h(first, 0, 0, 0)
                project(first, 0, 0, 0)
                with act.Fori(0, PAIRS - 1) as i:
                    body(i, True)
                body(PAIRS - 1, False)

            @block.tensor
            def _(pe):
                def flip_in(g, i, a, s):
                    pe.wait_ge(n[s]["ready"], i + 1)
                    b = g.claim(pe, s, a, "flip", 0)
                    flip(pe, b, lambda t: n[s]["out"][:, t, :], r).then_inc(ring_mm, 1)

                def project(g, i, a, s, between=None):
                    hh = [h[s][q][:, :] for q in range(2)]
                    pe.wait_ge(h_low[s], i + 1)
                    b = g.claim(pe, s, a, "alpha", 0)
                    split_mm(pe, b[:, :], (r["v_hi"][:, GT:GT + P], r["v_lo"][:, GT:GT + P]), hh, True, True).then_inc(ring_mm, 1)
                    for k in range(NH):
                        b = g.claim(pe, s, a, "q", k)
                        split_mm(pe, b[:, :], (r["m_hi"][:, k, :], r["m_lo"][:, k, :]), hh, True, True).then_inc(ring_mm, 1)
                    if between:
                        between()
                    for k in range(2):
                        b = g.claim(pe, s, a, "v", k)
                        for t in (2 * k, 2 * k + 1):
                            c = slice(t * P, (t + 1) * P)
                            o = (t % 2) * HV
                            mm = split_mm(pe, b[:, o:o + HV], [x[:, c] for x in hh], (r["v_hi"][:, VO:VO + HV], r["v_lo"][:, VO:VO + HV]), True, True)
                        mm.then_inc(ring_mm, 1)
                    for q in range(2):
                        b = g.claim(pe, s, a, "og", q)
                        at = slice(VO + HV + q * P, VO + HV + (q + 1) * P)
                        split_mm(pe, b[:, :], (r["v_hi"][:, at], r["v_lo"][:, at]), hh, True, True).then_inc(ring_mm, 1)
                    b = g.claim(pe, s, a, "htok", 0)
                    flip(pe, b, lambda t: hT[s][:, t * P:(t + 1) * P], r).then_inc(ring_mm, 1)
                    pe.wait_ge(ends_ready[s], i + 1)
                    b = g.claim(pe, s, a, "total", 0)
                    pe.matmul(b[:, 0:T * NH], r["ones8"][:, :], ends[s][:, :, :].rearrange("p c n -> p (c n)"), start=True, stop=True).then_inc(ring_mm, 1)
                    pe.wait_ge(cum_low[s], i + 1)
                    for q in range(2):
                        b = g.claim(pe, s, a, "wide", q)
                        pe.matmul(b[:, :], r["sel32"][:, q, :], cum_in[s][:, :], start=True, stop=True).then_inc(ring_mm, 1)

                def inside(i, s, k):
                    pe.wait_ge(prob_ready, nth(i, s, NH, k))
                    rows = slice((k % 4) * DV, (k % 4 + 1) * DV)
                    for c in range(T):
                        cc = slice(c * P, (c + 1) * P)
                        mm = pe.matmul(bank_o[k // 4][rows, cc], v[s][:, c, k * DV:(k + 1) * DV], prob[k % 2][:, cc], start=True, stop=True)
                    mm.then_inc(intra_mm[s], 1)

                def heads(g, i, s, at, then):
                    pe.wait_ge(cut_low[s], i + 1)
                    pe.wait_ge(v_ready[s], (i + 1) * 2)
                    pe.wait_ge(q_ready[s], (i + 1) * NH)
                    for k in range(NH):
                        b = g.claim(pe, s, 0, "decay", k)
                        pe.matmul(b[:, :], r["sel"][:, k, :], cut_in[s][:, :], start=True, stop=True).then_inc(ring_mm, 1)
                        b = g.claim(pe, s, 0, "score", k)
                        for c in range(T):
                            cc = slice(c * P, (c + 1) * P)
                            mm = pe.matmul(b[:, cc], hT[s][:, cc], qT[s][:, k, cc], start=True, stop=True)
                        mm.then_inc(ring_mm, 1)
                        if k == at and then:
                            then()
                        if k == 1 and s == 1:
                            pe.wait_ge(inner_ready[0], (i + 1) * 2)
                        if k >= 1:
                            inside(i, s, k - 1)

                def cross(g, i, s):
                    pe.wait_ge(vw_ready, nth(i, s, NH, NH - 1))
                    pe.wait_ge(htok_ready[s], i + 1)
                    for c in range(3):
                        b = g.claim(pe, s, 0, "state", c)
                        pe.matmul(b[:, 0:HV], htok[s][:, c, :], vw[s][:, c, :], start=True, stop=True).then_inc(ring_mm, 1)
                    for c in range(1, T):
                        pe.wait_ge(state_ready[s], i * 3 + c)
                        cc = slice(c * P, (c + 1) * P)
                        for k in range(NH):
                            rows = slice((k % 4) * DV, (k % 4 + 1) * DV)
                            mm = pe.matmul(bank_s[k // 4][rows, cc], state[s][:, c, k * DV:(k + 1) * DV], qT[s][:, k, cc], start=True, stop=True)
                    mm.then_inc(inter_mm[s], 1)

                def output(g, i, s):
                    pe.wait_ge(gated[s], i + 1)
                    b = g.claim(pe, s, 0, "y", 0)
                    for t in range(T):
                        c = slice(t * P, (t + 1) * P)
                        for q in range(2):
                            mm = pe.matmul(b[:, c], outer[s][:, q, c], r["wo"][:, q, :], start=(q == 0), stop=(q == 1))
                    mm.then_inc(ring_mm, 1)

                def body(i, more):
                    g = Ring(i, more)
                    heads(g, i, 0, FLIP1, lambda: flip_in(g, i, 0, 1))
                    inside(i, 0, NH - 1)
                    project(g, i, 0, 1)
                    cross(g, i, 0)
                    heads(g, i, 1, FLIP0, (lambda: flip_in(g, i + 1, 1, 0)) if more else None)
                    inside(i, 1, NH - 1)
                    output(g, i, 0)
                    cross(g, i, 1)
                    if more:
                        project(g, i + 1, 1, 0, lambda: output(g, i, 1))
                    else:
                        output(g, i, 1)

                first = Ring(None, True)
                flip_in(first, 0, 0, 0)
                project(first, 0, 0, 0)
                with pe.Fori(0, PAIRS - 1) as i:
                    body(i, True)
                body(PAIRS - 1, False)


def lora_ffn(nc, r, psum, out):
    SLOTS = 2
    with ExitStack() as ctx:
        def sb(name, shape, dt=F32):
            return ctx.enter_context(nc.sbuf_tensor(name, shape, dt))

        sem = ctx.enter_context(Signals(nc))

        slots = range(SLOTS)
        n = norm_buffers(sb, sem, "lora", SLOTS)
        hT = [sb(f"lora_hT{s}", [P, S]) for s in slots]
        h = [[sb(f"lora_h_{q}{s}", [P, S], F32R) for q in ("hi", "lo")] for s in slots]
        hid = [sb(f"lora_hid{s}", [P, KH, S]) for s in slots]
        def pairs(name, shape):
            return [[sb(f"lora_{name}{k}{s}", shape) for s in slots] for k in range(2)]

        top, shifted, expo = pairs("top", [P, T]), pairs("shifted", [P, T, E]), pairs("expo", [P, T, E])
        den, inv, prob = pairs("den", [P, T]), pairs("inv", [P, T]), pairs("prob", [P, T, E])
        zg, zT = pairs("zg", [P, T, ER]), pairs("zT", [ER + 1, S])
        upd = [sb(f"lora_upd{s}", [P, T, D]) for s in slots]
        res = [sb(f"lora_res{s}", [P, T, D]) for s in slots]

        def sems(name):
            return [sem(f"lora_{name}{s}") for s in slots]

        def sems2(name):
            return [sems(f"{name}_{k}_") for k in range(2)]

        ones_set = sem("lora_ones_set")
        flipped, h_ready, h_high, h_low = sems("flipped"), sems("h_ready"), sems("h_high"), sems("h_low")
        down_mm, top_ready, shift_ready, expo_ready = sems2("down_mm"), sems2("top_ready"), sems2("shift_ready"), sems2("expo_ready")
        den_ready, inv_ready, prob_ready, zg_ready = sems2("den_ready"), sems2("inv_ready"), sems2("prob_ready"), sems2("zg_ready")
        zT_mm, zT_ready = sems2("zT_mm"), sems2("zT_ready")
        hid_mm, hid_ready = sem("lora_hid_mm"), sem("lora_hid_ready")
        y_mm, scaled, res_ready, stored = sems("y_mm"), sems("scaled"), sems("res_ready"), sems("stored")
        bank_t = psum[0:2]
        ring = psum[2:4]
        bank_e = [psum[4:6], psum[6:8]]
        WIDE = 256

        def down(k, s, t0, t1):
            if k == 0:
                return bank_t[s][:, 0:T * 32].rearrange("p (t n) -> p t n", t=T)[:, t0:t1, 0:AR]
            return bank_e[s][t0 // 2][:, :].rearrange("p (t n) -> p t n", t=2)[:, 0:t1 - t0, D:D + AR]

        SPANS = [[(0, T)], [(0, 2), (2, T)]]

        with nc.Block() as block:
            @block.vector
            def _(dve):
                def x_tile(i, s):
                    return lambda t: r["x"][:, bass.ds(i * SLOTS + s, 1), t, :]

                def route(i, s, k):
                    dve.wait_ge(down_mm[k][s], i + 1)
                    for a, b in SPANS[k]:
                        ins = dve.tensor_reduce(top[k][s][:, a:b], down(k, s, a, b)[:, :, ER:AR], AX_X, ALU.max)
                    ins.then_inc(top_ready[k][s], 1)
                    dve.wait_ge(top_ready[k][s], i + 1)
                    for a, b in SPANS[k]:
                        ins = dve.tensor_tensor(shifted[k][s][:, a:b, :], down(k, s, a, b)[:, :, ER:AR], over(top[k][s][:, a:b], 2, [P, b - a, E]), ALU.subtract)
                    ins.then_inc(shift_ready[k][s], 1)
                    dve.wait_ge(expo_ready[k][s], i + 1)
                    dve.tensor_reduce(den[k][s][:, :], expo[k][s][:, :, :], AX_X, ALU.add).then_inc(den_ready[k][s], 1)
                    dve.wait_ge(den_ready[k][s], i + 1)
                    dve.reciprocal(inv[k][s][:, :], den[k][s][:, :]).then_inc(inv_ready[k][s], 1)
                    dve.wait_ge(inv_ready[k][s], i + 1)
                    dve.tensor_tensor(prob[k][s][:, :, :], expo[k][s][:, :, :], over(inv[k][s][:, :], 2, [P, T, E]), ALU.mult).then_inc(prob_ready[k][s], 1)
                    dve.wait_ge(prob_ready[k][s], i + 1)
                    for a, b in SPANS[k]:
                        for t in range(a, b):
                            z = down(k, s, a, b)[:, t - a, 0:ER].rearrange("p (e n) -> p e n", e=E)
                            ins = dve.tensor_tensor(zg[k][s][:, t, :].rearrange("p (e n) -> p e n", e=E), z, over(prob[k][s][:, t, :], 2, [P, E, R]), ALU.mult)
                    ins.then_inc(zg_ready[k][s], 1)

                def body(i, more):
                    for s in slots:
                        dve.wait_ge(h_ready[s], i + 1)
                        dve.tensor_copy(h[s][0][:, :], hT[s][:, :]).then_inc(h_high[s], 1)
                    for s in slots:
                        route(i, s, 0)
                    if more:
                        for s in slots:
                            norm_moments(dve, r, n[s], i + 1, x_tile(i + 1, s))
                        for s in slots:
                            norm_apply(dve, n[s], i + 1, x_tile(i + 1, s))
                    for s in slots:
                        route(i, s, 1)
                    for s in slots:
                        dve.wait_ge(y_mm[s], i + 1)
                        dve.wait_ge(res_ready[s], i)
                        g = r["gain_ffn1"][:, bass.ds(i * SLOTS + s, 1), :].broadcast_to([P, 2, D])
                        for q in range(2):
                            y = bank_e[s][q][:, :].rearrange("p (t n) -> p t n", t=2)[:, :, 0:D]
                            ins = dve.tensor_tensor(upd[s][:, 2 * q:2 * q + 2, :], y, g, ALU.mult)
                        ins.then_inc(scaled[s], 1)

                for k in range(2):
                    for s in slots:
                        dve.memset(zT[k][s][:, :], 1.0).then_inc(ones_set, 1)
                for s in slots:
                    norm_moments(dve, r, n[s], 0, x_tile(0, s))
                for s in slots:
                    norm_apply(dve, n[s], 0, x_tile(0, s))
                with dve.Fori(0, B // SLOTS - 1) as i:
                    body(i, True)
                body(B // SLOTS - 1, False)

            @block.gpsimd
            def _(pool):
                def body(i, more):
                    for s in slots:
                        pool.wait_ge(h_high[s], i + 1)
                        pool.tensor_tensor(h[s][1][:, :], hT[s][:, :], h[s][0][:, :].bitcast(F32), ALU.subtract).then_inc(h_low[s], 1)
                    if more:
                        for s in slots:
                            norm_rstd(pool, r, n[s], i + 1)
                    for s in slots:
                        pool.wait_ge(scaled[s], i + 1)
                        pool.wait_ge(stored[s], i * 16)
                        x = r["x"][:, bass.ds(i * SLOTS + s, 1), :, :].rearrange("p b t n -> p (b t) n")
                        pool.tensor_tensor(res[s][:, :, :], x, upd[s][:, :, :], ALU.add).then_inc(res_ready[s], 1)

                for s in slots:
                    norm_rstd(pool, r, n[s], 0)
                with pool.Fori(0, B // SLOTS - 1) as i:
                    body(i, True)
                body(B // SLOTS - 1, False)

            @block.sync
            def _(sp):
                with sp.Fori(0, B // SLOTS) as i:
                    for s in slots:
                        sp.wait_ge(res_ready[s], i + 1)
                        dst = out[bass.ds(i * SLOTS + s, 1), :, :].rearrange("b (t p) n -> p (b t) n", p=P)
                        sp.dma_start(dst, res[s][:, :, :]).then_inc(stored[s], 16)
                for s in slots:
                    sp.wait_ge(stored[s], 16 * (B // SLOTS))

            @block.scalar
            def _(act):
                act.wait_ge(ones_set, 4)
                with act.Fori(0, B // SLOTS) as i:
                    for s in slots:
                        act.wait_ge(flipped[s], i + 1)
                        act.wait_ge(h_low[s], i)
                        modulate(act, r, hT[s][:, :], bank_t[s][:, :], 1, 2, i * SLOTS + s).then_inc(h_ready[s], 1)
                    for s in slots:
                        act.wait_ge(shift_ready[0][s], i + 1)
                        act.activation(expo[0][s][:, :, :], shifted[0][s][:, :, :], ACT.Exp).then_inc(expo_ready[0][s], 1)
                    for s in slots:
                        act.wait_ge(zT_mm[0][s], i + 1)
                        act.copy(zT[0][s][0:ER, :], bank_t[s][0:ER, :]).then_inc(zT_ready[0][s], 1)
                    for s in slots:
                        for m in range(KH):
                            g = s * KH + m
                            act.wait_ge(hid_mm, i * SLOTS * KH + g + 1)
                            act.wait_ge(down_mm[1][s], i)
                            act.activation(hid[s][:, m, :], ring[g % 2][:, :], ACT.Relu).then_inc(hid_ready, 1)
                    for s in slots:
                        act.wait_ge(shift_ready[1][s], i + 1)
                        act.activation(expo[1][s][:, :, :], shifted[1][s][:, :, :], ACT.Exp).then_inc(expo_ready[1][s], 1)
                    for s in slots:
                        act.wait_ge(zT_mm[1][s], i + 1)
                        act.copy(zT[1][s][0:ER, :], bank_t[s][0:ER, :]).then_inc(zT_ready[1][s], 1)

            @block.tensor
            def _(pe):
                def flip_z(i, s, k):
                    pe.wait_ge(zg_ready[k][s], i + 1)
                    for t in range(T):
                        mm = pe.transpose(bank_t[s][0:ER, t * P:(t + 1) * P], zg[k][s][:, t, :], r["ident"][:, :])
                    mm.then_inc(zT_mm[k][s], 1)

                with pe.Fori(0, B // SLOTS) as i:
                    for s in slots:
                        pe.wait_ge(n[s]["ready"], i + 1)
                        pe.wait_ge(zT_ready[1][s], i)
                        flip(pe, bank_t[s], lambda t: n[s]["out"][:, t, :], r).then_inc(flipped[s], 1)
                    for s in slots:
                        pe.wait_ge(h_ready[s], i + 1)
                        for t in range(T):
                            mm = pe.matmul(bank_t[s][:, t * 32:t * 32 + AR], hT[s][:, t * P:(t + 1) * P], r["ar1"][:, :], start=True, stop=True)
                        mm.then_inc(down_mm[0][s], 1)
                    for s in slots:
                        flip_z(i, s, 0)
                    for s in slots:
                        pe.wait_ge(h_low[s], i + 1)
                        for m in range(KH):
                            g = s * KH + m
                            pe.wait_ge(hid_ready, i * SLOTS * KH + max(g - 1, 0))
                            c = slice(m * P, (m + 1) * P)
                            b = ring[g % 2]
                            at = slice(F1 + m * P, F1 + (m + 1) * P)
                            split_mm(pe, b[:, :], (r["v_hi"][:, at], r["v_lo"][:, at]), [h[s][q][:, :] for q in range(2)], True, False)
                            if m == 0:
                                pe.wait_ge(zT_ready[0][s], i + 1)
                            pe.matmul(b[:, :], r["b1e"][:, c], zT[0][s][:, :], start=False, stop=True).then_inc(hid_mm, 1)
                    for s in slots:
                        pe.wait_ge(hid_ready, i * SLOTS * KH + (s + 1) * KH)
                        pe.wait_ge(scaled[s], i)
                        for t in range(T):
                            b = bank_e[s][t // 2]
                            at = (t % 2) * WIDE
                            for k in range(KH):
                                mm = pe.matmul(b[:, at:at + D + AR], hid[s][:, k, t * P:(t + 1) * P], r["war2"][:, k, :], start=(k == 0 and t % 2 == 0), stop=(k == KH - 1), skip_group_check=True)
                        mm.then_inc(down_mm[1][s], 1)
                    for s in slots:
                        flip_z(i, s, 1)
                    for s in slots:
                        pe.wait_ge(zT_ready[1][s], i + 1)
                        for t in range(T):
                            at = (t % 2) * WIDE
                            mm = pe.matmul(bank_e[s][t // 2][:, at:at + D], zT[1][s][:, t * P:(t + 1) * P], r["b2e"][:, :], start=False, stop=True, skip_group_check=True)
                        mm.then_inc(y_mm[s], 1)


def kernel(**inputs):
    import numpy as np
    import concourse.bacc as bacc
    from concourse import mybir as _mybir
    from concourse.bass_utils import run_bass_kernel_spmd

    a = {k: np.asarray(v) for k, v in inputs.items()}

    def col(x, n=None):
        return x.reshape(-1, 1)

    def tiles(wT, k):
        return wT.reshape(k, P, -1).transpose(1, 0, 2).reshape(P, -1)

    keep = np.ones((GLO + NH, S), np.float32)
    keep[:, ::P] = 0
    sel = np.zeros((GLO + NH, NH, P), np.float32)
    for h in range(NH):
        sel[h, h] = sel[GLO + h, h] = 1
    sel32 = np.zeros((GLO + NH, 2, P), np.float32)
    for h in range(NH):
        rows = slice((h % 4) * DV, (h % 4 + 1) * DV)
        sel32[h, h // 4, rows] = sel32[GLO + h, h // 4, rows] = 1
    A1 = a["L1_ffn_A1"].transpose(1, 0, 2).reshape(D, ER)
    A2 = a["L1_ffn_A2"].transpose(1, 0, 2).reshape(HID, ER)
    arrays = {
        "x": a["L0_attn_x"],
        "cT": np.stack([a["L0_c"].T, a["L1_c"].T], 1),
        "wmod": np.stack([a["L0_wmod"].reshape(D, 6, D), a["L1_wmod"].reshape(D, 6, D)], 1),
        "ln_gamma": a["L0_attn_ln_gamma"], "ln_beta": a["L0_attn_ln_beta"],
        "B_row": a["L0_attn_B_param"].reshape(-1), "B_col": col(a["L0_attn_B_param"]),
        "bp": col(a["L0_attn_bp"]), "lam": col(a["L0_attn_log_neg_lambdas"]),
        "Wp": a["L0_attn_Wp"], "Wo0": a["L0_attn_Wo"], "bo": a["L0_attn_bo"].reshape(1, D), "C": a["L0_attn_C_param"],
        "w3_s": col(a["L0_ffn_w3_s"]),
        "w_scale": np.stack([a[f"L0_ffn_{k}_s"].reshape(KH, P).T for k in ("w1", "w2", "h1", "h2")], 1),
        "w_all": np.concatenate([
            a["L0_ffn_w1_w"].T, a["L0_ffn_w2_w"].T, tiles(a["L0_ffn_h1_w"].T, KH),
            tiles(a["L0_ffn_h2_w"].T, KH), tiles(a["L0_ffn_w3_w"].T, KH)], 1),
        "WqT": a["L1_attn_Wq"].reshape(D, NH, DK).transpose(2, 1, 0),
        "WkT": a["L1_attn_Wk"].reshape(D, NH, DK).transpose(2, 1, 0),
        "WvWog": np.concatenate([a["L1_attn_Wv"], a["L1_attn_Wog"]], 1),
        "Wg": a["L1_attn_Wg"], "bg": col(a["L1_attn_bg"]),
        "Wo1": a["L1_attn_Wo"].reshape(2, P, D).transpose(1, 0, 2),
        "W1": a["L1_ffn_W1"],
        "B1e": np.concatenate([a["L1_ffn_B1"].reshape(ER, HID), a["L1_ffn_b1"].reshape(1, HID)], 0),
        "B2e": np.concatenate([a["L1_ffn_B2"].reshape(ER, D), a["L1_ffn_b2"].reshape(1, D)], 0),
        "AR1": np.concatenate([A1, a["L1_ffn_R1"]], 1),
        "WAR2": np.concatenate([a["L1_ffn_W2"], A2, a["L1_ffn_R2"]], 1).reshape(KH, P, D + AR).transpose(1, 0, 2),
        "ident": np.eye(P, dtype=np.float32), "eye8": np.eye(NH, dtype=np.float32), "keep": keep, "sel": sel,
        "sel32": sel32,
    }
    nc = bacc.Bacc("TRN2", target_bir_lowering=False, num_devices=1)
    given, d = {}, {}
    for name, x in arrays.items():
        x = np.ascontiguousarray(x)
        given[f"in_{name}"] = x
        d[name] = nc.dram_tensor(f"in_{name}", x.shape, _mybir.dt.from_np(x.dtype), kind="ExternalInput").ap()
    out = nc.dram_tensor("out", (B, S, D), _mybir.dt.float32, kind="ExternalOutput").ap()
    build(nc, d, out)
    result = run_bass_kernel_spmd(nc, [given], core_ids=[0])
    return result.results[0]["out"]
```

```python
from contextlib import ExitStack

import concourse.bass as bass
from concourse import mybir

F32 = mybir.dt.float32
F32R = mybir.dt.float32r
I32 = mybir.dt.int32
ACT = mybir.ActivationFunctionType
ALU = mybir.AluOpType
AX_X = mybir.AxisListType.X

P = 128
B = 8
S = 512
T = S // P
D = 128
SD = 32
NH = 8
DV = 32
HV = NH * DV
HID = 512
KH = HID // P
E = 3
R = 8
ER = E * R
AR = ER + E
DK = 128
LN_EPS = 1e-5
GATE_NORM = 16.0
GLO = 32
W1, W2, H1, H2, W3 = 0, 512, 1024, 3072, 5120
WCOLS = 5632
VO, F1, GT = 0, 512, 1024
VCOLS = 1024 + 128
C_IDENT = 0
C_WP = C_IDENT + P
C_SCALE = C_WP + SD
C_GAMMA = C_SCALE + 4 * KH
C_BETA, C_W3S, COLS = C_GAMMA + 1, C_GAMMA + 2, C_GAMMA + 3
R_B, R_BP, R_LAM, R_C = 0, 1, 2, 3
R_WO = R_C + SD
ROWS = R_WO + D
L_WO = 0
L_AR1 = L_WO + 2 * D
L_WAR2 = L_AR1 + AR
L_BG = L_WAR2 + KH * (D + AR)
L1COLS = L_BG + 1
SA, CA, GA, SB, CB, GB = range(6)


def build(nc, d, out):
    with ExitStack() as ctx:
        def sb(name, shape, dt=F32):
            return ctx.enter_context(nc.sbuf_tensor(name, shape, dt))

        r = {"set_up": ctx.enter_context(nc.semaphore("set_up"))}
        r["x"] = sb("x", [P, B, T, D])
        r["cols"] = sb("cols", [P, COLS])
        r["ident"] = r["cols"][:, C_IDENT:C_IDENT + P]
        r["ident4"] = sb("ident4", [P, S])
        r["neg_half"] = sb("neg_half", [P, T])
        r["mod"] = sb("mod", [P, 2, 4, B])
        r["gain_ffn0"] = sb("gain_ffn0", [P, B])
        r["gain_attn1"] = sb("gain_attn1", [P, B, D])
        r["gain_ffn1"] = sb("gain_ffn1", [P, B, D])
        r["v_hi"] = sb("v_hi", [P, VCOLS], F32R)
        r["v_lo"] = sb("v_lo", [P, VCOLS], F32R)
        r["m_hi"] = sb("m_hi", [P, NH, P], F32R)
        r["m_lo"] = sb("m_lo", [P, NH, P], F32R)
        r["l1"] = sb("l1", [P, L1COLS])
        r["wo"] = r["l1"][:, L_WO:L_WO + 2 * D].rearrange("p (q n) -> p q n", q=2)
        r["ar1"] = r["l1"][:, L_AR1:L_AR1 + AR]
        r["war2"] = r["l1"][:, L_WAR2:L_BG].rearrange("p (k n) -> p k n", k=KH)
        r["gate_bias"] = sb("gate_bias", [P, 1])
        r["sel"] = sb("sel", [GLO + NH, NH, P], F32R)
        r["sel32"] = sb("sel32", [GLO + NH, 2, P], F32R)
        r["keep"] = sb("keep", [GLO + NH, S])
        r["eye8"] = sb("eye8", [NH, NH])
        r["ones8"] = sb("ones8", [NH, P])
        r["b1s"] = sb("b1s", [3 * GLO, HID], F32R)
        r["b2s"] = sb("b2s", [3 * GLO, D], F32R)
        psum = [ctx.enter_context(nc.psum_tensor(f"bank{n}", [P, S], F32)) for n in range(8)]

        with ExitStack() as block0:
            def sb0(name, shape, dt=F32):
                return block0.enter_context(nc.sbuf_tensor(name, shape, dt))

            r["w_hi"] = sb0("w_hi", [P, WCOLS], F32R)
            r["w_lo"] = sb0("w_lo", [P, WCOLS], F32R)
            r["w_inexact"] = sb0("w_inexact", [1, 1], I32)
            r["gain_attn0"] = sb0("gain_attn0", [P, B, D])
            r["bias_attn0"] = sb0("bias_attn0", [P, B, D])
            r["w_scale"] = r["cols"][:, C_SCALE:C_SCALE + 4 * KH].rearrange("p (k m) -> p k m", k=4)
            r["wp"] = r["cols"][:, C_WP:C_WP + SD]
            r["lam"] = sb0("lam", [SD, S])
            r["cw"] = sb0("cw", [SD + 1, D])
            setup_and_ssm(nc, d, r, psum)
            ternary_ffn(nc, r, psum)
        linear_attention(nc, r, psum)
        lora_ffn(nc, r, psum, out)


class Signals:

    def __init__(self, nc):
        self.nc, self.held = nc, []

    def __enter__(self):
        return self

    def __call__(self, name):
        self.held.append(self.nc.alloc_semaphore(name))
        return self.held[-1]

    def __exit__(self, *error):
        if error[0] is None:
            self.nc.clear_and_free_semaphores(self.held)
            self.nc.all_engine_barrier()


def wait_apart(eng, r, signal, count):
    if not isinstance(count, int):
        count = eng.to_reg(count)
    eng.wait_ge(r["set_up"], 1)
    eng.wait_ge(signal, count)


def over(ap, axis, shape):
    return ap.unsqueeze(axis).broadcast_to(shape)


def split_mm(pe, acc, w, x, start, stop):
    pe.matmul(acc, w[0], x[0], start=start, stop=False)
    pe.matmul(acc, w[0], x[1], start=False, stop=False)
    return pe.matmul(acc, w[1], x[0], start=False, stop=stop)


def before(b):
    s, j = b
    return (0, j) if s else (1, j - 1)


def after(b):
    s, j = b
    return (0, j + 1) if s else (1, j)


def steps(eng, first, step):
    first()
    step((0, 0), False, True, True)
    with eng.Fori(0, B // 2 - 2) as i:
        step((1, i), True, True, True)
        step((0, i + 1), True, True, True)
    step((1, B // 2 - 2), True, True, True)
    step((0, B // 2 - 1), True, True, False)
    step((1, B // 2 - 1), True, False, False)


def is_sequence(b, wanted):
    return isinstance(b[1], int) and b == wanted


def norm_buffers(sb, sem, tag, slots):
    return [{
        "stats": sb(f"{tag}_stats{s}", [P, T, 6]), "mv": sb(f"{tag}_mv{s}", [P, T, 2]),
        "var": sb(f"{tag}_var{s}", [P, T]), "rstd": sb(f"{tag}_rstd{s}", [P, T]),
        "out": sb(f"{tag}_out{s}", [P, T, D]),
        "stats_ready": sem(f"{tag}_stats_ready{s}"), "moments_ready": sem(f"{tag}_moments_ready{s}"),
        "var_ready": sem(f"{tag}_var_ready{s}"), "rstd_ready": sem(f"{tag}_rstd_ready{s}"),
        "ready": sem(f"{tag}_ready{s}"),
    } for s in range(slots)]


def norm_moments(dve, r, n, i, tile):
    for t in range(T):
        ins = dve.bn_stats(n["stats"][:, t, :], tile(t))
    ins.then_inc(n["stats_ready"], 1)
    wait_apart(dve, r, n["stats_ready"], i + 1)
    for t in range(T):
        ins = dve.bn_aggr(n["mv"][:, t, :], n["stats"][:, t, :])
    ins.then_inc(n["moments_ready"], 1)


def norm_rstd(pool, r, n, i):
    wait_apart(pool, r, n["moments_ready"], i + 1)
    pool.tensor_scalar(n["var"][:, :], n["mv"][:, :, 1], LN_EPS, None, ALU.add).then_inc(n["var_ready"], 1)
    pool.wait_ge(n["var_ready"], i + 1)
    pool.tensor_tensor(n["rstd"][:, :], n["var"][:, :], r["neg_half"][:, :], ALU.pow).then_inc(n["rstd_ready"], 1)


def norm_apply(dve, n, i, tile):
    dve.wait_ge(n["rstd_ready"], i + 1)
    for t in range(T):
        ins = dve.tensor_scalar(n["out"][:, t, :], tile(t), n["mv"][:, t, 0:1], n["rstd"][:, t:t + 1], ALU.subtract, ALU.mult)
    ins.then_inc(n["ready"], 1)


def flip(pe, bank, src, r):
    for t in range(T):
        ins = pe.transpose(bank[:, t * P:(t + 1) * P], src(t), r["ident"][:, :])
    return ins


def modulate(act, r, dst, bank, layer, kind, b):
    return act.activation(dst, bank, ACT.Identity, scale=r["mod"][:, layer, kind + 1, bass.ds(b, 1)], bias=r["mod"][:, layer, kind, bass.ds(b, 1)])


def setup_and_ssm(nc, d, r, psum):
    with ExitStack() as ctx:
        def sb(name, shape, dt=F32):
            return ctx.enter_context(nc.sbuf_tensor(name, shape, dt))

        sem = ctx.enter_context(Signals(nc))
        slots = range(2)

        def pair(name, shape, dt=F32):
            return [sb(f"{name}{s}", shape, dt) for s in slots]

        def sems(name):
            return [sem(f"{name}{s}") for s in slots]

        cT = sb("cT", [P, 2, B])
        scT = sb("scT", [P, 2, B])
        wmod = sb("wmod", [P, 2, 6, D])
        gate_mag, gate_sgn, gate_col = sb("gate_mag", [P, 4 * B]), sb("gate_sgn", [P, 4 * B]), sb("gate_col", [P, 4 * B])
        spread_col = sb("spread_col", [P, 4, B])
        diag = pair("diag", [P, S])
        ones = sb("ones", [P, P])
        rows = sb("rows", [SD, ROWS])
        b_bias = sb("b_bias", [SD, 1])
        lam_col = sb("lam_col", [SD, 1])
        wqT = sb("wqT", [P, NH, D])
        wkT = sb("wkT", [P, NH, D])
        w_raw = sb("w_raw", [P, WCOLS])
        w_lo_sum = sb("w_lo_sum", [P, B])
        w_total = sb("w_total", [P, 1])
        w_mark = sb("w_mark", [P, 1])
        v_raw = sb("v_raw", [P, VCOLS])
        m_raw = sb("m_raw", [P, NH * P])
        sel_raw = sb("sel_raw", [GLO + NH, NH + 2, P])
        b12 = sb("b12", [3 * GLO, HID + D + 1])
        b12_scaled = sb("b12_scaled", [3 * GLO, HID + D])
        n1 = norm_buffers(sb, sem, "ssm_in", 2)
        n2 = norm_buffers(sb, sem, "ssm_out", 2)
        neg_mean, shift = pair("ssm_neg_mean", [P, T]), pair("ssm_shift", [P, T])
        hT = pair("ssm_hT", [P, S])
        u = pair("ssm_u", [SD, S])
        state = pair("ssm_state", [SD + 1, S])
        centred = pair("ssm_centred", [P, T, D])

        loaded_cond, loaded_cols, loaded_rows = sem("loaded_cond"), sem("loaded_cols"), sem("loaded_rows")
        loaded_x = [sem(f"loaded_x{b}") for b in range(B // 2)]
        loaded_w, loaded_qk, loaded_l1 = sem("loaded_w"), sem("loaded_qk"), sem("loaded_l1")
        ones_set, state_set, silu_ready = sem("ones_set"), sem("state_set"), sem("silu_ready")
        mod_mm, mod_ready, gate_step, col_ready = sem("mod_mm"), sem("mod_ready"), sem("gate_step"), sem("col_ready")
        diag_ready, spread_mm, spread_ready = sem("diag_ready"), sem("spread_mm"), sem("spread_ready")
        cw_mm, cw_ready, lam_ready, lam_spread, bias_ready = sem("cw_mm"), sem("cw_ready"), sem("lam_ready"), sem("lam_spread"), sem("bias_ready")
        w_high, w_low = sem("w_high"), sem("w_low")
        w_summed, w_totalled, w_marked, w_counted = sem("w_summed"), sem("w_totalled"), sem("w_marked"), sem("w_counted")
        v_high, b_scaled, b_high, qk_mm, m_copied, m_high = sem("v_high"), sem("b_scaled"), sem("b_high"), sem("qk_mm"), sem("m_copied"), sem("m_high")
        neg_ready, shift_ready, biased = sems("ssm_neg_ready"), sems("ssm_shift_ready"), sems("ssm_biased")
        flipped, h_ready, u_mm, u_ready = sems("ssm_flipped"), sems("ssm_h_ready"), sems("ssm_u_mm"), sems("ssm_u_ready")
        scanned, z_mm, centred_ready = sems("ssm_scanned"), sems("ssm_z_mm"), sems("ssm_centred_ready")
        bank_t, bank_u, bank_z, bank_w = psum[0:2], psum[2:4], psum[4:6], psum[6:8]
        bank_m = bank_z
        bank_c = bank_u[1]
        SOON = [(0, SA), (0, CA), (0, GA)]
        LATER = [(0, SB), (0, CB), (1, SA), (1, CA), (1, SB), (1, CB), (1, GA), (1, GB), (0, GB)]

        PIECE = WCOLS // B
        SPREAD = ("gain_attn0", "bias_attn0", "gain_attn1", "gain_ffn1")
        SPREADS = [(v, half) for v in range(4) for half in range(2)]

        def piece(b):
            return bass.ds((b[1] * 2 + b[0]) * PIECE, PIECE)

        def x_of(b):
            return bass.ds(b[1] * 2 + b[0], 1)

        def load_x(eng, j):
            src = d["x"][2 * j:2 * j + 2].rearrange("b (t p) n -> p b t n", p=P)
            eng.dma_start(r["x"][:, 2 * j:2 * j + 2, :, :], src).then_inc(loaded_x[j], 16)

        third_last, second_last, last = (1, B // 2 - 2), (0, B // 2 - 1), (1, B // 2 - 1)

        with nc.Block() as block:
            @block.sync
            def _(sp):
                sp.dma_start(cT[:, :, :], d["cT"]).then_inc(loaded_cond, 16)
                sp.dma_start(wmod[:, :, :, :], d["wmod"]).then_inc(loaded_cond, 16)
                for j in range(1, B // 2):
                    load_x(sp, j)
                sp.dma_start(w_raw[:, :], d["w_all"]).then_inc(loaded_w, 16)
                sp.dma_start(wqT[:, :, :], d["WqT"]).then_inc(loaded_qk, 16)
                sp.dma_start(wkT[:, :, :], d["WkT"]).then_inc(loaded_qk, 16)
                l1 = [(v_raw[:, :], d["v_all"]), (b12[:, :], d["B12"]), (sel_raw[:, :, :], d["sel"]),
                      (r["keep"][:, :], d["keep"]), (r["eye8"][:, :], d["eye8"]), (r["l1"][:, :], d["l1"])]
                for dst, src in l1:
                    sp.dma_start(dst, src).then_inc(loaded_l1, 16)

            @block.vector
            def _(dve):
                def moments1(b):
                    norm_moments(dve, r, n1[b[0]], b[1], lambda t: r["x"][:, x_of(b), t, :])

                def scan(b):
                    s, j = b
                    dve.wait_ge(u_ready[s], j + 1)
                    dve.tensor_tensor_scan(state[s][0:SD, :], r["lam"][:, :], u[s][:, :], 0.0, ALU.mult, ALU.add).then_inc(scanned[s], 1)

                def moments2(b):
                    s, j = b
                    dve.wait_ge(z_mm[s], j + 1)
                    norm_moments(dve, r, n2[s], j, lambda t: bank_z[s][:, t * P:(t + 1) * P])

                def result(b):
                    s, j = b
                    gain = r["gain_attn0"][:, x_of(b), :].rearrange("p b n -> p (b n)")
                    dve.wait_ge(n2[s]["moments_ready"], j + 1)
                    for t in range(T):
                        ins = dve.scalar_tensor_tensor(out=centred[s][:, t, :], in0=bank_z[s][:, t * P:(t + 1) * P], scalar=n2[s]["mv"][:, t, 0:1], in1=gain, op0=ALU.subtract, op1=ALU.mult)
                    ins.then_inc(centred_ready[s], 1)
                    dve.wait_ge(n2[s]["rstd_ready"], j + 1)
                    dve.wait_ge(biased[s], j + 1)
                    dve.wait_ge(centred_ready[s], j + 1)
                    for t in range(T):
                        x = r["x"][:, x_of(b), t, :].rearrange("p b n -> p (b n)")
                        dve.scalar_tensor_tensor(out=x, in0=centred[s][:, t, :], scalar=n2[s]["rstd"][:, t:t + 1], in1=x, op0=ALU.mult, op1=ALU.add)

                def make_diag(k):
                    v, half = SPREADS[k]
                    if k >= 2:
                        dve.wait_ge(spread_mm, k - 1)
                    col = spread_col[:, v, 4 * half:4 * half + 4]
                    dst = diag[k % 2][:, :].rearrange("p (b n) -> p b n", b=4)
                    dve.tensor_tensor(dst, over(r["ident"][:, :], 1, [P, 4, P]), over(col, 2, [P, 4, P]), ALU.mult).then_inc(diag_ready, 1)

                def modulations(k0, k1, bank):
                    src = bank[:, 0:(k1 - k0) * B].rearrange("p (k b) -> p k b", b=B)
                    dst = r["mod"][:, :, :, :].rearrange("p l k b -> p (l k) b")
                    for one in range(2):
                        dve.tensor_scalar(dst[:, k0 + one:k1:2, :], src[:, one:k1 - k0:2, :], float(one), None, ALU.add).then_inc(mod_ready, 1)

                def gates(k0, k1, bank, at):
                    g = bank[:, at * B:(at + k1 - k0) * B]
                    here = slice(k0 * B, k1 * B)
                    done = 4 * (k0 > 0)
                    dve.tensor_scalar(gate_mag[:, here], g, -1.0, 0.25, ALU.mult, ALU.max).then_inc(gate_step, 1)
                    dve.tensor_scalar(gate_sgn[:, here], g, 0.0, 2.0, ALU.is_ge, ALU.mult).then_inc(gate_step, 1)
                    dve.wait_ge(gate_step, done + 2)
                    dve.tensor_tensor(gate_mag[:, here], gate_mag[:, here], g, ALU.max).then_inc(gate_step, 1)
                    dve.wait_ge(gate_step, done + 3)
                    dve.scalar_tensor_tensor(out=gate_col[:, here], in0=gate_sgn[:, here], scalar=-1.0, in1=gate_mag[:, here], op0=ALU.add, op1=ALU.mult).then_inc(gate_step, 1)
                    dve.wait_ge(gate_step, done + 4)

                def first():
                    for s in slots:
                        dve.memset(state[s][SD:SD + 1, :], 1.0).then_inc(state_set, 1)
                    dve.wait_ge(loaded_x[0], 16)
                    moments1((0, 0))
                    moments1((1, 0))
                    dve.wait_ge(mod_mm, 1)
                    modulations(0, 2, bank_m[0])
                    gates(0, 1, bank_m[0], 2)
                    ga0 = gate_col[:, 0:B]
                    dve.wait_ge(loaded_cols, 16)
                    dve.tensor_scalar(spread_col[:, 0, :], ga0, r["cols"][:, C_GAMMA:C_GAMMA + 1], None, ALU.mult)
                    dve.tensor_scalar(spread_col[:, 1, :], ga0, r["cols"][:, C_BETA:C_BETA + 1], None, ALU.mult).then_inc(col_ready, 1)
                    dve.wait_ge(loaded_rows, 32)
                    dve.tensor_tensor(b_bias[:, :], rows[:, R_BP:R_BP + 1], rows[:, R_B:R_B + 1], ALU.mult).then_inc(bias_ready, 1)
                    dve.wait_ge(col_ready, 1)
                    for k in range(4):
                        make_diag(k)
                    dve.wait_ge(lam_ready, 1)
                    dve.tensor_copy(r["lam"][:, :], lam_col[:, 0:1].broadcast_to([SD, S])).then_inc(lam_spread, 1)
                    dve.wait_ge(mod_mm, 2)
                    modulations(2, 8, bank_m[1])
                    gates(1, 4, bank_m[1], 6)
                    dve.tensor_copy(spread_col[:, 2:4, :], gate_col[:, B:3 * B].rearrange("p (v b) -> p v b", v=2)).then_inc(col_ready, 1)
                    dve.tensor_scalar(r["gain_ffn0"][:, :], gate_col[:, 3 * B:4 * B], r["cols"][:, C_W3S:C_W3S + 1], None, ALU.mult)
                    dve.wait_ge(col_ready, 2)
                    for k in (4, 5):
                        make_diag(k)
                    dve.wait_ge(lam_spread, 1)
                    dve.wait_ge(spread_ready, 4)
                    for j in range(1, B // 2):
                        dve.wait_ge(loaded_x[j], 16)

                def step(b, has_before, has_after, has_second):
                    scan(b)
                    if has_second:
                        moments1(after(after(b)))
                    if has_before:
                        result(before(b))
                    if is_sequence(b, third_last):
                        for k in (6, 7):
                            make_diag(k)
                    moments2(b)

                steps(dve, first, step)
                lo = slice(2 * GLO, 3 * GLO)
                result(last)
                dve.wait_ge(w_summed, B)
                dve.tensor_reduce(w_total[:, :], w_lo_sum[:, :], AX_X, ALU.add).then_inc(w_totalled, 1)
                dve.wait_ge(w_totalled, 1)
                dve.tensor_scalar(w_mark[:, :], w_total[:, :], 0.0, None, ALU.not_equal).then_inc(w_marked, 1)
                dve.wait_ge(b_high, 2)
                dve.tensor_tensor(r["b1s"][lo, :], b12_scaled[lo, 0:HID], r["b1s"][lo, :].bitcast(F32), ALU.subtract)
                dve.tensor_tensor(r["b2s"][lo, :], b12_scaled[lo, HID:HID + D], r["b2s"][lo, :].bitcast(F32), ALU.subtract)
                dve.wait_ge(w_counted, 1)
                dve.tensor_scalar(r["w_inexact"][:, :], bank_w[0][0:1, 0:1], 0.0, None, ALU.is_gt)

            @block.gpsimd
            def _(pool):
                def rstd1(b):
                    s, j = b
                    norm_rstd(pool, r, n1[s], j)
                    pool.tensor_scalar(neg_mean[s][:, :], n1[s]["mv"][:, :, 0], -1.0, None, ALU.mult).then_inc(neg_ready[s], 1)
                    pool.wait_ge(n1[s]["rstd_ready"], j + 1)
                    pool.wait_ge(neg_ready[s], j + 1)
                    pool.tensor_tensor(shift[s][:, :], neg_mean[s][:, :], n1[s]["rstd"][:, :], ALU.mult).then_inc(shift_ready[s], 1)

                def add_bias(b):
                    s, j = b
                    pool.wait_ge(n1[s]["ready"], j + 1)
                    x = r["x"][:, x_of(b), :, :].rearrange("p b t n -> p (b t) n")
                    pool.tensor_tensor(x, x, r["bias_attn0"][:, x_of(b), :].broadcast_to([P, T, D]), ALU.add).then_inc(biased[s], 1)

                def low_piece(b):
                    pool.wait_ge(w_high, b[1] * 2 + b[0] + 1)
                    pool.tensor_tensor(r["w_lo"][:, piece(b)], w_raw[:, piece(b)], r["w_hi"][:, piece(b)].bitcast(F32), ALU.subtract).then_inc(w_low, 1)

                def first():
                    pool.memset(r["neg_half"][:, :], -0.5).then_inc(r["set_up"], 1)
                    pool.memset(ones[:, :], 1.0).then_inc(ones_set, 1)
                    pool.memset(r["ones8"][:, :], 1.0)
                    pool.wait_ge(r["set_up"], 1)
                    pool.wait_ge(loaded_cols, 16)
                    for t in range(T):
                        pool.tensor_copy(r["ident4"][:, t * P:(t + 1) * P], r["ident"][:, :])
                    rstd1((0, 0))
                    rstd1((1, 0))
                    pool.wait_ge(spread_ready, 4)
                    add_bias((0, 0))

                def step(b, has_before, has_after, has_second):
                    if has_second:
                        rstd1(after(after(b)))
                    if has_after:
                        add_bias(after(b))
                    if has_before:
                        low_piece(before(b))
                    norm_rstd(pool, r, n2[b[0]], b[1])
                    if is_sequence(b, second_last):
                        pool.wait_ge(v_high, 1)
                        pool.tensor_tensor(r["v_lo"][:, :], v_raw[:, :], r["v_hi"][:, :].bitcast(F32), ALU.subtract)

                steps(pool, first, step)
                low_piece(last)
                pool.wait_ge(m_high, 1)
                pool.tensor_tensor(r["m_lo"][:, :, :].rearrange("p h n -> p (h n)"), m_raw[:, :], r["m_hi"][:, :, :].rearrange("p h n -> p (h n)").bitcast(F32), ALU.subtract)

            @block.scalar
            def _(act):
                def normed(b):
                    s, j = b
                    act.wait_ge(shift_ready[s], j + 1)
                    for t in range(T):
                        x = r["x"][:, x_of(b), t, :].rearrange("p b n -> p (b n)")
                        ins = act.activation(n1[s]["out"][:, t, :], x, ACT.Identity, scale=n1[s]["rstd"][:, t:t + 1], bias=shift[s][:, t:t + 1])
                    ins.then_inc(n1[s]["ready"], 1)

                def bring_h(b):
                    s, j = b
                    act.wait_ge(flipped[s], j + 1)
                    modulate(act, r, hT[s][:, :], bank_t[s][:, :], 0, 0, j * 2 + s).then_inc(h_ready[s], 1)

                def bring_u(b):
                    s, j = b
                    act.wait_ge(u_mm[s], j + 1)
                    act.activation(u[s][:, :], bank_u[s][0:SD, :], ACT.Identity, scale=rows[:, R_B:R_B + 1], bias=b_bias[:, 0:1]).then_inc(u_ready[s], 1)

                def spread(k):
                    v, half = SPREADS[k]
                    act.wait_ge(spread_mm, k + 1)
                    dst = r[SPREAD[v]][:, 4 * half:4 * half + 4, :].rearrange("p b n -> p (b n)")
                    act.copy(dst, bank_w[k % 2][:, :]).then_inc(spread_ready, 1)

                def high_piece(b):
                    act.copy(r["w_hi"][:, piece(b)], w_raw[:, piece(b)]).then_inc(w_high, 1)

                def sum_piece(b):
                    act.wait_ge(w_low, b[1] * 2 + b[0] + 1)
                    act.activation(w_raw[:, piece(b)], r["w_lo"][:, piece(b)].bitcast(F32), ACT.Abs, accum_out=w_lo_sum[:, x_of(b)]).then_inc(w_summed, 1)

                def first():
                    load_x(act, 0)
                    act.dma_start(r["cols"][:, :], d["cols"]).then_inc(loaded_cols, 16)
                    act.dma_start(rows[:, :], d["rows"]).then_inc(loaded_rows, 16)
                    act.dma_start(r["cw"][SD:SD + 1, :], d["bo"]).then_inc(loaded_rows, 16)
                    act.wait_ge(loaded_cond, 32)
                    act.activation(scT[:, :, :], cT[:, :, :], ACT.Silu).then_inc(silu_ready, 1)
                    act.wait_ge(loaded_rows, 32)
                    act.activation(lam_col[:, :], rows[:, R_LAM:R_LAM + 1], ACT.Sigmoid).then_inc(lam_ready, 1)
                    act.wait_ge(loaded_x[0], 16)
                    normed((0, 0))
                    act.wait_ge(mod_ready, 2)
                    bring_h((0, 0))
                    act.wait_ge(cw_mm, 1)
                    act.copy(r["cw"][0:SD, :], bank_c[0:SD, 0:D]).then_inc(cw_ready, 1)
                    act.wait_ge(bias_ready, 1)
                    bring_u((0, 0))
                    normed((1, 0))
                    for k in range(4):
                        spread(k)

                def step(b, has_before, has_after, has_second):
                    if has_after:
                        bring_h(after(b))
                        bring_u(after(b))
                    if has_second:
                        normed(after(after(b)))
                    if not has_before:
                        act.wait_ge(loaded_w, 16)
                    high_piece(b)
                    if has_before:
                        sum_piece(before(b))
                    if is_sequence(b, (0, 0)):
                        spread(4)
                        spread(5)
                    if is_sequence(b, third_last):
                        act.wait_ge(loaded_l1, 16 * 6)
                        act.copy(r["v_hi"][:, :], v_raw[:, :]).then_inc(v_high, 1)
                        act.mul(b12_scaled[:, :], b12[:, 0:HID + D], b12[:, HID + D:HID + D + 1]).then_inc(b_scaled, 1)
                        spread(6)
                        spread(7)
                    if is_sequence(b, second_last):
                        act.copy(r["sel"][:, :, :], sel_raw[:, 0:NH, :])
                        act.copy(r["sel32"][:, :, :], sel_raw[:, NH:NH + 2, :])
                        for k in range(2):
                            act.wait_ge(qk_mm, k + 1)
                            act.mul(m_raw[:, k * S:(k + 1) * S], bank_w[k][:, :], DK ** -0.5).then_inc(m_copied, 1)
                    if is_sequence(b, last):
                        act.wait_ge(m_copied, 2)
                        act.copy(r["m_hi"][:, :, :].rearrange("p h n -> p (h n)"), m_raw[:, :]).then_inc(m_high, 1)
                        act.wait_ge(b_scaled, 1)
                        act.copy(r["b1s"][:, :], b12_scaled[:, 0:HID]).then_inc(b_high, 1)
                        act.copy(r["b2s"][:, :], b12_scaled[:, HID:HID + D]).then_inc(b_high, 1)

                steps(act, first, step)
                sum_piece(last)
                act.mul(r["gate_bias"][:, :], r["l1"][:, L_BG:L_BG + 1], 1.0 / GATE_NORM)

            @block.tensor
            def _(pe):
                def flip_in(b):
                    s, j = b
                    pe.wait_ge(n1[s]["ready"], j + 1)
                    flip(pe, bank_t[s], lambda t: n1[s]["out"][:, t, :], r).then_inc(flipped[s], 1)

                def project(b):
                    s, j = b
                    pe.wait_ge(h_ready[s], j + 1)
                    pe.matmul(bank_u[s][0:SD, :], r["wp"][:, :], hT[s][:, :], start=True, stop=True).then_inc(u_mm[s], 1)

                def z(b):
                    s, j = b
                    pe.wait_ge(scanned[s], j + 1)
                    for t in range(T):
                        c = slice(t * P, (t + 1) * P)
                        pe.matmul(bank_z[s][:, c], hT[s][:, c], r["ident"][:, :], start=True, stop=False)
                        mm = pe.matmul(bank_z[s][:, c], state[s][:, c], r["cw"][:, :], start=False, stop=True)
                    mm.then_inc(z_mm[s], 1)

                def spread(k):
                    pe.wait_ge(diag_ready, k + 1)
                    if k >= 2:
                        pe.wait_ge(spread_ready, k - 1)
                    pe.matmul(bank_w[k % 2][:, :], ones[:, :], diag[k % 2][:, :], start=True, stop=True).then_inc(spread_mm, 1)

                def vectors(which, bank):
                    for k, (layer, kind) in enumerate(which):
                        mm = pe.matmul(bank[:, k * B:(k + 1) * B], wmod[:, layer, kind, :], scT[:, layer, :], start=True, stop=True)
                    mm.then_inc(mod_mm, 1)

                def first():
                    pe.wait_ge(silu_ready, 1)
                    vectors(SOON, bank_m[0])
                    vectors(LATER, bank_m[1])
                    pe.wait_ge(loaded_cols, 16)
                    flip_in((0, 0))
                    pe.wait_ge(loaded_rows, 32)
                    pe.matmul(bank_c[0:SD, 0:D], rows[:, R_C:R_C + SD], rows[:, R_WO:R_WO + D], start=True, stop=True).then_inc(cw_mm, 1)
                    project((0, 0))
                    pe.wait_ge(ones_set, 1)
                    for k in range(4):
                        spread(k)
                    pe.wait_ge(state_set, 2)
                    pe.wait_ge(cw_ready, 1)

                def step(b, has_before, has_after, has_second):
                    if has_after:
                        flip_in(after(b))
                    z(b)
                    if has_after:
                        project(after(b))
                    if is_sequence(b, (0, 0)):
                        spread(4)
                        spread(5)
                    if is_sequence(b, third_last):
                        spread(6)
                        spread(7)
                    if is_sequence(b, second_last):
                        pe.wait_ge(loaded_qk, 32)
                        pe.wait_ge(spread_ready, 8)
                        for h in range(NH):
                            mm = pe.matmul(bank_w[h // 4][:, (h % 4) * P:(h % 4 + 1) * P], wqT[:, h, :], wkT[:, h, :], start=True, stop=True)
                            if h % 4 == 3:
                                mm.then_inc(qk_mm, 1)

                steps(pe, first, step)
                pe.wait_ge(w_marked, 1)
                pe.matmul(bank_w[0][0:1, 0:1], w_mark[:, 0:1], ones[:, 0:1], start=True, stop=True).then_inc(w_counted, 1)


def ternary_ffn(nc, r, psum):
    SLOTS = 2
    RING = 4
    with ExitStack() as ctx:
        def sb(name, shape, dt=F32):
            return ctx.enter_context(nc.sbuf_tensor(name, shape, dt))

        sem = ctx.enter_context(Signals(nc))

        slots = range(SLOTS)
        n = norm_buffers(sb, sem, "ffn", SLOTS)
        hf = [sb(f"ffn_h{s}", [P, S]) for s in slots]
        h = [[sb(f"ffn_h_{q}{s}", [P, S], F32R) for q in ("hi", "lo")] for s in slots]
        hid = [[[sb(f"ffn_g{k}_{q}{s}", [P, KH, S], F32R) for q in ("hi", "lo")] for k in range(2)] for s in slots]
        gate = [sb(f"ffn_gate{m}", [P, S]) for m in range(2)]
        full = [sb(f"ffn_full{m}", [P, S]) for m in range(4)]
        yT = hf
        flipped = [sem(f"ffn_flipped{s}") for s in slots]
        h_ready = [sem(f"ffn_h_ready{s}") for s in slots]
        h_high = [sem(f"ffn_h_high{s}") for s in slots]
        h_low = [sem(f"ffn_h_low{s}") for s in slots]
        ring_mm = sem("ffn_ring_mm")
        gate_ready = sem("ffn_gate_ready")
        product_ready = sem("ffn_product_ready")
        gelu_ready = sem("ffn_gelu_ready")
        high = sem("ffn_high")
        low = sem("ffn_low")
        y_mm = [sem(f"ffn_y_mm{s}") for s in slots]
        scaled = [sem(f"ffn_scaled{s}") for s in slots]
        y_flipped = [sem(f"ffn_y_flipped{s}") for s in slots]
        ring = psum[0:RING]
        bank_y = psum[4:6]
        bank_t = psum[6:8]

        TILES = [(s, 0, m) for s in slots for m in range(KH)] + [(s, k, m) for k in (1, 2) for s in slots for m in range(KH)]
        N = len(TILES)
        BANKS = [(j, which) for j, (_, k, _) in enumerate(TILES) for which in ((0, 1) if k == 0 else (0,))]
        NB = len(BANKS)
        N0 = SLOTS * KH
        MOMENTS, RSTD, APPLY, SPLIT = (8, 10), (11, 12), (14, 16), (20, 21)

        def made(i, j):
            return i * N + j + 1

        def layer_done(i, s, k):
            return made(i, TILES.index((s, k, KH - 1)))

        def products(i, j):
            return i * N0 + j + 1

        def gelus(i, j):
            return i * (N - N0) + j - N0 + 1

        PAIRS = B // SLOTS
        LAYER = {0: range(0, N0), 1: range(N0, N - N0), 2: range(N - N0, N)}

        with nc.Block() as block:
            @block.vector
            def _(dve):
                def tile_of(i, s):
                    return lambda t: r["x"][:, bass.ds(i * SLOTS + s, 1), t, :]

                def split_h(i, s):
                    dve.wait_ge(h_ready[s], i + 1)
                    dve.tensor_copy(h[s][0][:, :], hf[s][:, :]).then_inc(h_high[s], 1)
                    dve.wait_ge(h_high[s], i + 1)
                    dve.tensor_tensor(h[s][1][:, :], hf[s][:, :], h[s][0][:, :].bitcast(F32), ALU.subtract).then_inc(h_low[s], 1)

                def add(i, s):
                    dve.wait_ge(y_flipped[s], i + 1)
                    x = r["x"][:, bass.ds(i * SLOTS + s, 1), :, :].rearrange("p b t n -> p (b t n)")
                    dve.tensor_tensor(x, x, bank_y[s][:, :], ALU.add)

                def layer0(i, first):
                    for j in LAYER[0]:
                        s, _, m = TILES[j]
                        f = full[j % 4]
                        dve.wait_ge(gate_ready, products(i, j))
                        dve.wait_ge(ring_mm, i * NB + 2 * j + 2)
                        if j >= 4 or not first:
                            dve.wait_ge(low, made(i, j - 4))
                        dve.scalar_tensor_tensor(out=f[:, :], in0=ring[(2 * j + 1) % RING][:, :], scalar=r["w_scale"][:, 1, m:m + 1], in1=gate[j % 2][:, :], op0=ALU.mult, op1=ALU.mult).then_inc(product_ready, 1)
                        dve.wait_ge(product_ready, products(i, j))
                        dve.tensor_copy(hid[s][0][0][:, m, :], f[:, :]).then_inc(high, 1)
                        if not first and m == KH - 1:
                            add(i - 1, s)

                def body(i, more):
                    for j in (*LAYER[1], *LAYER[2]):
                        s, k, m = TILES[j]
                        dve.wait_ge(gelu_ready, gelus(i, j))
                        dve.tensor_copy(hid[s][k % 2][0][:, m, :], full[j % 4][:, :]).then_inc(high, 1)
                        if more and j in MOMENTS:
                            q = MOMENTS.index(j)
                            norm_moments(dve, r, n[q], i + 1, tile_of(i + 1, q))
                        if more and j in APPLY:
                            q = APPLY.index(j)
                            norm_apply(dve, n[q], i + 1, tile_of(i + 1, q))
                        if more and j in SPLIT:
                            split_h(i + 1, SPLIT.index(j))
                    if more:
                        layer0(i + 1, False)

                for q in slots:
                    norm_moments(dve, r, n[q], 0, tile_of(0, q))
                for q in slots:
                    norm_apply(dve, n[q], 0, tile_of(0, q))
                for s in slots:
                    split_h(0, s)
                layer0(0, True)
                with dve.Fori(0, PAIRS - 1) as i:
                    body(i, True)
                body(PAIRS - 1, False)
                for s in slots:
                    add(PAIRS - 1, s)

            @block.gpsimd
            def _(pool):
                def lows(i, js, more):
                    for j in js:
                        s, k, m = TILES[j]
                        pool.wait_ge(high, made(i, j))
                        pool.tensor_tensor(hid[s][k % 2][1][:, m, :], full[j % 4][:, :], hid[s][k % 2][0][:, m, :].bitcast(F32), ALU.subtract).then_inc(low, 1)
                        if more and j in RSTD:
                            norm_rstd(pool, r, n[RSTD.index(j)], i + 1)

                def body(i, more):
                    lows(i, (*LAYER[1], *LAYER[2]), more)
                    if more:
                        lows(i + 1, LAYER[0], False)

                for q in slots:
                    norm_rstd(pool, r, n[q], 0)
                lows(0, LAYER[0], False)
                with pool.Fori(0, PAIRS - 1) as i:
                    body(i, True)
                body(PAIRS - 1, False)

            @block.scalar
            def _(act):
                def bring_h(i, s):
                    act.wait_ge(flipped[s], i + 1)
                    modulate(act, r, hf[s][:, :], bank_t[s][:, :], 0, 2, i * SLOTS + s).then_inc(h_ready[s], 1)

                def bring_y(i, s, split):
                    act.wait_ge(y_mm[s], i + 1)
                    act.wait_ge(h_low[s], split)
                    act.activation(yT[s][:, :], bank_y[s][:, :], ACT.Copy, scale=r["gain_ffn0"][:, bass.ds(i * SLOTS + s, 1)]).then_inc(scaled[s], 1)

                def layer0(i, first):
                    for j in LAYER[0]:
                        s, _, m = TILES[j]
                        act.wait_ge(ring_mm, i * NB + 2 * j + 1)
                        if j >= 2:
                            act.wait_ge(product_ready, products(i, j - 2))
                        act.activation(gate[j % 2][:, :], ring[(2 * j) % RING][:, :], ACT.Silu, scale=r["w_scale"][:, 0, m:m + 1]).then_inc(gate_ready, 1)
                        if not first and j == KH - 1:
                            bring_y(i - 1, 1, i + 1)

                def body(i, more):
                    for j in (*LAYER[1], *LAYER[2]):
                        s, k, m = TILES[j]
                        act.wait_ge(ring_mm, i * NB + N0 + j + 1)
                        act.wait_ge(low, made(i, j - 4))
                        act.activation(full[j % 4][:, :], ring[(N0 + j) % RING][:, :], ACT.Gelu, scale=r["w_scale"][:, 1 + k, m:m + 1]).then_inc(gelu_ready, 1)
                        if more and (s, k, m) == (0, 2, KH - 1):
                            for q in slots:
                                bring_h(i + 1, q)
                    bring_y(i, 0, i + 2 if more else i + 1)
                    if more:
                        layer0(i + 1, False)

                for s in slots:
                    bring_h(0, s)
                layer0(0, True)
                with act.Fori(0, PAIRS - 1) as i:
                    body(i, True)
                body(PAIRS - 1, False)
                bring_y(PAIRS - 1, 1, PAIRS)

            @block.tensor
            def _(pe):
                def w(col, k, width):
                    at = col + k * width
                    return r["w_hi"][:, at:at + P], r["w_lo"][:, at:at + P]

                def run(rounded):
                    def products_of(acc, w, x, start, stop):
                        if not rounded:
                            return split_mm(pe, acc, w, x, start, stop)
                        pe.matmul(acc, w[0], x[0], start=start, stop=False)
                        return pe.matmul(acc, w[0], x[1], start=False, stop=stop)

                    def flip_in(i, s):
                        pe.wait_ge(n[s]["ready"], i + 1)
                        flip(pe, bank_t[s], lambda t: n[s]["out"][:, t, :], r).then_inc(flipped[s], 1)

                    def hidden(i, js, first):
                        for g, (j, which) in enumerate(BANKS):
                            if j not in js:
                                continue
                            s, k, m = TILES[j]
                            acc = ring[g % RING]
                            if g < RING:
                                if not first:
                                    pe.wait_ge(gelu_ready, gelus(i - 1, N - RING + g))
                            else:
                                pj, pw = BANKS[g - RING]
                                if TILES[pj][1] == 0:
                                    pe.wait_ge(product_ready if pw else gate_ready, products(i, pj))
                                else:
                                    pe.wait_ge(gelu_ready, gelus(i, pj))
                            if k == 0:
                                if m == 0 and which == 0:
                                    pe.wait_ge(h_low[s], i + 1)
                                col = (W1, W2)[which] + m * P
                                mm = products_of(acc[:, :], w(col, 0, 0), [h[s][q][:, :] for q in range(2)], True, True)
                            else:
                                if m == 0:
                                    pe.wait_ge(low, layer_done(i, s, k - 1))
                                x = hid[s][(k - 1) % 2]
                                for kk in range(KH):
                                    mm = products_of(acc[:, :], w((H1, H2)[k - 1] + m * P, kk, HID), [x[q][:, kk, :] for q in range(2)], kk == 0, kk == KH - 1)
                            mm.then_inc(ring_mm, 1)

                    def y(i, s):
                        pe.wait_ge(low, layer_done(i, s, 2))
                        for kk in range(KH):
                            mm = products_of(bank_y[s][:, :], w(W3, kk, D), [hid[s][0][q][:, kk, :] for q in range(2)], kk == 0, kk == KH - 1)
                        mm.then_inc(y_mm[s], 1)

                    def flip_back(i, s):
                        pe.wait_ge(scaled[s], i + 1)
                        flip(pe, bank_y[s], lambda t: yT[s][:, t * P:(t + 1) * P], r).then_inc(y_flipped[s], 1)

                    def body(i, more):
                        hidden(i, LAYER[1], False)
                        hidden(i, LAYER[2][:KH], False)
                        if more:
                            for s in slots:
                                flip_in(i + 1, s)
                        hidden(i, LAYER[2][KH:], False)
                        y(i, 0)
                        if more:
                            hidden(i + 1, LAYER[0][:KH], False)
                        y(i, 1)
                        flip_back(i, 0)
                        if more:
                            hidden(i + 1, LAYER[0][KH:], False)
                        flip_back(i, 1)

                    for s in slots:
                        flip_in(0, s)
                    hidden(0, LAYER[0], True)
                    with pe.Fori(0, PAIRS - 1) as i:
                        body(i, True)
                    body(PAIRS - 1, False)

                inexact = pe.value_load(r["w_inexact"][0:1, 0:1], min_val=0, max_val=1)
                with pe.If(inexact):
                    run(False)
                with pe.Else():
                    run(True)


def linear_attention(nc, r, psum):
    SLOTS = 2
    PAIRS = B // SLOTS
    RING = 4
    with ExitStack() as ctx:
        def sb(name, shape, dt=F32):
            return ctx.enter_context(nc.sbuf_tensor(name, shape, dt))

        sem = ctx.enter_context(Signals(nc))

        slots = range(SLOTS)
        n = norm_buffers(sb, sem, "att", SLOTS)
        hT = [sb(f"att_hT{s}", [P, S]) for s in slots]
        h = [[sb(f"att_h_{q}{s}", [P, S], F32R) for q in ("hi", "lo")] for s in slots]
        htok = [sb(f"att_htok{s}", [P, T, D]) for s in slots]
        qT = [sb(f"att_qT{s}", [P, NH, S]) for s in slots]
        v = [sb(f"att_v{s}", [P, T, HV]) for s in slots]
        og = [sb(f"att_og{s}", [P, 2, S]) for s in slots]
        GR = GLO + NH
        alpha = [sb(f"att_alpha{s}", [GR, S]) for s in slots]
        cut = [sb(f"att_cut{s}", [GR, S]) for s in slots]
        start = [sb(f"att_start{s}", [GR, S]) for s in slots]
        cut_in = [sb(f"att_cut_in{s}", [GR, S], F32R) for s in slots]
        cum = [sb(f"att_cum{s}", [GR, S]) for s in slots]
        cum_in = [sb(f"att_cum_in{s}", [GR, S], F32R) for s in slots]
        ends = [sb(f"att_ends{s}", [NH, T, NH]) for s in slots]
        total = [sb(f"att_total{s}", [P, T, NH]) for s in slots]
        wide = [sb(f"att_wide{s}", [P, 2, S]) for s in slots]
        decay = [sb(f"att_decay{m}", [P, S]) for m in range(2)]
        prob = [sb(f"att_prob{m}", [P, S]) for m in range(2)]
        vw = [sb(f"att_vw{s}", [P, T, HV]) for s in slots]
        state = [sb(f"att_state{s}", [P, T, HV]) for s in slots]
        grown = sb("att_grown", [P, HV])
        inner = [sb(f"att_inner{s}", [P, 2, S]) for s in slots]
        outer = [sb(f"att_outer{s}", [P, 2, S]) for s in slots]
        upd = [sb(f"att_upd{s}", [P, T, D]) for s in slots]

        def sems(name):
            return [sem(f"att_{name}{s}") for s in slots]

        ring_mm = sem("att_ring_mm")
        h_ready, h_high, h_low = sems("h_ready"), sems("h_high"), sems("h_low")
        q_ready, v_ready, og_ready, htok_ready = sems("q_ready"), sems("v_ready"), sems("og_ready"), sems("htok_ready")
        alpha_ready, cut_ready, cut_high, cut_low = sems("alpha_ready"), sems("cut_ready"), sems("cut_high"), sems("cut_low")
        start_ready, cum_ready, cum_high, cum_low = sems("start_ready"), sems("cum_ready"), sems("cum_high"), sems("cum_low")
        ends_ready, total_ready, wide_ready = sems("ends_ready"), sems("total_ready"), sems("wide_ready")
        decay_ready, prob_ready, vw_ready = sem("att_decay_ready"), sem("att_prob_ready"), sem("att_vw_ready")
        intra_mm, inter_mm, state_ready, grown_ready = sems("intra_mm"), sems("inter_mm"), sems("state_ready"), sem("att_grown_ready")
        inner_ready, outer_ready, summed, gated = sems("inner_ready"), sems("outer_ready"), sems("summed"), sems("gated")
        scaled, added = sems("scaled"), sems("added")
        ring = psum[0:RING]
        bank_o = psum[4:6]
        bank_s = psum[6:8]

        def project_uses(s, a):
            return ([(s, a, "alpha", 0)] + [(s, a, "q", k) for k in range(NH)],
                    [(s, a, "v", 0), (s, a, "v", 1), (s, a, "og", 0), (s, a, "og", 1), (s, a, "htok", 0),
                     (s, a, "total", 0), (s, a, "wide", 0), (s, a, "wide", 1)])

        FLIP1, FLIP0 = 5, 6

        def pair_uses(more):
            uses = []
            for s, at in ((0, FLIP1), (1, FLIP0)):
                for k in range(NH):
                    uses += [(s, 0, "decay", k), (s, 0, "score", k)]
                    if k == at and s == 0:
                        uses.append((1, 0, "flip", 0))
                    if k == at and s == 1 and more:
                        uses.append((0, 1, "flip", 0))
                if s == 0:
                    a, b = project_uses(1, 0)
                    uses += a + b + [(0, 0, "state", c) for c in range(3)]
            uses += [(0, 0, "y", 0)] + [(1, 0, "state", c) for c in range(3)]
            if more:
                a, b = project_uses(0, 1)
                return uses + a + [(1, 0, "y", 0)] + b
            return uses + [(1, 0, "y", 0)]

        a, b = project_uses(0, 0)
        FIRST = [(0, 0, "flip", 0)] + a + b
        OFFSET = -len(FIRST) % RING
        USES = {more: pair_uses(more) for more in (True, False)}
        assert len(USES[True]) % RING == 0 and USES[True][-RING:] == [(s, 1, w, k) for s, _, w, k in FIRST[-RING:]]

        class Ring:

            def __init__(self, i, more):
                self.i, self.uses = i, FIRST if i is None else USES[more]
                self.base = 0 if i is None else len(FIRST) + i * len(USES[True])
                self.skew = OFFSET if i is None else 0

            def full(self, *use):
                return self.base + self.uses.index(use) + 1

            def bank(self, *use):
                return ring[(self.skew + self.uses.index(use)) % RING]

            def pair(self, ahead):
                return ahead if self.i is None else self.i + ahead

            def claim(self, pe, *use):
                at = self.uses.index(use) - RING
                if at >= 0:
                    s, ahead, what, k = self.uses[at]
                    i = self.pair(ahead)
                elif self.i is not None:
                    s, _, what, k = FIRST[at]
                    i = self.i
                else:
                    return self.bank(*use)
                signal, count = {
                    "flip": (h_ready[s], i + 1), "alpha": (alpha_ready[s], i + 1), "q": (q_ready[s], i * NH + k + 1),
                    "v": (v_ready[s], i * 2 + k + 1), "og": (og_ready[s], i * 2 + k + 1), "htok": (htok_ready[s], i + 1),
                    "total": (total_ready[s], i + 1), "wide": (wide_ready[s], i * 2 + k + 1),
                    "decay": (decay_ready, nth(i, s, NH, k)), "score": (prob_ready, nth(i, s, NH, k)),
                    "state": (state_ready[s], i * 3 + k + 1), "y": (scaled[s], i + 1),
                }[what]
                pe.wait_ge(signal, count)
                return self.bank(*use)

        def nth(i, s, per, k):
            return i * SLOTS * per + s * per + k + 1

        with nc.Block() as block:
            def x_tile(i, s):
                return lambda t: r["x"][:, bass.ds(i * SLOTS + s, 1), t, :]

            def by_head(ap):
                return ap.rearrange("p (h n) -> p h n", h=NH)

            @block.vector
            def _(dve):
                def split(i, s):
                    dve.wait_ge(h_ready[s], i + 1)
                    dve.tensor_copy(h[s][0][:, :], hT[s][:, :]).then_inc(h_high[s], 1)

                def decays(i, s):
                    dve.wait_ge(alpha_ready[s], i + 1)
                    dve.tensor_tensor(cut[s][:, :], alpha[s][:, :], r["keep"][:, :], ALU.mult).then_inc(cut_ready[s], 1)
                    dve.wait_ge(cut_ready[s], i + 1)
                    dve.tensor_tensor(start[s][:, :], alpha[s][:, :], cut[s][:, :], ALU.subtract).then_inc(start_ready[s], 1)
                    dve.wait_ge(start_ready[s], i + 1)
                    dve.tensor_tensor_scan(cum[s][:, :], cut[s][:, :], start[s][:, :], 0.0, ALU.mult, ALU.add).then_inc(cum_ready[s], 1)
                    dve.wait_ge(cum_ready[s], i + 1)
                    last = cum[s][0:NH, :].rearrange("p (c n) -> p c n", c=T)[:, :, P - 1:P]
                    dve.tensor_tensor(ends[s][:, :, :], last.broadcast_to([NH, T, NH]), over(r["eye8"][:, :], 1, [NH, T, NH]), ALU.mult).then_inc(ends_ready[s], 1)

                def values(g, i, a, s):
                    for k in range(2):
                        dve.wait_ge(ring_mm, g.full(s, a, "v", k))
                        dve.tensor_copy(v[s][:, 2 * k:2 * k + 2, :].rearrange("p c n -> p (c n)"), g.bank(s, a, "v", k)[:, :]).then_inc(v_ready[s], 1)
                    dve.wait_ge(ring_mm, g.full(s, a, "total", 0))
                    dve.tensor_copy(total[s][:, :, :].rearrange("p c n -> p (c n)"), g.bank(s, a, "total", 0)[:, 0:T * NH]).then_inc(total_ready[s], 1)

                def head(g, i, s, k):
                    m = k % 2
                    dve.wait_ge(ring_mm, g.full(s, 0, "decay", k))
                    if s or k >= 2:
                        dve.wait_ge(vw_ready, nth(i, s, NH, k - 2))
                    dve.tensor_tensor_scan(decay[m][:, :], g.bank(s, 0, "decay", k)[:, :], r["ident4"][:, :], 0.0, ALU.mult, ALU.add).then_inc(decay_ready, 1)
                    dve.wait_ge(decay_ready, nth(i, s, NH, k))
                    dve.wait_ge(ring_mm, g.full(s, 0, "score", k))
                    if k >= 2:
                        dve.wait_ge(intra_mm[s], i * NH + k - 1)
                    elif s:
                        dve.wait_ge(intra_mm[0], i * NH + NH - 1 + k)
                    dve.tensor_tensor(prob[m][:, :], g.bank(s, 0, "score", k)[:, :], decay[m][:, :], ALU.mult).then_inc(prob_ready, 1)

                def states(g, i, s):
                    for c in range(3):
                        new = state[s][:, c + 1, :]
                        ps = g.bank(s, 0, "state", c)[:, 0:HV]
                        dve.wait_ge(ring_mm, g.full(s, 0, "state", c))
                        if c == 0:
                            dve.tensor_copy(new, ps).then_inc(state_ready[s], 1)
                            continue
                        dve.wait_ge(state_ready[s], i * 3 + c)
                        dve.tensor_tensor(by_head(grown[:, :]), by_head(state[s][:, c, :]), over(total[s][:, c, :], 2, [P, NH, DV]), ALU.mult).then_inc(grown_ready, 1)
                        dve.wait_ge(grown_ready, nth(i, s, 2, c - 1))
                        dve.tensor_tensor(new, grown[:, :], ps, ALU.add).then_inc(state_ready[s], 1)

                def across(i, s, q):
                    dve.wait_ge(inter_mm[s], i + 1)
                    dve.wait_ge(wide_ready[s], (i + 1) * 2)
                    dve.tensor_tensor(outer[s][:, q, P:S], bank_s[q][:, P:S], wide[s][:, q, P:S], ALU.mult).then_inc(outer_ready[s], 1)

                def scale(g, i, s):
                    dve.wait_ge(ring_mm, g.full(s, 0, "y", 0))
                    gain = r["gain_attn1"][:, bass.ds(i * SLOTS + s, 1), :].broadcast_to([P, T, D])
                    dve.tensor_tensor(upd[s][:, :, :], g.bank(s, 0, "y", 0)[:, :].rearrange("p (t n) -> p t n", t=T), gain, ALU.mult).then_inc(scaled[s], 1)

                def body(i, more):
                    g = Ring(i, more)
                    for k in range(NH):
                        head(g, i, 0, k)
                        if k == FLIP1 + 1:
                            split(i, 1)
                    decays(i, 1)
                    values(g, i, 0, 1)
                    states(g, i, 0)
                    if more:
                        norm_moments(dve, r, n[0], i + 1, x_tile(i + 1, 0))
                    for k in range(NH):
                        head(g, i, 1, k)
                        if k in (1, 2):
                            across(i, 0, k - 1)
                        if k == 4 and more:
                            norm_apply(dve, n[0], i + 1, x_tile(i + 1, 0))
                        if k == FLIP0 + 1 and more:
                            split(i + 1, 0)
                    scale(g, i, 0)
                    states(g, i, 1)
                    across(i, 1, 0)
                    across(i, 1, 1)
                    if more:
                        decays(i + 1, 0)
                        norm_moments(dve, r, n[1], i + 1, x_tile(i + 1, 1))
                    scale(g, i, 1)
                    if more:
                        values(g, i + 1, 1, 0)
                        norm_apply(dve, n[1], i + 1, x_tile(i + 1, 1))

                for s in slots:
                    norm_moments(dve, r, n[s], 0, x_tile(0, s))
                for s in slots:
                    norm_apply(dve, n[s], 0, x_tile(0, s))
                split(0, 0)
                decays(0, 0)
                values(Ring(None, True), 0, 0, 0)
                with dve.Fori(0, PAIRS - 1) as i:
                    body(i, True)
                body(PAIRS - 1, False)

            @block.gpsimd
            def _(pool):
                def low_h(i, s):
                    pool.wait_ge(h_high[s], i + 1)
                    pool.tensor_tensor(h[s][1][:, :], hT[s][:, :], h[s][0][:, :].bitcast(F32), ALU.subtract).then_inc(h_low[s], 1)

                def low_cut(i, s, before, count):
                    lo = slice(GLO, GR)
                    pool.wait_ge(before, count)
                    pool.wait_ge(cut_high[s], i + 1)
                    pool.tensor_tensor(cut_in[s][lo, :], cut[s][lo, :], cut_in[s][lo, :].bitcast(F32), ALU.subtract).then_inc(cut_low[s], 1)
                    pool.wait_ge(cut_low[s], i + 1)

                def low_cum(i, s, before, count):
                    lo = slice(GLO, GR)
                    pool.wait_ge(before, count)
                    pool.wait_ge(cum_high[s], i + 1)
                    pool.tensor_tensor(cum_in[s][lo, :], cum[s][lo, :], cum_in[s][lo, :].bitcast(F32), ALU.subtract).then_inc(cum_low[s], 1)
                    wait_apart(pool, r, cum_low[s], i + 1)

                def decay_v(i, s, k):
                    if k == 0:
                        pool.wait_ge(v_ready[s], (i + 1) * 2)
                    pool.wait_ge(decay_ready, nth(i, s, NH, k))
                    hs = slice(k * DV, (k + 1) * DV)
                    last = decay[k % 2][:, :].rearrange("p (c n) -> p c n", c=T)[:, :, P - 1:P]
                    pool.tensor_tensor(vw[s][:, :, hs], v[s][:, :, hs], last.broadcast_to([P, T, DV]), ALU.mult).then_inc(vw_ready, 1)

                def gate(i, s):
                    pool.wait_ge(inner_ready[s], (i + 1) * 2)
                    pool.wait_ge(outer_ready[s], (i + 1) * 2)
                    pool.tensor_tensor(outer[s][:, :, P:S], outer[s][:, :, P:S], inner[s][:, :, P:S], ALU.add).then_inc(summed[s], 1)
                    pool.tensor_tensor(outer[s][:, :, 0:P], inner[s][:, :, 0:P], og[s][:, :, 0:P], ALU.mult)
                    pool.wait_ge(summed[s], i + 1)
                    pool.tensor_tensor(outer[s][:, :, P:S], outer[s][:, :, P:S], og[s][:, :, P:S], ALU.mult).then_inc(gated[s], 1)

                def add(i, s):
                    pool.wait_ge(scaled[s], i + 1)
                    x = r["x"][:, bass.ds(i * SLOTS + s, 1), :, :].rearrange("p b t n -> p (b t) n")
                    pool.tensor_tensor(x, x, upd[s][:, :, :], ALU.add).then_inc(added[s], 1)

                def body(i, more):
                    for k in range(NH):
                        decay_v(i, 0, k)
                        if k == FLIP1 + 1:
                            low_h(i, 1)
                    low_cut(i, 1, vw_ready, nth(i, 0, NH, NH - 1))
                    low_cum(i, 1, cut_low[1], i + 1)
                    if more:
                        norm_rstd(pool, r, n[0], i + 1)
                    for k in range(NH):
                        decay_v(i, 1, k)
                        if k == 3:
                            gate(i, 0)
                    if more:
                        low_h(i + 1, 0)
                    add(i, 0)
                    if more:
                        low_cut(i + 1, 0, added[0], i + 1)
                    gate(i, 1)
                    if more:
                        low_cum(i + 1, 0, gated[1], i + 1)
                    if more:
                        norm_rstd(pool, r, n[1], i + 1)
                    add(i, 1)

                for s in slots:
                    norm_rstd(pool, r, n[s], 0)
                low_h(0, 0)
                low_cut(0, 0, h_low[0], 1)
                low_cum(0, 0, cut_low[0], 1)
                with pool.Fori(0, PAIRS - 1) as i:
                    body(i, True)
                body(PAIRS - 1, False)

            @block.scalar
            def _(act):
                def bring_h(g, i, a, s):
                    act.wait_ge(ring_mm, g.full(s, a, "flip", 0))
                    modulate(act, r, hT[s][:, :], g.bank(s, a, "flip", 0)[:, :], 1, 0, i * SLOTS + s).then_inc(h_ready[s], 1)

                def queries(g, s, a, ks):
                    for k in ks:
                        act.wait_ge(ring_mm, g.full(s, a, "q", k))
                        act.copy(qT[s][:, k, :], g.bank(s, a, "q", k)[:, :]).then_inc(q_ready[s], 1)

                def project(g, i, a, s):
                    act.wait_ge(ring_mm, g.full(s, a, "alpha", 0))
                    act.activation(alpha[s][:, :], g.bank(s, a, "alpha", 0)[0:GR, :], ACT.Sigmoid, scale=1.0 / GATE_NORM, bias=r["gate_bias"][0:GR, 0:1]).then_inc(alpha_ready[s], 1)
                    queries(g, s, a, range(0, 2))
                    act.wait_ge(cut_ready[s], i + 1)
                    act.copy(cut_in[s][:, :], cut[s][:, :]).then_inc(cut_high[s], 1)
                    queries(g, s, a, range(2, 5))
                    act.wait_ge(cum_ready[s], i + 1)
                    act.copy(cum_in[s][:, :], cum[s][:, :]).then_inc(cum_high[s], 1)
                    queries(g, s, a, range(5, NH))
                    for q in range(2):
                        act.wait_ge(ring_mm, g.full(s, a, "og", q))
                        act.activation(og[s][:, q, :], g.bank(s, a, "og", q)[:, :], ACT.Sigmoid).then_inc(og_ready[s], 1)
                    act.wait_ge(ring_mm, g.full(s, a, "htok", 0))
                    act.copy(htok[s][:, :, :].rearrange("p t n -> p (t n)"), g.bank(s, a, "htok", 0)[:, :]).then_inc(htok_ready[s], 1)
                    for q in range(2):
                        act.wait_ge(ring_mm, g.full(s, a, "wide", q))
                        act.copy(wide[s][:, q, :], g.bank(s, a, "wide", q)[:, :]).then_inc(wide_ready[s], 1)

                def keep_inner(i, s):
                    act.wait_ge(intra_mm[s], (i + 1) * NH)
                    for q in range(2):
                        act.copy(inner[s][:, q, :], bank_o[q][:, :]).then_inc(inner_ready[s], 1)

                def body(i, more):
                    g = Ring(i, more)
                    bring_h(g, i, 0, 1)
                    project(g, i, 0, 1)
                    keep_inner(i, 0)
                    if more:
                        bring_h(g, i + 1, 1, 0)
                    keep_inner(i, 1)
                    if more:
                        project(g, i + 1, 1, 0)

                first = Ring(None, True)
                bring_h(first, 0, 0, 0)
                project(first, 0, 0, 0)
                with act.Fori(0, PAIRS - 1) as i:
                    body(i, True)
                body(PAIRS - 1, False)

            @block.tensor
            def _(pe):
                def flip_in(g, i, a, s):
                    pe.wait_ge(n[s]["ready"], i + 1)
                    b = g.claim(pe, s, a, "flip", 0)
                    flip(pe, b, lambda t: n[s]["out"][:, t, :], r).then_inc(ring_mm, 1)

                def project(g, i, a, s, between=None):
                    hh = [h[s][q][:, :] for q in range(2)]
                    pe.wait_ge(h_low[s], i + 1)
                    b = g.claim(pe, s, a, "alpha", 0)
                    split_mm(pe, b[:, :], (r["v_hi"][:, GT:GT + P], r["v_lo"][:, GT:GT + P]), hh, True, True).then_inc(ring_mm, 1)
                    for k in range(NH):
                        b = g.claim(pe, s, a, "q", k)
                        split_mm(pe, b[:, :], (r["m_hi"][:, k, :], r["m_lo"][:, k, :]), hh, True, True).then_inc(ring_mm, 1)
                    if between:
                        between()
                    for k in range(2):
                        b = g.claim(pe, s, a, "v", k)
                        for t in (2 * k, 2 * k + 1):
                            c = slice(t * P, (t + 1) * P)
                            o = (t % 2) * HV
                            mm = split_mm(pe, b[:, o:o + HV], [x[:, c] for x in hh], (r["v_hi"][:, VO:VO + HV], r["v_lo"][:, VO:VO + HV]), True, True)
                        mm.then_inc(ring_mm, 1)
                    for q in range(2):
                        b = g.claim(pe, s, a, "og", q)
                        at = slice(VO + HV + q * P, VO + HV + (q + 1) * P)
                        split_mm(pe, b[:, :], (r["v_hi"][:, at], r["v_lo"][:, at]), hh, True, True).then_inc(ring_mm, 1)
                    b = g.claim(pe, s, a, "htok", 0)
                    flip(pe, b, lambda t: hT[s][:, t * P:(t + 1) * P], r).then_inc(ring_mm, 1)
                    pe.wait_ge(ends_ready[s], i + 1)
                    b = g.claim(pe, s, a, "total", 0)
                    pe.matmul(b[:, 0:T * NH], r["ones8"][:, :], ends[s][:, :, :].rearrange("p c n -> p (c n)"), start=True, stop=True).then_inc(ring_mm, 1)
                    pe.wait_ge(cum_low[s], i + 1)
                    for q in range(2):
                        b = g.claim(pe, s, a, "wide", q)
                        pe.matmul(b[:, :], r["sel32"][:, q, :], cum_in[s][:, :], start=True, stop=True).then_inc(ring_mm, 1)

                def inside(i, s, k):
                    pe.wait_ge(prob_ready, nth(i, s, NH, k))
                    rows = slice((k % 4) * DV, (k % 4 + 1) * DV)
                    for c in range(T):
                        cc = slice(c * P, (c + 1) * P)
                        mm = pe.matmul(bank_o[k // 4][rows, cc], v[s][:, c, k * DV:(k + 1) * DV], prob[k % 2][:, cc], start=True, stop=True)
                    mm.then_inc(intra_mm[s], 1)

                def heads(g, i, s, at, then):
                    pe.wait_ge(cut_low[s], i + 1)
                    pe.wait_ge(v_ready[s], (i + 1) * 2)
                    pe.wait_ge(q_ready[s], (i + 1) * NH)
                    for k in range(NH):
                        b = g.claim(pe, s, 0, "decay", k)
                        pe.matmul(b[:, :], r["sel"][:, k, :], cut_in[s][:, :], start=True, stop=True).then_inc(ring_mm, 1)
                        b = g.claim(pe, s, 0, "score", k)
                        for c in range(T):
                            cc = slice(c * P, (c + 1) * P)
                            mm = pe.matmul(b[:, cc], hT[s][:, cc], qT[s][:, k, cc], start=True, stop=True)
                        mm.then_inc(ring_mm, 1)
                        if k == at and then:
                            then()
                        if k == 1 and s == 1:
                            pe.wait_ge(inner_ready[0], (i + 1) * 2)
                        if k >= 1:
                            inside(i, s, k - 1)

                def cross(g, i, s):
                    pe.wait_ge(vw_ready, nth(i, s, NH, NH - 1))
                    pe.wait_ge(htok_ready[s], i + 1)
                    for c in range(3):
                        b = g.claim(pe, s, 0, "state", c)
                        pe.matmul(b[:, 0:HV], htok[s][:, c, :], vw[s][:, c, :], start=True, stop=True).then_inc(ring_mm, 1)
                    for c in range(1, T):
                        pe.wait_ge(state_ready[s], i * 3 + c)
                        cc = slice(c * P, (c + 1) * P)
                        for k in range(NH):
                            rows = slice((k % 4) * DV, (k % 4 + 1) * DV)
                            mm = pe.matmul(bank_s[k // 4][rows, cc], state[s][:, c, k * DV:(k + 1) * DV], qT[s][:, k, cc], start=True, stop=True)
                    mm.then_inc(inter_mm[s], 1)

                def output(g, i, s):
                    pe.wait_ge(gated[s], i + 1)
                    b = g.claim(pe, s, 0, "y", 0)
                    for t in range(T):
                        c = slice(t * P, (t + 1) * P)
                        for q in range(2):
                            mm = pe.matmul(b[:, c], outer[s][:, q, c], r["wo"][:, q, :], start=(q == 0), stop=(q == 1))
                    mm.then_inc(ring_mm, 1)

                def body(i, more):
                    g = Ring(i, more)
                    heads(g, i, 0, FLIP1, lambda: flip_in(g, i, 0, 1))
                    inside(i, 0, NH - 1)
                    project(g, i, 0, 1)
                    cross(g, i, 0)
                    heads(g, i, 1, FLIP0, (lambda: flip_in(g, i + 1, 1, 0)) if more else None)
                    inside(i, 1, NH - 1)
                    output(g, i, 0)
                    cross(g, i, 1)
                    if more:
                        project(g, i + 1, 1, 0, lambda: output(g, i, 1))
                    else:
                        output(g, i, 1)

                first = Ring(None, True)
                flip_in(first, 0, 0, 0)
                project(first, 0, 0, 0)
                with pe.Fori(0, PAIRS - 1) as i:
                    body(i, True)
                body(PAIRS - 1, False)


def lora_ffn(nc, r, psum, out):
    with ExitStack() as ctx:
        def sb(name, shape, dt=F32):
            return ctx.enter_context(nc.sbuf_tensor(name, shape, dt))

        sem = ctx.enter_context(Signals(nc))
        slots = range(2)
        n = norm_buffers(sb, sem, "lora", 2)
        hT = [sb(f"lora_hT{s}", [P, S]) for s in slots]
        h = [[sb(f"lora_h_{q}{s}", [P, S], F32R) for q in ("hi", "lo")] for s in slots]
        hid = [sb(f"lora_hid{s}", [P, KH, S]) for s in slots]

        def pairs(name, shape, dt=F32):
            return [[sb(f"lora_{name}{k}{s}", shape, dt) for s in slots] for k in range(2)]

        top, shifted, expo = pairs("top", [P, T]), pairs("shifted", [P, T, E]), pairs("expo", [P, T, E])
        den, inv, prob = pairs("den", [P, T]), pairs("inv", [P, T]), pairs("prob", [P, T, E])
        zg = pairs("zg", [P, T, ER])
        stack = pairs("stack", [P, T, 3 * GLO])
        zT = pairs("zT", [3 * GLO, S], F32R)
        upd = [sb(f"lora_upd{s}", [P, T, D]) for s in slots]
        res = [sb(f"lora_res{s}", [P, T, D]) for s in slots]

        def sems(name):
            return [sem(f"lora_{name}{s}") for s in slots]

        def sems2(name):
            return [sems(f"{name}_{k}_") for k in range(2)]

        stack_cleared, stack_set = sem("lora_stack_cleared"), sem("lora_stack_set")
        flipped, h_ready, h_high, h_low = sems("flipped"), sems("h_ready"), sems("h_high"), sems("h_low")
        down_mm, top_ready, shift_ready, expo_ready = sems2("down_mm"), sems2("top_ready"), sems2("shift_ready"), sems2("expo_ready")
        den_ready, inv_ready, prob_ready, zg_ready = sems2("den_ready"), sems2("inv_ready"), sems2("prob_ready"), sems2("zg_ready")
        z_high, z_low = sems2("z_high"), sems2("z_low")
        zT_mm, zT_ready = sems2("zT_mm"), sems2("zT_ready")
        hid_mm, hid_ready = sems("hid_mm"), sems("hid_ready")
        y_mm, scaled, res_ready, stored = sems("y_mm"), sems("scaled"), sems("res_ready"), sems("stored")
        bank_t = psum[0]
        bank_d = psum[1]
        ring = psum[2:4]
        bank_e = [psum[4:6], psum[6:8]]
        WIDE = 256

        def hid_bank(s, m):
            return ring[(s + m) % 2]

        def down(k, s, t0, t1):
            if k == 0:
                return bank_d[:, 0:T * 32].rearrange("p (t n) -> p t n", t=T)[:, t0:t1, 0:AR]
            return bank_e[s][t0 // 2][:, :].rearrange("p (t n) -> p t n", t=2)[:, 0:t1 - t0, D:D + AR]

        SPANS = [[(0, T)], [(0, 2), (2, T)]]

        with nc.Block() as block:
            @block.vector
            def _(dve):
                def x_tile(b):
                    return lambda t: r["x"][:, bass.ds(b[1] * 2 + b[0], 1), t, :]

                def moments(b):
                    norm_moments(dve, r, n[b[0]], b[1], x_tile(b))

                def apply(b):
                    norm_apply(dve, n[b[0]], b[1], x_tile(b))

                def split(b):
                    s, j = b
                    dve.wait_ge(h_ready[s], j + 1)
                    dve.tensor_copy(h[s][0][:, :], hT[s][:, :]).then_inc(h_high[s], 1)

                def route(b, k):
                    s, j = b
                    dve.wait_ge(down_mm[k][s], j + 1)
                    for t0, t1 in SPANS[k]:
                        ins = dve.tensor_reduce(top[k][s][:, t0:t1], down(k, s, t0, t1)[:, :, ER:AR], AX_X, ALU.max)
                    ins.then_inc(top_ready[k][s], 1)
                    dve.wait_ge(top_ready[k][s], j + 1)
                    for t0, t1 in SPANS[k]:
                        ins = dve.tensor_tensor(shifted[k][s][:, t0:t1, :], down(k, s, t0, t1)[:, :, ER:AR], over(top[k][s][:, t0:t1], 2, [P, t1 - t0, E]), ALU.subtract)
                    ins.then_inc(shift_ready[k][s], 1)
                    dve.wait_ge(expo_ready[k][s], j + 1)
                    dve.tensor_reduce(den[k][s][:, :], expo[k][s][:, :, :], AX_X, ALU.add).then_inc(den_ready[k][s], 1)
                    dve.wait_ge(den_ready[k][s], j + 1)
                    dve.reciprocal(inv[k][s][:, :], den[k][s][:, :]).then_inc(inv_ready[k][s], 1)
                    dve.wait_ge(inv_ready[k][s], j + 1)
                    dve.tensor_tensor(prob[k][s][:, :, :], expo[k][s][:, :, :], over(inv[k][s][:, :], 2, [P, T, E]), ALU.mult).then_inc(prob_ready[k][s], 1)
                    dve.wait_ge(prob_ready[k][s], j + 1)
                    for t0, t1 in SPANS[k]:
                        z = down(k, s, t0, t1)[:, :, 0:ER].rearrange("p t (e n) -> p t e n", e=E)
                        g = zg[k][s][:, t0:t1, :].rearrange("p t (e n) -> p t e n", e=E)
                        ins = dve.tensor_tensor(g, z, over(prob[k][s][:, t0:t1, :], 3, [P, t1 - t0, E, R]), ALU.mult)
                    ins.then_inc(zg_ready[k][s], 1)
                    dve.wait_ge(zg_ready[k][s], j + 1)
                    parts = stack[k][s][:, :, :].rearrange("p t (q n) -> p t q n", q=3)
                    dve.tensor_copy(parts[:, :, 0:3:2, 0:ER].bitcast(F32R), over(zg[k][s][:, :, :], 2, [P, T, 2, ER])).then_inc(z_high[k][s], 1)
                    dve.wait_ge(z_high[k][s], j + 1)
                    dve.tensor_tensor(parts[:, :, 1, 0:ER], zg[k][s][:, :, :], parts[:, :, 0, 0:ER], ALU.subtract).then_inc(z_low[k][s], 1)

                def scale(b):
                    s, j = b
                    dve.wait_ge(y_mm[s], j + 1)
                    g = r["gain_ffn1"][:, bass.ds(j * 2 + s, 1), :].broadcast_to([P, 2, D])
                    for q in range(2):
                        y = bank_e[s][q][:, :].rearrange("p (t n) -> p t n", t=2)[:, :, 0:D]
                        ins = dve.tensor_tensor(upd[s][:, 2 * q:2 * q + 2, :], y, g, ALU.mult)
                    ins.then_inc(scaled[s], 1)

                def first():
                    moments((0, 0))
                    moments((1, 0))
                    apply((0, 0))
                    apply((1, 0))
                    for k in range(2):
                        for s in slots:
                            dve.memset(stack[k][s][:, :, :], 0.0).then_inc(stack_cleared, 1)
                    dve.wait_ge(stack_cleared, 4)
                    for k in range(2):
                        for s in slots:
                            ones = stack[k][s][:, :, :].rearrange("p t (q n) -> p t q n", q=3)[:, :, 0:3:2, ER:ER + 1]
                            dve.memset(ones, 1.0).then_inc(stack_set, 1)
                    split((0, 0))
                    route((0, 0), 0)

                def step(b, has_before, has_after, has_second):
                    if has_before:
                        route(before(b), 1)
                    if has_after:
                        split(after(b))
                        if has_second:
                            moments(after(after(b)))
                        route(after(b), 0)
                    if has_before:
                        scale(before(b))
                    if has_second:
                        apply(after(after(b)))

                steps(dve, first, step)
                route((1, B // 2 - 1), 1)
                dve.wait_ge(res_ready[1], B // 2 - 1)
                scale((1, B // 2 - 1))

            @block.gpsimd
            def _(pool):
                def low(b):
                    s, j = b
                    pool.wait_ge(h_high[s], j + 1)
                    pool.tensor_tensor(h[s][1][:, :], hT[s][:, :], h[s][0][:, :].bitcast(F32), ALU.subtract).then_inc(h_low[s], 1)

                def finish(b):
                    s, j = b
                    pool.wait_ge(scaled[s], j + 1)
                    pool.wait_ge(stored[s], (j + 1) * 16)
                    x = r["x"][:, bass.ds(j * 2 + s, 1), :, :].rearrange("p b t n -> p (b t) n")
                    pool.tensor_tensor(res[s][:, :, :], x, upd[s][:, :, :], ALU.add).then_inc(res_ready[s], 1)

                def first():
                    norm_rstd(pool, r, n[0], 0)
                    norm_rstd(pool, r, n[1], 0)
                    low((0, 0))

                def step(b, has_before, has_after, has_second):
                    if has_after:
                        low(after(b))
                    if has_second:
                        s, j = after(after(b))
                        norm_rstd(pool, r, n[s], j)
                    if has_before:
                        finish(before(b))

                steps(pool, first, step)
                finish((1, B // 2 - 1))

            @block.sync
            def _(sp):
                for s in slots:
                    sp.sem_inc(stored[s], 16)
                with sp.Fori(0, B // 2) as i:
                    for s in slots:
                        sp.wait_ge(res_ready[s], i + 1)
                        dst = out[bass.ds(i * 2 + s, 1), :, :].rearrange("b (t p) n -> p (b t) n", p=P)
                        sp.dma_start(dst, res[s][:, :, :]).then_inc(stored[s], 16)
                for s in slots:
                    sp.wait_ge(stored[s], 16 * (B // 2 + 1))

            @block.scalar
            def _(act):
                def bring_h(b):
                    s, j = b
                    act.wait_ge(flipped[s], j + 1)
                    modulate(act, r, hT[s][:, :], bank_t[:, :], 1, 2, j * 2 + s).then_inc(h_ready[s], 1)

                def exps(b, k):
                    s, j = b
                    act.wait_ge(shift_ready[k][s], j + 1)
                    act.activation(expo[k][s][:, :, :], shifted[k][s][:, :, :], ACT.Exp).then_inc(expo_ready[k][s], 1)

                def ranks(b, k):
                    s, j = b
                    act.wait_ge(zT_mm[k][s], j + 1)
                    bank = hid_bank(1 - s, 4) if k else bank_t
                    act.copy(zT[k][s][:, :], bank[0:3 * GLO, :]).then_inc(zT_ready[k][s], 1)

                def first():
                    bring_h((0, 0))
                    exps((0, 0), 0)
                    ranks((0, 0), 0)

                def step(b, has_before, has_after, has_second):
                    s, j = b
                    if has_before:
                        exps(before(b), 1)
                    for m in range(KH):
                        act.wait_ge(hid_mm[s], j * KH + m + 1)
                        act.activation(hid[s][:, m, :], hid_bank(s, m)[:, :], ACT.Relu).then_inc(hid_ready[s], 1)
                    if has_after:
                        bring_h(after(b))
                    if has_before:
                        ranks(before(b), 1)
                    if has_after:
                        exps(after(b), 0)
                        ranks(after(b), 0)

                steps(act, first, step)
                exps((1, B // 2 - 1), 1)
                ranks((1, B // 2 - 1), 1)

            @block.tensor
            def _(pe):
                def flip_in(b):
                    s, j = b
                    pe.wait_ge(n[s]["ready"], j + 1)
                    flip(pe, bank_t, lambda t: n[s]["out"][:, t, :], r).then_inc(flipped[s], 1)

                def down_in(b):
                    s, j = b
                    pe.wait_ge(h_ready[s], j + 1)
                    for t in range(T):
                        mm = pe.matmul(bank_d[:, t * 32:t * 32 + AR], hT[s][:, t * P:(t + 1) * P], r["ar1"][:, :], start=True, stop=True)
                    mm.then_inc(down_mm[0][s], 1)

                def flip_ranks(b, k):
                    s, j = b
                    pe.wait_ge(z_low[k][s], j + 1)
                    bank = hid_bank(1 - s, 4) if k else bank_t
                    for t in range(T):
                        mm = pe.transpose(bank[0:3 * GLO, t * P:(t + 1) * P], stack[k][s][:, t, :], r["ident"][:, :])
                    mm.then_inc(zT_mm[k][s], 1)

                def layer1(b):
                    s, j = b
                    pe.wait_ge(h_low[s], j + 1)
                    for m in range(KH):
                        if m >= 2:
                            pe.wait_ge(hid_ready[s], j * KH + m - 1)
                        at = slice(F1 + m * P, F1 + (m + 1) * P)
                        acc = hid_bank(s, m)[:, :]
                        split_mm(pe, acc, (r["v_hi"][:, at], r["v_lo"][:, at]), [h[s][q][:, :] for q in range(2)], True, False)
                        if m == 0:
                            pe.wait_ge(zT_ready[0][s], j + 1)
                        pe.matmul(acc, r["b1s"][:, m * P:(m + 1) * P], zT[0][s][:, :], start=False, stop=True).then_inc(hid_mm[s], 1)

                def layer2(b):
                    s, j = b
                    pe.wait_ge(hid_ready[s], (j + 1) * KH)
                    for t in range(T):
                        at = (t % 2) * WIDE
                        for k in range(KH):
                            mm = pe.matmul(bank_e[s][t // 2][:, at:at + D + AR], hid[s][:, k, t * P:(t + 1) * P], r["war2"][:, k, :], start=(k == 0 and t % 2 == 0), stop=(k == KH - 1), skip_group_check=True)
                    mm.then_inc(down_mm[1][s], 1)

                def layer2_end(b):
                    s, j = b
                    pe.wait_ge(zT_ready[1][s], j + 1)
                    for t in range(T):
                        at = (t % 2) * WIDE
                        mm = pe.matmul(bank_e[s][t // 2][:, at:at + D], zT[1][s][:, t * P:(t + 1) * P], r["b2s"][:, :], start=False, stop=True, skip_group_check=True)
                    mm.then_inc(y_mm[s], 1)

                def first():
                    pe.wait_ge(stack_set, 4)
                    flip_in((0, 0))
                    down_in((0, 0))
                    flip_ranks((0, 0), 0)

                def step(b, has_before, has_after, has_second):
                    layer1(b)
                    if has_after:
                        flip_in(after(b))
                    if has_before:
                        pe.wait_ge(hid_ready[b[0]], b[1] * KH + 3)
                        flip_ranks(before(b), 1)
                    if has_after:
                        down_in(after(b))
                    if has_before:
                        layer2_end(before(b))
                    layer2(b)
                    if has_after:
                        flip_ranks(after(b), 0)

                steps(pe, first, step)
                last = (1, B // 2 - 1)
                flip_ranks(last, 1)
                layer2_end(last)


def kernel(**inputs):
    import numpy as np
    import concourse.bacc as bacc
    from concourse import mybir as _mybir
    from concourse.bass_utils import run_bass_kernel_spmd

    a = {k: np.asarray(v) for k, v in inputs.items()}

    def col(x, n=None):
        return x.reshape(-1, 1)

    def tiles(wT, k):
        return wT.reshape(k, P, -1).transpose(1, 0, 2).reshape(P, -1)

    keep = np.ones((GLO + NH, S), np.float32)
    keep[:, ::P] = 0
    sel = np.zeros((GLO + NH, NH + 2, P), np.float32)
    for h in range(NH):
        rows = slice((h % 4) * DV, (h % 4 + 1) * DV)
        for at in (h, GLO + h):
            sel[at, h] = sel[at, NH + h // 4, rows] = 1
    b12 = np.zeros((3 * GLO, HID + D + 1), np.float32)
    b12[:, HID + D] = 1
    for q in range(3):
        rows = slice(q * GLO, q * GLO + ER)
        b12[rows, :HID], b12[rows, HID:HID + D] = a["L1_ffn_B1"].reshape(ER, HID), a["L1_ffn_B2"].reshape(ER, D)
        b12[rows, HID + D] = 1.0 / R
        if q != 1:
            b12[q * GLO + ER, :HID], b12[q * GLO + ER, HID:HID + D] = a["L1_ffn_b1"], a["L1_ffn_b2"]
    A1 = a["L1_ffn_A1"].transpose(1, 0, 2).reshape(D, ER)
    A2 = a["L1_ffn_A2"].transpose(1, 0, 2).reshape(HID, ER)
    c_diag = np.zeros((SD, SD), np.float32)
    for h in range(2):
        at = slice(h * SD // 2, (h + 1) * SD // 2)
        c_diag[at, at] = a["L0_attn_C_param"][h]
    v_all = np.zeros((D, VCOLS), np.float32)
    v_all[:, VO:VO + HV], v_all[:, VO + HV:VO + 2 * HV] = a["L1_attn_Wv"], a["L1_attn_Wog"]
    v_all[:, F1:F1 + HID] = a["L1_ffn_W1"]
    bg = np.zeros((P, 1), np.float32)
    for at in (0, GLO):
        v_all[:, GT + at:GT + at + NH] = a["L1_attn_Wg"]
        bg[at:at + NH] = col(a["L1_attn_bg"])
    WAR2 = np.concatenate([a["L1_ffn_W2"], A2, a["L1_ffn_R2"]], 1)
    arrays = {
        "x": a["L0_attn_x"],
        "cT": np.stack([a["L0_c"].T, a["L1_c"].T], 1),
        "wmod": np.stack([a["L0_wmod"].reshape(D, 6, D), a["L1_wmod"].reshape(D, 6, D)], 1),
        "cols": np.concatenate([
            np.eye(P, dtype=np.float32), a["L0_attn_Wp"],
            *(a[f"L0_ffn_{k}_s"].reshape(KH, P).T for k in ("w1", "w2", "h1", "h2")),
            col(a["L0_attn_ln_gamma"]), col(a["L0_attn_ln_beta"]), col(a["L0_ffn_w3_s"])], 1),
        "rows": np.concatenate([
            col(a["L0_attn_B_param"]), col(a["L0_attn_bp"]), col(a["L0_attn_log_neg_lambdas"]),
            c_diag, a["L0_attn_Wo"]], 1),
        "bo": a["L0_attn_bo"].reshape(1, D),
        "w_all": np.concatenate([
            a["L0_ffn_w1_w"].T, a["L0_ffn_w2_w"].T, tiles(a["L0_ffn_h1_w"].T, KH),
            tiles(a["L0_ffn_h2_w"].T, KH), tiles(a["L0_ffn_w3_w"].T, KH)], 1),
        "WqT": a["L1_attn_Wq"].reshape(D, NH, DK).transpose(2, 1, 0),
        "WkT": a["L1_attn_Wk"].reshape(D, NH, DK).transpose(2, 1, 0),
        "v_all": v_all, "B12": b12,
        "l1": np.concatenate([tiles(a["L1_attn_Wo"], 2), A1, a["L1_ffn_R1"], tiles(WAR2, KH), bg], 1),
        "eye8": np.eye(NH, dtype=np.float32), "keep": keep, "sel": sel,
    }
    nc = bacc.Bacc("TRN2", target_bir_lowering=False, num_devices=1)
    given, d = {}, {}
    for name, x in arrays.items():
        x = np.ascontiguousarray(x)
        given[f"in_{name}"] = x
        d[name] = nc.dram_tensor(f"in_{name}", x.shape, _mybir.dt.from_np(x.dtype), kind="ExternalInput").ap()
    out = nc.dram_tensor("out", (B, S, D), _mybir.dt.float32, kind="ExternalOutput").ap()
    build(nc, d, out)
    result = run_bass_kernel_spmd(nc, [given], core_ids=[0])
    return result.results[0]["out"]
```
